# Optimizing a Trainium2 kernel written in Bass

```python
import numpy as np
import jax
import jax.numpy as jnp

def _softmax(x, axis=-1):
    return jax.nn.softmax(x, axis=axis)

def _gelu(x):
    return jax.nn.gelu(x, approximate=True)

def _silu(x):
    return jax.nn.silu(x)

def _sigmoid(x):
    return jax.nn.sigmoid(x)

def _layernorm(x, axis=-1, eps=1e-05):
    m = jnp.mean(x, axis=axis, keepdims=True)
    v = jnp.var(x, axis=axis, keepdims=True)
    return (x - m) / jnp.sqrt(v + eps)

def _scatter_add(tgt, idx, src, axis=0):
    return tgt.at[idx].add(src)

def _segment_sum(src, seg, n):
    return jax.ops.segment_sum(src, seg, n)
kernel_name = 'mk_macaron_d1_jaxref_r4_3ccc56'

def setup_inputs(seed: int=0):
    np.random.seed(seed)
    _w = jnp.asarray

    def _L0_attn_setup():
        import jax, jax.numpy as jnp
        import numpy as np
        B, S, H = (8, 512, 256)
        CHUNK = 64
        INTER = 512
        BASE_LR = 0.01
        MAX_GRAD_NORM = 1.0
        EPS = 1e-06

        def rmsnorm(x, w):
            return x * jax.lax.rsqrt(jnp.mean(x * x, axis=-1, keepdims=True) + EPS) * w

        def mem_fwd(params, x):
            w0, w1, ln = params
            h = jax.nn.silu(x @ w0.T)
            y = h @ w1.T
            return x + rmsnorm(y, ln)

        def forward(x, wq_w, wk_w, wv_w, q_norm_w, k_norm_w, alpha_w, theta_w, eta_w, mem_w0, mem_w1, mem_ln_w):
            Bx, Sx, Hx = x.shape
            NC = Sx // CHUNK
            xc = x.reshape(Bx, NC, CHUNK, Hx)
            xf = xc.reshape(Bx, NC, CHUNK * Hx)
            alpha = jax.nn.sigmoid(jnp.mean(xf @ alpha_w.T, axis=0))
            theta = jax.nn.sigmoid(xf @ theta_w.T) * BASE_LR
            eta = jax.nn.sigmoid(jnp.mean(xf @ eta_w.T, axis=0))
            beta = 1.0 - alpha
            k = rmsnorm(jax.nn.silu(xc @ wk_w.T), k_norm_w)
            v = jax.nn.silu(xc @ wv_w.T)
            mem0 = (mem_w0, mem_w1, mem_ln_w)
            surp0 = jax.tree_util.tree_map(jnp.zeros_like, mem0)

            def step(carry, inp):
                mem, surp = carry
                k_c, v_c, th_c, eta_c, beta_c = inp

                def loss_fn(p):
                    pred = mem_fwd(p, k_c)
                    return jnp.mean((v_c - pred) ** 2 * th_c[:, :, None])
                grads = jax.grad(loss_fn)(mem)
                total = jnp.sqrt(sum((jnp.sum(g * g) for g in grads)))
                clip = jax.lax.stop_gradient(jnp.minimum(MAX_GRAD_NORM / (total + 1e-06), 1.0))
                new_surp = tuple((eta_c * s_ - g * clip for s_, g in zip(surp, grads)))
                new_mem = tuple((beta_c * m + ns for m, ns in zip(mem, new_surp)))
                return ((new_mem, new_surp), None)
            xs = (jnp.swapaxes(k, 0, 1), jnp.swapaxes(v, 0, 1), jnp.swapaxes(theta, 0, 1), eta, beta)
            (mem_f, _), _ = jax.lax.scan(step, (mem0, surp0), xs)
            q = rmsnorm(jax.nn.silu(x @ wq_w.T), q_norm_w)
            return mem_fwd(mem_f, q)
        key = jax.random.key(seed)
        ks = jax.random.split(key, 9)
        s = 0.02
        return {'x': jax.random.normal(ks[0], (B, S, H), jnp.float32), 'wq_w': jax.random.normal(ks[1], (H, H), jnp.float32) * s, 'wk_w': jax.random.normal(ks[2], (H, H), jnp.float32) * s, 'wv_w': jax.random.normal(ks[3], (H, H), jnp.float32) * s, 'q_norm_w': jnp.ones((H,), jnp.float32), 'k_norm_w': jnp.ones((H,), jnp.float32), 'alpha_w': jax.random.normal(ks[4], (1, CHUNK * H), jnp.float32) * s, 'theta_w': jax.random.normal(ks[5], (1, CHUNK * H), jnp.float32) * s, 'eta_w': jax.random.normal(ks[6], (1, CHUNK * H), jnp.float32) * s, 'mem_w0': jax.random.normal(ks[7], (INTER, H), jnp.float32) * s, 'mem_w1': jax.random.normal(ks[8], (H, INTER), jnp.float32) * s, 'mem_ln_w': jnp.ones((H,), jnp.float32)}
    _L0_attn_in = _L0_attn_setup()

    def _L0_ffn_setup():
        import jax, jax.numpy as jnp
        import numpy as np
        D = 256
        H = 512
        E = 8
        TOP_K = 2
        N_SHARED = 1
        B, S = (2, 256)
        key = jax.random.key(seed)
        ks = jax.random.split(key, 12)
        sc = 0.02
        return {'hidden': jax.random.normal(ks[0], (B, S, D), jnp.float32), 'router_w': jax.random.normal(ks[1], (D, E), jnp.float32) * sc, 'router_b': jnp.zeros((E,), jnp.float32), 'sw1': jax.random.normal(ks[2], (D, H), jnp.float32) * sc, 'sb1': jnp.zeros((H,), jnp.float32), 'sw2': jax.random.normal(ks[3], (H, D), jnp.float32) * sc, 'sb2': jnp.zeros((D,), jnp.float32), 'rw1': jax.random.normal(ks[4], (E, D, H), jnp.float32) * sc, 'rb1': jnp.zeros((E, H), jnp.float32), 'rw2': jax.random.normal(ks[5], (E, H, D), jnp.float32) * sc, 'rb2': jnp.zeros((E, D), jnp.float32)}
    _L0_ffn_in = _L0_ffn_setup()
    _d = {'L0_attn_x': _L0_attn_in['x'], 'L0_attn_wq_w': _L0_attn_in['wq_w'], 'L0_attn_wk_w': _L0_attn_in['wk_w'], 'L0_attn_wv_w': _L0_attn_in['wv_w'], 'L0_attn_q_norm_w': _L0_attn_in['q_norm_w'], 'L0_attn_k_norm_w': _L0_attn_in['k_norm_w'], 'L0_attn_alpha_w': _L0_attn_in['alpha_w'], 'L0_attn_theta_w': _L0_attn_in['theta_w'], 'L0_attn_eta_w': _L0_attn_in['eta_w'], 'L0_attn_mem_w0': _L0_attn_in['mem_w0'], 'L0_attn_mem_w1': _L0_attn_in['mem_w1'], 'L0_attn_mem_ln_w': _L0_attn_in['mem_ln_w'], 'L0_ffn_router_w': _L0_ffn_in['router_w'], 'L0_ffn_router_b': _L0_ffn_in['router_b'], 'L0_ffn_sw1': _L0_ffn_in['sw1'], 'L0_ffn_sb1': _L0_ffn_in['sb1'], 'L0_ffn_sw2': _L0_ffn_in['sw2'], 'L0_ffn_sb2': _L0_ffn_in['sb2'], 'L0_ffn_rw1': _L0_ffn_in['rw1'], 'L0_ffn_rb1': _L0_ffn_in['rb1'], 'L0_ffn_rw2': _L0_ffn_in['rw2'], 'L0_ffn_rb2': _L0_ffn_in['rb2']}
    _x0 = _d['L0_attn_x']
    _d['L0_attn_x'] = jax.random.normal(jax.random.fold_in(jax.random.key(seed), 1), (8, 512, 256), dtype=_x0.dtype)
    del _x0
    return _d

def reference(L0_attn_x, L0_attn_wq_w, L0_attn_wk_w, L0_attn_wv_w, L0_attn_q_norm_w, L0_attn_k_norm_w, L0_attn_alpha_w, L0_attn_theta_w, L0_attn_eta_w, L0_attn_mem_w0, L0_attn_mem_w1, L0_attn_mem_ln_w, L0_ffn_router_w, L0_ffn_router_b, L0_ffn_sw1, L0_ffn_sb1, L0_ffn_sw2, L0_ffn_sb2, L0_ffn_rw1, L0_ffn_rb1, L0_ffn_rw2, L0_ffn_rb2):

    def _L0_attn_ref(x, wq_w, wk_w, wv_w, q_norm_w, k_norm_w, alpha_w, theta_w, eta_w, mem_w0, mem_w1, mem_ln_w):
        import jax, jax.numpy as jnp
        import numpy as np
        B, S, H = (8, 512, 256)
        CHUNK = 64
        INTER = 512
        BASE_LR = 0.01
        MAX_GRAD_NORM = 1.0
        EPS = 1e-06

        def rmsnorm(x, w):
            return x * jax.lax.rsqrt(jnp.mean(x * x, axis=-1, keepdims=True) + EPS) * w

        def mem_fwd(params, x):
            w0, w1, ln = params
            h = jax.nn.silu(x @ w0.T)
            y = h @ w1.T
            return x + rmsnorm(y, ln)

        def forward(x, wq_w, wk_w, wv_w, q_norm_w, k_norm_w, alpha_w, theta_w, eta_w, mem_w0, mem_w1, mem_ln_w):
            Bx, Sx, Hx = x.shape
            NC = Sx // CHUNK
            xc = x.reshape(Bx, NC, CHUNK, Hx)
            xf = xc.reshape(Bx, NC, CHUNK * Hx)
            alpha = jax.nn.sigmoid(jnp.mean(xf @ alpha_w.T, axis=0))
            theta = jax.nn.sigmoid(xf @ theta_w.T) * BASE_LR
            eta = jax.nn.sigmoid(jnp.mean(xf @ eta_w.T, axis=0))
            beta = 1.0 - alpha
            k = rmsnorm(jax.nn.silu(xc @ wk_w.T), k_norm_w)
            v = jax.nn.silu(xc @ wv_w.T)
            mem0 = (mem_w0, mem_w1, mem_ln_w)
            surp0 = jax.tree_util.tree_map(jnp.zeros_like, mem0)

            def step(carry, inp):
                mem, surp = carry
                k_c, v_c, th_c, eta_c, beta_c = inp

                def loss_fn(p):
                    pred = mem_fwd(p, k_c)
                    return jnp.mean((v_c - pred) ** 2 * th_c[:, :, None])
                grads = jax.grad(loss_fn)(mem)
                total = jnp.sqrt(sum((jnp.sum(g * g) for g in grads)))
                clip = jax.lax.stop_gradient(jnp.minimum(MAX_GRAD_NORM / (total + 1e-06), 1.0))
                new_surp = tuple((eta_c * s_ - g * clip for s_, g in zip(surp, grads)))
                new_mem = tuple((beta_c * m + ns for m, ns in zip(mem, new_surp)))
                return ((new_mem, new_surp), None)
            xs = (jnp.swapaxes(k, 0, 1), jnp.swapaxes(v, 0, 1), jnp.swapaxes(theta, 0, 1), eta, beta)
            (mem_f, _), _ = jax.lax.scan(step, (mem0, surp0), xs)
            q = rmsnorm(jax.nn.silu(x @ wq_w.T), q_norm_w)
            return mem_fwd(mem_f, q)
        return forward(x, wq_w, wk_w, wv_w, q_norm_w, k_norm_w, alpha_w, theta_w, eta_w, mem_w0, mem_w1, mem_ln_w)

    def _L0_ffn_ref(hidden, router_w, router_b, sw1, sb1, sw2, sb2, rw1, rb1, rw2, rb2):
        import jax, jax.numpy as jnp
        import numpy as np
        D = 256
        H = 512
        E = 8
        TOP_K = 2
        N_SHARED = 1
        B, S = (2, 256)
        b, s, d = hidden.shape
        T = b * s
        flat = hidden.reshape(T, d)
        router_logits = flat @ router_w + router_b
        router_probs = jax.nn.softmax(router_logits, axis=-1)
        topk_probs, topk_idx = jax.lax.top_k(router_probs, TOP_K)
        weights = jnp.zeros_like(router_probs).at[jnp.arange(T)[:, None], topk_idx].add(topk_probs)
        sh = jax.nn.gelu(flat @ sw1 + sb1, approximate=False)
        shared_out = (sh @ sw2 + sb2) / N_SHARED
        h1 = jax.nn.gelu(jnp.einsum('td,edh->teh', flat, rw1) + rb1[None], approximate=False)
        expert_out = jnp.einsum('teh,ehd->ted', h1, rw2) + rb2[None]
        mixed = jnp.einsum('ted,te->td', expert_out, weights)
        return (shared_out + mixed).reshape(b, s, d)
    x = L0_attn_x
    x = x + 0.5 * _L0_ffn_ref(_layernorm(x, axis=-1), L0_ffn_router_w, L0_ffn_router_b, L0_ffn_sw1, L0_ffn_sb1, L0_ffn_sw2, L0_ffn_sb2, L0_ffn_rw1, L0_ffn_rb1, L0_ffn_rw2, L0_ffn_rb2)
    x = x + _L0_attn_ref(_layernorm(x, axis=-1), L0_attn_wq_w, L0_attn_wk_w, L0_attn_wv_w, L0_attn_q_norm_w, L0_attn_k_norm_w, L0_attn_alpha_w, L0_attn_theta_w, L0_attn_eta_w, L0_attn_mem_w0, L0_attn_mem_w1, L0_attn_mem_ln_w)
    x = x + 0.5 * _L0_ffn_ref(_layernorm(x, axis=-1), L0_ffn_router_w, L0_ffn_router_b, L0_ffn_sw1, L0_ffn_sb1, L0_ffn_sw2, L0_ffn_sb2, L0_ffn_rw1, L0_ffn_rb1, L0_ffn_rw2, L0_ffn_rb2)
    return x

_drawn_inputs = setup_inputs


def setup_inputs(seed=0):
    import zlib

    import numpy as np

    out = dict(_drawn_inputs(seed))
    spreads = {'L0_attn_q_norm_w': (1.0, 0.2),
     'L0_attn_k_norm_w': (1.0, 0.6),
     'L0_attn_mem_ln_w': (1.0, 0.6),
     'L0_ffn_router_b': (0.0, 0.8),
     'L0_ffn_sb1': (0.0, 0.454),
     'L0_ffn_sb2': (0.0, 0.1),
     'L0_ffn_rb1': (0.0, 0.8),
     'L0_ffn_rb2': (0.0, 0.449)}
    factors = {'L0_attn_wk_w': 8.0,
     'L0_attn_wv_w': 8.0,
     'L0_attn_alpha_w': 64.0,
     'L0_attn_theta_w': 8.0,
     'L0_attn_eta_w': 8.0,
     'L0_attn_mem_w0': 8.0,
     'L0_attn_mem_w1': 8.0,
     'L0_ffn_router_w': 2.961,
     'L0_ffn_rw1': 4.234,
     'L0_ffn_rw2': 3.893}
    for name, (base, spread) in spreads.items():
        noise = np.random.default_rng([zlib.crc32(name.encode()), seed]).standard_normal(out[name].shape)
        drawn = base * np.exp(spread * noise) if base else spread * noise
        out[name] = jnp.asarray(drawn.astype(out[name].dtype))
    for name, factor in factors.items():
        out[name] = (out[name] * factor).astype(out[name].dtype)
    return out
```

```python
import concourse.bass as bass
from concourse import mybir
from contextlib import ExitStack

B, S, D = 8, 512, 256
CH = 64
NM = S // CH
NT = B * CH // 128
TOK = NT * 128
I = 512
E = 8
NU = E + 1
DC, IC = D // 128, I // 128
WE = DC * I + IC * D
MEMW = IC * D + DC * I + D

SX = 64.0
SW = 64.0
SH = 16.0
LN_EPS, RMS_EPS = 1e-5, 1e-6
GRAD = 2.0 * 0.01 / (B * CH * D)

C_ID, C_BLK, C_ONE = 0, 128, 256
C_AW = 384
C_KN = C_AW + 3 * D
C_QN = C_KN + D
C_B1 = C_QN + D
C_RB = C_B1 + NU * IC
C_REV = C_RB + E
C_RW = C_REV + E
C_B2 = C_RW + DC * E
NC_COLS = C_B2 + D


class Event:

    def __init__(self, sem, per):
        self.sem, self.per = sem, per

    def at(self, occurrence, k=None):
        return occurrence * self.per + (self.per if k is None else k)


def macaron_kernel(nc, x_in, w_experts, w_attn, mem_in, w1n_in, consts_in, out):
    F, H = mybir.dt.float32, mybir.dt.float16
    ALU, ACT, AX = mybir.AluOpType, mybir.ActivationFunctionType, mybir.AxisListType
    x1_dram = nc.dram_tensor("x1_scratch", (128, NM, NT * D), F, kind="Internal").ap()

    ctx = ExitStack()
    with ctx:
        def sb(name, shape, dt=F):
            return ctx.enter_context(nc.sbuf_tensor(name, shape, dt))

        def ev(name, per=1):
            return Event(ctx.enter_context(nc.semaphore(name)), per)

        we_hi = sb("we_hi", [128, NU, WE], H)
        we_lo = sb("we_lo", [128, NU, WE], H)
        wa_hi = sb("wa_hi", [128, 3 * DC * D], H)
        wa_lo = sb("wa_lo", [128, 3 * DC * D], H)
        rw_hi = sb("rw_hi", [128, DC * E], H)
        rw_lo = sb("rw_lo", [128, DC * E], H)
        cst = sb("cst", [128, NC_COLS])
        xt = sb("xt", [128, 2, NT, D])
        fx_hi = sb("fx_hi", [128, DC, TOK], H)
        fx_lo = sb("fx_lo", [128, DC, TOK], H)
        gel = sb("gel", [128, 2, TOK])
        hh = sb("hh", [128, 2, IC, TOK], H)
        hl = sb("hl", [128, 2, IC, TOK], H)
        mem = sb("mem", [128, MEMW])
        sur = sb("sur", [128, MEMW])
        w1n = sb("w1n", [128, DC, I])
        reg_a = sb("reg_a", [128, MEMW])
        reg_b = sb("reg_b", [128, WE])
        reg_c = sb("reg_c", [128, NT, D])
        reg_d = sb("reg_d", [128, NT, D])
        reg_e = sb("reg_e", [128, NT * D])
        reg_f = sb("reg_f", [128, DC, TOK])
        kn = sb("kn", [128, NT, D])
        kv = sb("kv", [128, NT, D])
        hp = sb("hp", [128, NT, I])
        d2 = sb("d2", [128, NT, I])
        stats = sb("stats", [128, 2, NT, 6])
        mv = sb("mv", [128, 2, NT, 2])
        sm = sb("sm", [128, 128])
        lg = sb("lg", [128, 10, NT, E])
        wgt = sb("wgt", [128, NT, NU])
        wacc = sb("wacc", [128, NT, E])
        wgt_t = sb("wgt_t", [NU, NT, 128])

        ident = cst[:, C_ID:C_ID + 128]
        blk = cst[:, C_BLK:C_BLK + 128]
        ones = cst[:, C_ONE:C_ONE + 128]
        aw = cst[:, C_AW:C_AW + 3 * D].rearrange("p (g d) -> p g d", g=3)
        knb, qnb = cst[:, C_KN:C_KN + D], cst[:, C_QN:C_QN + D]
        rb = cst[:, C_RB:C_RB + E]
        rev = cst[:, C_REV:C_REV + E]
        b2 = cst[0:NU, C_B2:C_B2 + D]

        stage = [reg_a[:, 0:WE], reg_b[:, :]]
        tnh = reg_a[:, 0:NT * I].rearrange("p (j i) -> p j i", j=NT)
        ht = reg_a[:, 0:IC * TOK].rearrange("p (c t) -> p c t", c=IC)
        grad = reg_a
        sp = reg_b[:, :].rearrange("p (j i) -> p j i", j=NT)
        dz = sp
        xna, yn = reg_c, reg_c
        xnf, gy = reg_d, reg_d
        half = reg_e[:, :].bitcast(H)
        ax_hi = half[:, 0:DC * TOK].rearrange("p (c t) -> p c t", c=DC)
        ax_lo = half[:, DC * TOK:2 * DC * TOK].rearrange("p (c t) -> p c t", c=DC)
        pr = reg_e[:, :].rearrange("p (j d) -> p j d", j=NT)
        kt, dyt = reg_f, reg_f
        junk = reg_f[:, 0, 0:D]
        mem_w1t = mem[:, 0:IC * D].rearrange("p (c d) -> p c d", c=IC)
        mem_w0t = mem[:, IC * D:IC * D + DC * I].rearrange("p (c i) -> p c i", c=DC)
        mem_ln = mem[:, IC * D + DC * I:MEMW]

        at_sm = [0]

        def col(n):
            at_sm[0] += n
            return sm[:, at_sm[0] - n:at_sm[0]]

        var_eps, rstd = [col(NT), col(NT)], [col(NT), col(NT)]
        neg_half, pos_half, ln_eps, rms_eps = col(NT), col(1), col(NT), col(NT)
        gate_dot = col(3 * NT)
        gate_in, gate_tanh, gate = col(NT + 2), col(NT + 2), col(NT + 2)
        k_ms, k_ms_eps, k_r = col(NT), col(NT), col(NT)
        y_ms, y_ms_eps, y_r = col(NT), col(NT), col(NT)
        dot, dot_neg = col(NT), col(NT)
        nrm, nrm_sum, nrm_all, nrm_root = col(2), col(1), col(1), col(1)
        nrm_c = [col(1) for _ in range(4)]
        waited = [col(1) for _ in range(4)]

        def bank(name):
            return ctx.enter_context(nc.psum_tensor(name, [128, 512], F))

        ps_h = [bank(f"ps_h{i}") for i in range(2)]
        ps_y = [bank(f"ps_y{i}") for i in range(2)]
        ps_s = [bank(f"ps_s{i}") for i in range(4)]

        c_in = ev("constants_loaded", 16)
        mem_ld = ev("memory_loaded", 32)
        stage_ld = [ev(f"stage{i}_loaded", 16) for i in range(2)]
        x_ld = ev("x_loaded", 16)
        x_st = ev("x_stored", 16)
        pool_c = ev("pool_constants", 4)
        w_hi, w_lo = ev("weights_hi"), ev("weights_lo")
        rw_h, rw_l = ev("router_weights_hi"), ev("router_weights_lo")
        nscale = ev("norm_weights_scaled")
        ones_col, sur0 = ev("shared_weight_set"), ev("surprise_zeroed")
        mm1_ps = ev("hidden_in_psum", IC)
        gelu_ok, hid_hi, hid_lo = ev("gelu_done", IC), ev("hidden_hi", IC), ev("hidden_lo", IC)
        mm2_ps = ev("expert_out_in_psum", 2)
        acc_ok = ev("expert_out_added", 2)
        nm = ["ffn", "attn"]
        ln_st = [ev(f"{n}_ln_stats", NT) for n in nm]
        ln_mv = [ev(f"{n}_ln_mean_var", NT) for n in nm]
        ln_ve = [ev(f"{n}_ln_var_eps") for n in nm]
        ln_rs = [ev(f"{n}_ln_rstd") for n in nm]
        ln_xn = [ev(f"{n}_ln_out", NT) for n in nm]
        ln_tp = [ev(f"{n}_lnT_in_psum", DC) for n in nm]
        ln_hi = [ev(f"{n}_lnT_hi", DC) for n in nm]
        ln_lo = [ev(f"{n}_lnT_lo", DC) for n in nm]
        lg_ps, lg_v = ev("logits_in_psum"), ev("router_steps", 19)
        ex_ok = ev("router_exp")
        wt_ps, wt_ok = ev("weightsT_in_psum"), ev("weightsT_copied")
        b_ps, b_ok = ev("bias_in_psum", 2), ev("bias_added", 2)
        g_v, g_ps, g_th, g_ok = ev("gate_dots", 8), ev("gates_in_psum"), ev("gate_tanh", 2), ev("gates", 2)
        p_ps, p_th, p_s = ev("proj_in_psum", NT), ev("proj_tanh", NT), ev("proj_silu", NT)
        p_sq, p_ve, p_r = ev("k_mean_square", NT), ev("k_ms_eps"), ev("k_rms_inv")
        k_ok, kv_ok = ev("k_done", NT), ev("k_minus_v")
        kt_ps, kt_ok = ev("kT_in_psum", DC), ev("kT_copied", DC)
        z_ps, z_th, h_ok = ev("z_in_psum", NT), ev("z_tanh", NT), ev("hidden_mem", NT)
        d2_ok = ev("silu_derivative", 2)
        ht_ps, ht_ok = ev("hT_in_psum", IC), ev("hT_copied", IC)
        y_ps, y_sq, y_ve, y_ri = ev("y_in_psum", 2), ev("y_mean_square", NT), ev("y_ms_eps"), ev("y_rms_inv")
        y_n = ev("y_normalised", NT)
        pred_v = ev("memory_out", 2)
        x_att = ev("attention_added")
        bw = ev("backward_steps", 13)
        dln_ps, dln_ok = ev("dln_in_psum"), ev("dln_copied")
        dyt_ps, dyt_ok = ev("dyT_in_psum", DC), ev("dyT_copied", DC)
        dh_ps, dz_ok = ev("dh_in_psum", NT), ev("dz_done", NT)
        dw_ps, dw_ok, dw_sq = ev("dW_in_psum", 4), ev("dW_copied", 4), ev("grad_squares", 2)
        n_v, n_ps, n_cp, n_rt = ev("norm_partial", 1), ev("norm_in_psum"), ev("norm_copied"), ev("norm_root")
        clip = ev("clip_steps", 4)
        upd = ev("memory_update_steps", 3)
        w1_ps, w1_ok = ev("w1_in_psum", DC), ev("w1_copied", DC)

        block = ctx.enter_context(nc.Block())

        @block.sync
        def _(sp_eng):
            eng = sp_eng

            def load_x(M, src):
                eng.dma_start(xt[:, M % 2, :, :].rearrange("p j d -> p (j d)"), src)\
                   .then_inc(x_ld.sem, 16)

            eng.dma_start(xt[:, 0, :, :].rearrange("p j d -> p (j d)"), x_in[:, 0, :]).then_inc(x_ld.sem, 16)
            for k in range(2):
                eng.dma_start(stage[k], w_experts[:, k, :]).then_inc(stage_ld[k].sem, 16)
            eng.wait_ge(x_ld.sem, x_ld.at(0))
            load_x(1, x_in[:, 1, :])
            for k in range(2, NU + 1):
                eng.wait_ge(w_lo.sem, w_lo.at(k - 2))
                if k < NU:
                    eng.dma_start(stage[k % 2], w_experts[:, k, :]).then_inc(stage_ld[k % 2].sem, 16)
                else:
                    eng.dma_start(stage[k % 2][:, 0:3 * DC * D], w_attn).then_inc(stage_ld[k % 2].sem, 16)

            def store(M, dst):
                eng.wait_ge(acc_ok.sem, acc_ok.at(NU * M + E))
                eng.wait_ge(b_ok.sem, b_ok.at(M))
                eng.dma_start(dst, xt[:, M % 2, :, :].rearrange("p j d -> p (j d)"))\
                   .then_inc(x_st.sem, 16)

            def turn_over(M, dst, src):
                store(M - 1, dst)
                eng.wait_ge(x_st.sem, x_st.at(M - 1))
                load_x(M + 1, src)

            with eng.Fori(1, NM - 1) as M:
                eng.wait_ge(ln_xn[1].sem, ln_xn[1].at(M - 1))
                turn_over(M, x1_dram[:, M - 1, :], x_in[:, M + 1, :])
            for M in (NM - 1, NM):
                eng.wait_ge(ln_xn[1].sem, ln_xn[1].at(M - 1))
                turn_over(M, x1_dram[:, M - 1, :], x1_dram[:, M + 1 - NM, :])
            with eng.Fori(NM + 1, 2 * NM - 1) as M:
                turn_over(M, out[:, M - 1 - NM, :], x1_dram[:, M + 1 - NM, :])
            store(2 * NM - 2, out[:, NM - 2, :])
            store(2 * NM - 1, out[:, NM - 1, :])
            eng.wait_ge(x_st.sem, x_st.at(2 * NM - 1))

        @block.gpsimd
        def _(pool):
            pool.memset(neg_half, -0.5).then_inc(pool_c.sem, 1)
            pool.memset(pos_half, 0.5).then_inc(pool_c.sem, 1)
            pool.memset(ln_eps, LN_EPS).then_inc(pool_c.sem, 1)
            pool.memset(rms_eps, RMS_EPS).then_inc(pool_c.sem, 1)
            pool.memset(sur[:, :], 0.0).then_inc(sur0.sem, 1)
            pool.wait_ge(pool_c.sem, pool_c.at(0))

            def ln_rstd(n, occ):
                pool.wait_ge(ln_mv[n].sem, ln_mv[n].at(occ))
                pool.tensor_tensor(var_eps[n], mv[:, n, :, 1], ln_eps, ALU.add)\
                    .then_inc(ln_ve[n].sem, 1)
                pool.wait_ge(ln_ve[n].sem, ln_ve[n].at(occ))
                pool.tensor_tensor(rstd[n], var_eps[n], neg_half, ALU.pow).then_inc(ln_rs[n].sem, 1)

            def rms_inv(ms, ms_eps, r, have, mid, done, occ):
                pool.wait_ge(have.sem, have.at(occ))
                pool.tensor_tensor(ms_eps, ms, rms_eps, ALU.add).then_inc(mid.sem, 1)
                pool.wait_ge(mid.sem, mid.at(occ))
                pool.tensor_tensor(r, ms_eps, neg_half, ALU.pow).then_inc(done.sem, 1)

            def k_rms(a):
                rms_inv(k_ms, k_ms_eps, k_r, p_sq, p_ve, p_r, a)

            def y_rms(a):
                rms_inv(y_ms, y_ms_eps, y_r, y_sq, y_ve, y_ri, a)

            def scan(a):
                ln_rstd(1, a)
                k_rms(a)
                y_rms(a)
                pool.wait_ge(n_cp.sem, n_cp.at(a))
                pool.tensor_tensor(nrm_root, nrm_all, pos_half, ALU.pow).then_inc(n_rt.sem, 1)

            def apply(a):
                ln_rstd(1, a)
                k_rms(a)
                y_rms(a)

            ln_rstd(0, 0)
            ln_rstd(0, 1)
            with pool.Fori(1, NM - 1) as M:
                scan(M - 1)
                ln_rstd(0, M + 1)
            scan(NM - 2)
            scan(NM - 1)
            apply(NM)
            ln_rstd(0, NM)
            with pool.Fori(NM, 2 * NM - 1) as M:
                apply(M + 1)
                ln_rstd(0, M + 1)

        @block.tensor
        def _(pe):
            def products(out_ap, pairs):
                for n, (lhs, rhs) in enumerate(pairs):
                    last = pe.matmul(out_ap, lhs, rhs, start=(n == 0), stop=(n == len(pairs) - 1))
                return last

            def guard(*waits):
                for event, value in waits:
                    pe.wait_ge(event.sem, value)

            def mm1(M, e):
                u = NU * M + e
                for c in range(IC):
                    if not (isinstance(M, int) and M == 0 and e == 0 and c < 2):
                        pe.wait_ge(gelu_ok.sem, gelu_ok.at(u, c - 1))
                    pairs = []
                    for dc in range(DC):
                        w = slice(dc * I + c * 128, dc * I + (c + 1) * 128)
                        pairs += [(we_hi[:, e, w], fx_hi[:, dc, :]), (we_hi[:, e, w], fx_lo[:, dc, :]),
                                  (we_lo[:, e, w], fx_hi[:, dc, :])]
                    products(ps_h[c % 2][:, :], pairs).then_inc(mm1_ps.sem, 1)

            def mm2(M, e):
                u = NU * M + e
                pe.wait_ge(hid_lo.sem, hid_lo.at(u))
                for b in range(2):
                    if not (isinstance(M, int) and M == 0 and e == 0):
                        pe.wait_ge(acc_ok.sem, acc_ok.at(u - 1, b + 1))
                    for j in (2 * b, 2 * b + 1):
                        pairs = []
                        for c in range(IC):
                            w = slice(DC * I + c * D, DC * I + (c + 1) * D)
                            t = slice(j * 128, (j + 1) * 128)
                            pairs += [(hh[:, e % 2, c, t], we_hi[:, e, w]), (hh[:, e % 2, c, t], we_lo[:, e, w]),
                                      (hl[:, e % 2, c, t], we_hi[:, e, w])]
                        last = products(ps_y[b][:, (j % 2) * D:(j % 2 + 1) * D], pairs)
                    last.then_inc(mm2_ps.sem, 1)

            def transposes(src, banks, done, occ_wait, *guards):
                guard(occ_wait, *guards)
                for c, ps in enumerate(banks):
                    for j in range(NT):
                        last = pe.transpose(ps[:, j * 128:(j + 1) * 128], src[:, j, c * 128:(c + 1) * 128], ident)
                    last.then_inc(done.sem, 1)

            def ln_t(n, occ, *guards):
                src, banks = (xnf, ps_s[2:4]) if n == 0 else (xna, ps_s[0:2])
                transposes(src, banks, ln_tp[n], (ln_xn[n], ln_xn[n].at(occ)), *guards)

            def router(M):
                guard((ln_lo[0], ln_lo[0].at(M)))
                for j in range(NT):
                    t = slice(j * 128, (j + 1) * 128)
                    pairs = []
                    for c in range(DC):
                        w = slice(c * E, (c + 1) * E)
                        pairs += [(fx_hi[:, c, t], rw_hi[:, w]), (fx_hi[:, c, t], rw_lo[:, w]),
                                  (fx_lo[:, c, t], rw_hi[:, w])]
                    last = products(ps_s[2][:, j * E:(j + 1) * E], pairs)
                last.then_inc(lg_ps.sem, 1)

            def weights_t(M):
                guard((lg_v, lg_v.at(M)))
                for j in range(NT):
                    last = pe.transpose(ps_s[3][0:NU, j * 128:(j + 1) * 128], wgt[:, j, :], ident)
                last.then_inc(wt_ps.sem, 1)

            def biases(M, *guards):
                guard((wt_ok, wt_ok.at(M)), *guards)
                for b in range(2):
                    for j in (2 * b, 2 * b + 1):
                        last = pe.matmul(ps_s[b][:, (j % 2) * D:(j % 2 + 1) * D], wgt_t[:, j, :], b2,
                                         start=True, stop=True)
                    last.then_inc(b_ps.sem, 1)

            def gates(a, *guards):
                guard((g_v, g_v.at(a)), *guards)
                pe.matmul(ps_s[2][:, 0:NT], blk, gate_in[:, 0:NT], start=True, stop=True)
                pe.matmul(ps_s[2][:, NT:NT + 2], ones, gate_in[:, NT:NT + 2], start=True, stop=True)\
                  .then_inc(g_ps.sem, 1)

            def project(a, first, width, where, *guards):
                guard((ln_lo[1], ln_lo[1].at(a)), *guards)
                for j in range(NT):
                    t = slice(j * 128, (j + 1) * 128)
                    pairs = []
                    for c in range(DC):
                        w = slice(first + c * width, first + (c + 1) * width)
                        pairs += [(ax_hi[:, c, t], wa_hi[:, w]), (ax_hi[:, c, t], wa_lo[:, w]),
                                  (ax_lo[:, c, t], wa_hi[:, w])]
                    products(where(j), pairs).then_inc(p_ps.sem, 1)

            def project_kv(a, *guards):
                project(a, 0, 2 * D, lambda j: ps_s[j][:, :], *guards)

            def project_q(a, *guards):
                project(a, 2 * DC * D, D, lambda j: ps_s[j // 2][:, (j % 2) * D:(j % 2 + 1) * D], *guards)

            def k_t(a, *guards):
                transposes(kn, ps_s[2:4], kt_ps, (k_ok, k_ok.at(a)), *guards)

            def z(a, *guards):
                guard((kt_ok, kt_ok.at(a)), *guards)
                for j in range(NT):
                    t = slice(j * 128, (j + 1) * 128)
                    products(ps_s[j][:, :], [(kt[:, c, t], mem_w0t[:, c, :]) for c in range(DC)])\
                        .then_inc(z_ps.sem, 1)

            def h_t(a, *guards):
                transposes(hp, ps_s, ht_ps, (h_ok, h_ok.at(a)), *guards)

            def y(a):
                guard((ht_ok, ht_ok.at(a)))
                for b in range(2):
                    for j in (2 * b, 2 * b + 1):
                        t = slice(j * 128, (j + 1) * 128)
                        last = products(ps_s[b][:, (j % 2) * D:(j % 2 + 1) * D],
                                        [(ht[:, c, t], mem_w1t[:, c, :]) for c in range(IC)])
                    last.then_inc(y_ps.sem, 1)

            def dln_dyt(a):
                guard((bw, bw.at(a)))
                products(ps_s[0][:, 0:D], [(ones, gy[:, j, :]) for j in range(NT)]).then_inc(dln_ps.sem, 1)
                transposes(pr, ps_s[2:4], dyt_ps, (bw, bw.at(a)))

            def dh(a):
                guard((dyt_ok, dyt_ok.at(a)), (dln_ok, dln_ok.at(a)))
                for j in range(NT):
                    t = slice(j * 128, (j + 1) * 128)
                    products(ps_s[j][:, :], [(dyt[:, c, t], w1n[:, c, :]) for c in range(DC)])\
                        .then_inc(dh_ps.sem, 1)

            def dw(a):
                guard((dz_ok, dz_ok.at(a)))
                for b in range(2):
                    for c in (2 * b, 2 * b + 1):
                        last = products(ps_s[b][:, (c % 2) * D:(c % 2 + 1) * D],
                                        [(hp[:, j, c * 128:(c + 1) * 128], pr[:, j, :]) for j in range(NT)])
                    last.then_inc(dw_ps.sem, 1)
                for c in range(DC):
                    products(ps_s[2 + c][:, :],
                             [(kn[:, j, c * 128:(c + 1) * 128], dz[:, j, :]) for j in range(NT)])\
                        .then_inc(dw_ps.sem, 1)

            def norm(a):
                guard((n_v, n_v.at(a)))
                pe.matmul(ps_s[0][:, 0:1], ones, nrm_sum, start=True, stop=True).then_inc(n_ps.sem, 1)

            def w1_natural(a):
                guard((upd, upd.at(a)))
                for dc in range(DC):
                    for c in range(IC):
                        last = pe.transpose(ps_s[dc][:, c * 128:(c + 1) * 128],
                                            mem_w1t[:, c, dc * 128:(dc + 1) * 128], ident)
                    last.then_inc(w1_ps.sem, 1)

            def experts(M, fill, first=False):
                guard((ln_lo[0], ln_lo[0].at(M)))
                if first:
                    guard((w_lo, w_lo.at(0)))
                mm1(M, 0)
                for e in range(NU):
                    if e < NU - 1:
                        if first:
                            guard((w_lo, w_lo.at(e + 1)))
                        mm1(M, e + 1)
                    for step in fill.get(2 * e, ()):
                        step()
                    mm2(M, e)
                    for step in fill.get(2 * e + 1, ()):
                        step()

            def next_ln(M, *guards):
                return lambda: ln_t(0, M, *guards)

            def scan_fill(a, M):
                return {
                    1: [lambda: ln_t(1, a, *([(w1_ok, w1_ok.at(a - 1))] if not (isinstance(a, int) and a == 0) else [])),
                        lambda: gates(a, (lg_v, lg_v.at(M, 1)))],
                    2: [lambda: weights_t(M)],
                    3: [lambda: project_kv(a, (g_th, g_th.at(a)), (wt_ok, wt_ok.at(M)))],
                    4: [lambda: biases(M, (p_s, p_s.at(a)))],
                    5: [lambda: k_t(a)],
                    6: [lambda: z(a, (b_ok, b_ok.at(M)))],
                    8: [lambda: h_t(a)],
                    9: [lambda: y(a)],
                    11: [lambda: dln_dyt(a)],
                    12: [lambda: dh(a)],
                    14: [lambda: dw(a)],
                    15: [lambda: norm(a)],
                    16: [lambda: next_ln(M + 1, (dw_ok, dw_ok.at(a)))()],
                    17: [lambda: w1_natural(a), lambda: router(M + 1)],
                }

            def apply_steps(a, *guards):
                return [lambda: ln_t(1, a, *guards), lambda: project_q(a), lambda: k_t(a),
                        lambda: z(a), lambda: h_t(a), lambda: y(a)]

            guard((c_in, c_in.at(0)))
            ln_t(0, 0)
            guard((rw_l, rw_l.at(0)))
            router(0)
            experts(0, {2: [lambda: weights_t(0)], 4: [lambda: biases(0)],
                        16: [next_ln(1)], 17: [lambda: router(1)]}, first=True)
            guard((mem_ld, mem_ld.at(0)), (w_lo, w_lo.at(NU)))
            pe.wait_ge(b_ok.sem, b_ok.at(0))
            with pe.Fori(1, NM - 1) as M:
                fill = scan_fill(M - 1, M)
                fill[1][0] = lambda: ln_t(1, M - 1, (w1_ok, w1_ok.per * (M - 1)))
                experts(M, fill)
            fill = scan_fill(NM - 2, NM - 1)
            del fill[16]
            fill[17] = fill[17][:1]
            experts(NM - 1, fill)
            tail = scan_fill(NM - 1, NM - 1)
            for place in sorted(tail):
                if place in (2, 4, 16):
                    continue
                for step in tail[place][:1] if place == 17 else tail[place]:
                    step()
            for step in apply_steps(NM, (w1_ok, w1_ok.at(NM - 1)), (wt_ok, wt_ok.at(NM - 1))):
                step()
            ln_t(0, NM)
            router(NM)

            def apply_fill(M):
                steps = apply_steps(M + 1, (b_ok, b_ok.at(M)), (wt_ok, wt_ok.at(M)))
                return {2: [lambda: weights_t(M)], 4: [lambda: biases(M, (y_n, y_n.at(M)))],
                        7: steps[0:1], 8: steps[1:2], 9: steps[2:3], 10: steps[3:4], 12: steps[4:5],
                        13: steps[5:6], 16: [next_ln(M + 1)], 17: [lambda: router(M + 1)]}

            with pe.Fori(NM, 2 * NM - 1) as M:
                experts(M, apply_fill(M))
            M = 2 * NM - 1
            experts(M, {2: [lambda: weights_t(M)], 4: [lambda: biases(M, (y_n, y_n.at(M)))]})

        @block.scalar
        def _(act):
            act.dma_start(cst[:, :], consts_in).then_inc(c_in.sem, 16)
            act.dma_start(mem[:, :], mem_in).then_inc(mem_ld.sem, 16)
            act.dma_start(w1n[:, :, :].rearrange("p c i -> p (c i)"), w1n_in).then_inc(mem_ld.sem, 16)

            def copy(dst, src, scale=1.0):
                return act.activation(dst, src, ACT.Copy, scale=scale)

            def split_weights(k):
                act.wait_ge(stage_ld[k % 2].sem, stage_ld[k % 2].at(k // 2))
                if k < NU:
                    copy(we_hi[:, k, :], stage[k % 2], SW).then_inc(w_hi.sem, 1)
                else:
                    copy(wa_hi[:, :], stage[k % 2][:, 0:3 * DC * D], SW).then_inc(w_hi.sem, 1)

            def hidden(M, e):
                u = NU * M + e
                first = isinstance(M, int) and M == 0 and e == 0
                for c in range(IC):
                    act.wait_ge(mm1_ps.sem, mm1_ps.at(u, c + 1))
                    if not (first and c < 2):
                        act.wait_ge(hid_lo.sem, hid_lo.at(u, c - 1))
                    act.activation(gel[:, c % 2, :], ps_h[c % 2][:, :], ACT.Gelu, scale=1.0 / (SX * SW),
                                   bias=cst[:, C_B1 + e * IC + c:C_B1 + e * IC + c + 1])\
                       .then_inc(gelu_ok.sem, 1)
                    if c == 0 and not (isinstance(M, int) and M == 0 and e < 2):
                        act.wait_ge(mm2_ps.sem, mm2_ps.at(u - (1 if e == 0 else 2)))
                    act.wait_ge(gelu_ok.sem, gelu_ok.at(u, c + 1))
                    copy(hh[:, e % 2, c, :], gel[:, c % 2, :], SH).then_inc(hid_hi.sem, 1)

            def ln_high(n, occ):
                dst, banks = (fx_hi, ps_s[2:4]) if n == 0 else (ax_hi, ps_s[0:2])
                for c in range(DC):
                    act.wait_ge(ln_tp[n].sem, ln_tp[n].at(occ, c + 1))
                    copy(dst[:, c, :], banks[c][:, :], SX).then_inc(ln_hi[n].sem, 1)

            def ln_high_ffn(M):
                act.wait_ge(mm1_ps.sem, mm1_ps.at(NU * M - 1))
                ln_high(0, M)

            def router_exp(M):
                act.wait_ge(lg_v.sem, lg_v.at(M, 3))
                act.activation(lg[:, 2, :, :], lg[:, 1, :, :], ACT.Exp).then_inc(ex_ok.sem, 1)

            def weights_t(M):
                act.wait_ge(wt_ps.sem, wt_ps.at(M))
                copy(wgt_t[:, :, :].rearrange("u j t -> u (j t)"), ps_s[3][0:NU, :]).then_inc(wt_ok.sem, 1)

            def gates(a):
                act.wait_ge(g_ps.sem, g_ps.at(a))
                act.activation(gate_tanh[:, 0:NT], ps_s[2][:, 0:NT], ACT.Tanh, scale=0.5).then_inc(g_th.sem, 1)
                act.activation(gate_tanh[:, NT:NT + 2], ps_s[2][:, NT:NT + 2], ACT.Tanh, scale=0.5 / B)\
                   .then_inc(g_th.sem, 1)

            def project(a, width, where, ready):
                for j in range(NT):
                    act.wait_ge(p_ps.sem, p_ps.at(a, ready(j)))
                    act.activation(tnh[:, j, 0:width], where(j), ACT.Tanh, scale=0.5 / (SX * SW))\
                       .then_inc(p_th.sem, 1)
                for j in range(NT):
                    act.wait_ge(p_s.sem, p_s.at(a, j + 1))
                    act.wait_ge(p_sq.sem, p_sq.at(a, j))
                    act.activation(junk, sp[:, j, 0:D], ACT.Square, scale=1.0 / (2 * SX * SW * D ** 0.5),
                                   accum_out=k_ms[:, j:j + 1]).then_inc(p_sq.sem, 1)

            def project_kv(a):
                project(a, 2 * D, lambda j: ps_s[j][:, :], lambda j: j + 1)

            def project_q(a):
                project(a, D, lambda j: ps_s[j // 2][:, (j % 2) * D:(j % 2 + 1) * D],
                        lambda j: 2 * (j // 2) + 2)

            def k_t(a):
                act.wait_ge(p_sq.sem, p_sq.at(a))
                for c in range(DC):
                    act.wait_ge(kt_ps.sem, kt_ps.at(a, c + 1))
                    copy(kt[:, c, :], ps_s[2 + c][:, :]).then_inc(kt_ok.sem, 1)

            def z(a):
                for j in range(NT):
                    act.wait_ge(z_ps.sem, z_ps.at(a, j + 1))
                    act.activation(tnh[:, j, :], ps_s[j][:, :], ACT.Tanh, scale=0.5).then_inc(z_th.sem, 1)

            def h_t(a, backward):
                if backward:
                    act.wait_ge(d2_ok.sem, d2_ok.at(a))
                for c in range(IC):
                    act.wait_ge(ht_ps.sem, ht_ps.at(a, c + 1))
                    copy(ht[:, c, :], ps_s[c][:, :], 0.5).then_inc(ht_ok.sem, 1)

            def y(a):
                for j in range(NT):
                    act.wait_ge(y_ps.sem, y_ps.at(a, j // 2 + 1))
                    act.wait_ge(y_sq.sem, y_sq.at(a, j))
                    act.activation(junk, ps_s[j // 2][:, (j % 2) * D:(j % 2 + 1) * D], ACT.Square,
                                   scale=1.0 / D ** 0.5, accum_out=y_ms[:, j:j + 1]).then_inc(y_sq.sem, 1)

            def dyt_copy(a):
                act.wait_ge(dln_ps.sem, dln_ps.at(a))
                copy(grad[:, IC * D + DC * I:MEMW], ps_s[0][:, 0:D]).then_inc(dln_ok.sem, 1)
                for c in range(DC):
                    act.wait_ge(dyt_ps.sem, dyt_ps.at(a, c + 1))
                    copy(dyt[:, c, :], ps_s[2 + c][:, :]).then_inc(dyt_ok.sem, 1)

            def dw(a):
                for b in range(4):
                    act.wait_ge(dw_ps.sem, dw_ps.at(a, b + 1))
                    copy(grad[:, b * 512:(b + 1) * 512], ps_s[b][:, :], 0.5).then_inc(dw_ok.sem, 1)
                act.wait_ge(dw_ok.sem, dw_ok.at(a))
                act.activation(d2[:, :, :].rearrange("p j i -> p (j i)"), grad[:, 0:IC * D + DC * I],
                               ACT.Square, accum_out=nrm[:, 0:1]).then_inc(dw_sq.sem, 1)
                act.wait_ge(dln_ok.sem, dln_ok.at(a))
                act.activation(junk, grad[:, IC * D + DC * I:MEMW], ACT.Square, accum_out=nrm[:, 1:2])\
                   .then_inc(dw_sq.sem, 1)

            def w1_natural(a):
                for c in range(DC):
                    act.wait_ge(w1_ps.sem, w1_ps.at(a, c + 1))
                    copy(w1n[:, c, :], ps_s[c][:, :]).then_inc(w1_ok.sem, 1)

            def experts(M, fill, prep=()):
                hidden(M, 0)
                for e in range(NU):
                    if e < NU - 1:
                        hidden(M, e + 1)
                    if e in prep:
                        split_weights(e + 2)
                    for step in fill.get(2 * e, ()):
                        step()
                    for step in fill.get(2 * e + 1, ()):
                        step()

            def scan_fill(a, M):
                return {
                    1: [lambda: ln_high(1, a), lambda: gates(a)],
                    2: [lambda: weights_t(M)],
                    3: [lambda: project_kv(a)],
                    5: [lambda: k_t(a)],
                    6: [lambda: z(a)],
                    8: [lambda: h_t(a, True)],
                    9: [lambda: y(a)],
                    11: [lambda: dyt_copy(a)],
                    14: [lambda: dw(a)],
                    16: [lambda: ln_high_ffn(M + 1)],
                    17: [lambda: w1_natural(a), lambda: router_exp(M + 1)],
                }

            def apply_steps(a):
                return [lambda: ln_high(1, a), lambda: project_q(a), lambda: k_t(a), lambda: z(a),
                        lambda: h_t(a, False), lambda: y(a)]

            act.wait_ge(c_in.sem, c_in.at(0))
            copy(rw_hi[:, :], cst[:, C_RW:C_RW + DC * E], SW).then_inc(rw_h.sem, 1)
            ln_high(0, 0)
            split_weights(0)
            router_exp(0)
            split_weights(1)
            experts(0, {2: [lambda: weights_t(0)], 16: [lambda: ln_high_ffn(1)],
                        17: [lambda: router_exp(1)]}, prep=range(NU - 1))
            with act.Fori(1, NM - 1) as M:
                experts(M, scan_fill(M - 1, M))
            fill = scan_fill(NM - 2, NM - 1)
            del fill[16]
            fill[17] = fill[17][:1]
            experts(NM - 1, fill)
            tail = scan_fill(NM - 1, NM - 1)
            for place in sorted(tail):
                if place in (2, 16):
                    continue
                for step in tail[place][:1] if place == 17 else tail[place]:
                    step()
            for step in apply_steps(NM):
                step()
            ln_high_ffn(NM)
            router_exp(NM)
            with act.Fori(NM, 2 * NM - 1) as M:
                steps = apply_steps(M + 1)
                experts(M, {2: [lambda: weights_t(M)], 7: steps[0:1], 8: steps[1:2], 9: steps[2:3],
                            10: steps[3:4], 12: steps[4:5], 13: steps[5:6],
                            16: [lambda: ln_high_ffn(M + 1)], 17: [lambda: router_exp(M + 1)]})
            M = 2 * NM - 1
            experts(M, {2: [lambda: weights_t(M)]})

        @block.vector
        def _(dve):
            def low(dst, src, hi, scale):
                return dve.scalar_tensor_tensor(dst, src, scale, hi, ALU.mult, ALU.subtract)

            def over_d(c):
                return c.unsqueeze(2).to_broadcast([128, NT, D])

            def over_tiles(row, n=D):
                return row.unsqueeze(1).to_broadcast([128, NT, n])

            def split_weights(k):
                dve.wait_ge(w_hi.sem, w_hi.at(k))
                if k < NU:
                    low(we_lo[:, k, :], stage[k % 2], we_hi[:, k, :], SW).then_inc(w_lo.sem, 1)
                else:
                    low(wa_lo[:, :], stage[k % 2][:, 0:3 * DC * D], wa_hi[:, :], SW).then_inc(w_lo.sem, 1)

            def hidden(M, e):
                u = NU * M + e
                for c in range(IC):
                    dve.wait_ge(hid_hi.sem, hid_hi.at(u, c + 1))
                    low(hl[:, e % 2, c, :], gel[:, c % 2, :], hh[:, e % 2, c, :], SH).then_inc(hid_lo.sem, 1)

            def accumulate(M, e):
                u = NU * M + e
                if e == 0:
                    dve.wait_ge(lg_v.sem, lg_v.at(M))
                else:
                    dve.wait_ge(acc_ok.sem, acc_ok.at(u - 1))
                if e == 2:
                    dve.wait_ge(b_ok.sem, b_ok.at(M))
                for b in range(2):
                    dve.wait_ge(mm2_ps.sem, mm2_ps.at(u, b + 1))
                    for j in (2 * b, 2 * b + 1):
                        w = wacc[:, j, e:e + 1] if e < E else 0.5 / (SH * SW)
                        x = xt[:, M % 2, j, :]
                        last = dve.scalar_tensor_tensor(x, ps_y[b][:, (j % 2) * D:(j % 2 + 1) * D], w, x,
                                                        ALU.mult, ALU.add)
                    last.then_inc(acc_ok.sem, 1)

            def layer_norm(n, occ, *waits):
                dst = xnf if n == 0 else xna
                for event, value in waits:
                    dve.wait_ge(event.sem, value)
                dve.memset(waited[2 * n], 0.0)
                for j in range(NT):
                    dve.bn_stats(stats[:, n, j, :], xt[:, occ % 2, j, :]).then_inc(ln_st[n].sem, 1)
                dve.wait_ge(ln_st[n].sem, ln_st[n].at(occ))
                dve.memset(waited[2 * n + 1], 0.0)
                for j in range(NT):
                    dve.bn_aggr(mv[:, n, j, :], stats[:, n, j, :]).then_inc(ln_mv[n].sem, 1)
                dve.wait_ge(ln_rs[n].sem, ln_rs[n].at(occ))
                for j in range(NT):
                    dve.tensor_scalar(dst[:, j, :], xt[:, occ % 2, j, :], mv[:, n, j, 0:1],
                                      rstd[n][:, j:j + 1], ALU.subtract, ALU.mult).then_inc(ln_xn[n].sem, 1)

            def ln_low(n, occ):
                dst, hi, banks = (fx_lo, fx_hi, ps_s[2:4]) if n == 0 else (ax_lo, ax_hi, ps_s[0:2])
                for c in range(DC):
                    dve.wait_ge(ln_hi[n].sem, ln_hi[n].at(occ, c + 1))
                    low(dst[:, c, :], banks[c][:, :], hi[:, c, :], SX).then_inc(ln_lo[n].sem, 1)

            def router(M):
                k = [0]

                def step(ins):
                    k[0] += 1
                    ins.then_inc(lg_v.sem, 1)
                    dve.wait_ge(lg_v.sem, lg_v.at(M, k[0]))

                def over_e(c):
                    return c.unsqueeze(2).to_broadcast([128, NT, E])

                top, rnk, tot, inv = lg[:, 3, :, 0], lg[:, 3, :, 1], lg[:, 3, :, 2], lg[:, 3, :, 3]
                prob, rest, eq, order, s1, s2 = (lg[:, n, :, :] for n in range(4, 10))
                dve.wait_ge(lg_ps.sem, lg_ps.at(M))
                step(dve.scalar_tensor_tensor(lg[:, 0, :, :], ps_s[2][:, 0:NT * E].rearrange("p (j e) -> p j e", j=NT),
                                              1.0 / (SX * SW), over_tiles(rb, E), ALU.mult, ALU.add))
                step(dve.tensor_reduce(top, lg[:, 0, :, :], AX.X, ALU.max))
                step(dve.tensor_tensor(lg[:, 1, :, :], lg[:, 0, :, :], over_e(top), ALU.subtract))
                dve.wait_ge(ex_ok.sem, ex_ok.at(M))
                step(dve.tensor_reduce(tot, lg[:, 2, :, :], AX.X, ALU.add))
                step(dve.reciprocal(inv, tot))
                step(dve.tensor_tensor(prob, lg[:, 2, :, :], over_e(inv), ALU.mult))

                def first_of_largest(values, chosen):
                    step(dve.tensor_reduce(top, values, AX.X, ALU.max))
                    step(dve.tensor_tensor(eq, values, over_e(top), ALU.is_equal))
                    step(dve.tensor_tensor(order, eq, over_tiles(rev, E), ALU.mult))
                    step(dve.tensor_reduce(rnk, order, AX.X, ALU.max))
                    step(dve.tensor_tensor(chosen, order, over_e(rnk), ALU.is_equal))

                first_of_largest(prob, s1)
                step(dve.scalar_tensor_tensor(rest, s1, -4.0, prob, ALU.mult, ALU.add))
                first_of_largest(rest, s2)
                dve.tensor_tensor(s1, s1, s2, ALU.add).then_inc(lg_v.sem, 1)
                dve.wait_ge(lg_v.sem, lg_v.at(M, 18))
                dve.tensor_tensor(wgt[:, :, 0:E], prob, s1, ALU.mult)
                dve.scalar_tensor_tensor(wacc[:, :, :], prob, 0.5 / (SH * SW), s1, ALU.mult, ALU.mult)\
                   .then_inc(lg_v.sem, 1)

            def biases(M):
                dve.wait_ge(acc_ok.sem, acc_ok.at(NU * M + 1))
                for b in range(2):
                    dve.wait_ge(b_ps.sem, b_ps.at(M, b + 1))
                    x = xt[:, M % 2, 2 * b:2 * b + 2, :].rearrange("p j d -> p (j d)")
                    dve.scalar_tensor_tensor(x, ps_s[b][:, :], 0.5, x, ALU.mult, ALU.add).then_inc(b_ok.sem, 1)

            def gate_dots(a):
                k = [0]

                def step(ins):
                    k[0] += 1
                    ins.then_inc(g_v.sem, 1)
                    dve.wait_ge(g_v.sem, g_v.at(a, k[0]))

                dve.wait_ge(ln_xn[1].sem, ln_xn[1].at(a))
                for g in range(3):
                    dst = gate_in[:, 0:NT] if g == 0 else gate_dot[:, g * NT:(g + 1) * NT]
                    step(dve.tensor_tensor(kv[:, :, :], xna[:, :, :], over_tiles(aw[:, g, :]), ALU.mult))
                    step(dve.tensor_reduce(dst, kv[:, :, :], AX.X, ALU.add))
                step(dve.tensor_reduce(gate_in[:, NT:NT + 1], gate_dot[:, NT:2 * NT], AX.X, ALU.add))
                step(dve.tensor_reduce(gate_in[:, NT + 1:NT + 2], gate_dot[:, 2 * NT:3 * NT], AX.X, ALU.add))

            def gates(a):
                dve.wait_ge(g_th.sem, g_th.at(a))
                dve.tensor_scalar(gate[:, :], gate_tanh[:, :], 0.5, 0.5, ALU.mult, ALU.add).then_inc(g_ok.sem, 1)
                dve.wait_ge(g_ok.sem, g_ok.at(a, 1))
                dve.tensor_scalar(gate[:, NT:NT + 1], gate_tanh[:, NT:NT + 1], -0.5, 0.5, ALU.mult, ALU.add)\
                   .then_inc(g_ok.sem, 1)

            def project(a, width, where, weight, with_v):
                for j in range(NT):
                    dve.wait_ge(p_th.sem, p_th.at(a, j + 1) if with_v else p_th.at(a, 2 * (j // 2) + 2))
                    dve.scalar_tensor_tensor(sp[:, j, 0:width], tnh[:, j, 0:width], 1.0, where(j),
                                             ALU.add, ALU.mult).then_inc(p_s.sem, 1)
                dve.wait_ge(p_r.sem, p_r.at(a))
                dve.wait_ge(p_s.sem, p_s.at(a))
                for j in range(NT):
                    dve.scalar_tensor_tensor(kn[:, j, :], sp[:, j, 0:D], k_r[:, j:j + 1], weight,
                                             ALU.mult, ALU.mult).then_inc(k_ok.sem, 1)

            def project_kv(a):
                project(a, 2 * D, lambda j: ps_s[j][:, :], knb, True)
                dve.wait_ge(k_ok.sem, k_ok.at(a))
                dve.scalar_tensor_tensor(kv[:, :, :], sp[:, :, D:2 * D], -0.5 / (SX * SW), kn[:, :, :],
                                         ALU.mult, ALU.add).then_inc(kv_ok.sem, 1)

            def project_q(a):
                project(a, D, lambda j: ps_s[j // 2][:, (j % 2) * D:(j % 2 + 1) * D], qnb, False)

            def z(a, backward):
                for j in range(NT):
                    dve.wait_ge(z_th.sem, z_th.at(a, j + 1))
                    dve.scalar_tensor_tensor(hp[:, j, :], tnh[:, j, :], 1.0, ps_s[j][:, :], ALU.add, ALU.mult)\
                       .then_inc(h_ok.sem, 1)
                if backward:
                    dve.wait_ge(h_ok.sem, h_ok.at(a))
                    dve.scalar_tensor_tensor(d2[:, :, :], tnh[:, :, :], 1.0, hp[:, :, :], ALU.subtract, ALU.mult)\
                       .then_inc(d2_ok.sem, 1)
                    dve.wait_ge(d2_ok.sem, d2_ok.at(a, 1))
                    dve.scalar_tensor_tensor(d2[:, :, :], d2[:, :, :], -0.5, tnh[:, :, :], ALU.mult, ALU.add)\
                       .then_inc(d2_ok.sem, 1)

            def normalise_y(a):
                dve.wait_ge(y_ri.sem, y_ri.at(a))
                for j in range(NT):
                    dve.tensor_scalar(yn[:, j, :], ps_s[j // 2][:, (j % 2) * D:(j % 2 + 1) * D],
                                      y_r[:, j:j + 1], None, ALU.mult).then_inc(y_n.sem, 1)
                dve.wait_ge(y_n.sem, y_n.at(a))

            def backward_y(a):
                normalise_y(a)
                k = [0]

                def step(ins):
                    k[0] += 1
                    ins.then_inc(bw.sem, 1)
                    dve.wait_ge(bw.sem, bw.at(a, k[0]))

                tt, mul, add = dve.tensor_tensor, ALU.mult, ALU.add
                step(tt(pr, yn[:, :, :], over_tiles(mem_ln), mul))
                step(tt(pr, pr, kv[:, :, :], add))
                step(tt(kv[:, :, :], pr, over_d(gate[:, 0:NT]), mul))
                step(tt(gy[:, :, :], kv[:, :, :], yn[:, :, :], mul))
                step(tt(pr, kv[:, :, :], over_tiles(mem_ln), mul))
                step(tt(kv[:, :, :], gy[:, :, :], over_tiles(mem_ln), mul))
                step(dve.tensor_reduce(dot, kv[:, :, :], AX.X, add))
                step(dve.tensor_scalar(dot_neg, dot, -1.0 / D, None, mul))
                for j in range(NT):
                    ins = dve.scalar_tensor_tensor(pr[:, j, :], yn[:, j, :], dot_neg[:, j:j + 1], pr[:, j, :], mul, add)
                    if j < NT - 1:
                        ins.then_inc(bw.sem, 1)
                        k[0] += 1
                    else:
                        step(ins)
                step(tt(pr, pr, over_d(y_r), mul))

            def output_y(a):
                normalise_y(a)
                dve.tensor_tensor(pr, yn[:, :, :], over_tiles(mem_ln), ALU.mult).then_inc(pred_v.sem, 1)
                dve.wait_ge(pred_v.sem, pred_v.at(a - NM, 1))
                dve.tensor_tensor(pr, pr, kn[:, :, :], ALU.add).then_inc(pred_v.sem, 1)
                dve.wait_ge(pred_v.sem, pred_v.at(a - NM))
                x = xt[:, a % 2, :, :]
                dve.tensor_tensor(x, x, pr, ALU.add).then_inc(x_att.sem, 1)

            def dz_step(a):
                for j in range(NT):
                    dve.wait_ge(dh_ps.sem, dh_ps.at(a, j + 1))
                    dve.scalar_tensor_tensor(dz[:, j, :], d2[:, j, :], 1.0, ps_s[j][:, :], ALU.add, ALU.mult)\
                       .then_inc(dz_ok.sem, 1)

            def norm_sum(a):
                dve.wait_ge(dw_sq.sem, dw_sq.at(a))
                dve.scalar_tensor_tensor(nrm_sum, nrm[:, 1:2], 1.0 / 128, nrm[:, 0:1], ALU.mult, ALU.add)\
                   .then_inc(n_v.sem, 1)

            def update(a):
                dve.wait_ge(n_ps.sem, n_ps.at(a))
                dve.tensor_copy(nrm_all, ps_s[0][:, 0:1]).then_inc(n_cp.sem, 1)
                dve.wait_ge(n_rt.sem, n_rt.at(a))
                total, inv, lim, scale = nrm_c
                dve.tensor_scalar(total, nrm_root, GRAD, 1e-6, ALU.mult, ALU.add).then_inc(clip.sem, 1)
                dve.wait_ge(clip.sem, clip.at(a, 1))
                dve.reciprocal(inv, total).then_inc(clip.sem, 1)
                dve.wait_ge(clip.sem, clip.at(a, 2))
                dve.tensor_scalar(lim, inv, 1.0, -GRAD, ALU.min, ALU.mult).then_inc(clip.sem, 1)
                dve.wait_ge(clip.sem, clip.at(a, 3))
                dve.tensor_scalar(grad[:, :], grad[:, :], lim, None, ALU.mult).then_inc(clip.sem, 1)
                dve.wait_ge(clip.sem, clip.at(a))
                dve.scalar_tensor_tensor(sur[:, :], sur[:, :], gate[:, NT + 1:NT + 2], grad[:, :], ALU.mult, ALU.add)\
                   .then_inc(upd.sem, 1)
                dve.wait_ge(upd.sem, upd.at(a, 1))
                dve.scalar_tensor_tensor(mem[:, :], mem[:, :], gate[:, NT:NT + 1], sur[:, :], ALU.mult, ALU.add)\
                   .then_inc(upd.sem, 1)
                dve.wait_ge(upd.sem, upd.at(a, 2))
                dve.tensor_copy(nrm_c[3], nrm_c[2]).then_inc(upd.sem, 1)

            def experts(M, fill, prep=()):
                hidden(M, 0)
                for e in range(NU):
                    if e < NU - 1:
                        hidden(M, e + 1)
                    if e in prep:
                        split_weights(e + 2)
                    for step in fill.get(2 * e, ()):
                        step()
                    accumulate(M, e)
                    for step in fill.get(2 * e + 1, ()):
                        step()

            def attn_ln(a):
                return lambda: layer_norm(1, a, (acc_ok, acc_ok.at(NU * a + E)), (b_ok, b_ok.at(a)))

            def scan_fill(a, M):
                return {
                    0: [attn_ln(a), lambda: gate_dots(a)],
                    1: [lambda: ln_low(1, a), lambda: gates(a)],
                    3: [lambda: project_kv(a)],
                    4: [lambda: biases(M)],
                    6: [lambda: z(a, True)],
                    9: [lambda: backward_y(a)],
                    12: [lambda: dz_step(a)],
                    14: [lambda: norm_sum(a)],
                    15: [lambda: update(a), lambda: layer_norm(0, M + 1, (x_ld, x_ld.at(M + 1)))],
                    16: [lambda: ln_low(0, M + 1)],
                    17: [lambda: router(M + 1)],
                }

            def apply_steps(a):
                return [lambda: layer_norm(1, a, (x_ld, x_ld.at(a))), lambda: ln_low(1, a),
                        lambda: project_q(a), lambda: z(a, False), lambda: output_y(a)]

            dve.wait_ge(c_in.sem, c_in.at(0))
            dve.tensor_scalar(cst[:, C_KN:C_KN + 2 * D], cst[:, C_KN:C_KN + 2 * D], 0.5 / (SX * SW), None,
                              ALU.mult).then_inc(nscale.sem, 1)
            dve.memset(wgt[:, :, E:NU], 1.0).then_inc(ones_col.sem, 1)
            dve.wait_ge(rw_h.sem, rw_h.at(0))
            low(rw_lo[:, :], cst[:, C_RW:C_RW + DC * E], rw_hi[:, :], SW).then_inc(rw_l.sem, 1)
            layer_norm(0, 0, (x_ld, x_ld.at(0)))
            ln_low(0, 0)
            split_weights(0)
            router(0)
            split_weights(1)
            experts(0, {4: [lambda: biases(0)], 15: [lambda: layer_norm(0, 1, (x_ld, x_ld.at(1)))],
                        16: [lambda: ln_low(0, 1)], 17: [lambda: router(1)]}, prep=range(NU - 1))
            dve.wait_ge(mem_ld.sem, mem_ld.at(0))
            dve.wait_ge(sur0.sem, sur0.at(0))
            dve.wait_ge(nscale.sem, nscale.at(0))
            with dve.Fori(1, NM - 1) as M:
                experts(M, scan_fill(M - 1, M))
            fill = scan_fill(NM - 2, NM - 1)
            fill[15] = fill[15][:1]
            del fill[16], fill[17]
            experts(NM - 1, fill)
            tail = scan_fill(NM - 1, NM - 1)
            for place in sorted(tail):
                if place in (4, 16, 17):
                    continue
                for step in tail[place][:1] if place == 15 else tail[place]:
                    step()
            for step in apply_steps(NM):
                step()
            layer_norm(0, NM, (x_att, x_att.at(0)))
            ln_low(0, NM)
            router(NM)
            with dve.Fori(NM, 2 * NM - 1) as M:
                steps = apply_steps(M + 1)
                experts(M, {4: [lambda: biases(M)], 6: steps[0:1], 7: steps[1:2], 8: steps[2:3],
                            10: steps[3:4], 13: steps[4:5],
                            15: [lambda: layer_norm(0, M + 1, (x_att, x_att.at(M + 1 - NM)))],
                            16: [lambda: ln_low(0, M + 1)], 17: [lambda: router(M + 1)]})
            M = 2 * NM - 1
            experts(M, {4: [lambda: biases(M)]})


def kernel(**inputs):
    import numpy as np
    import concourse.bacc as bacc
    from concourse import mybir as mb
    from concourse.bass_utils import run_bass_kernel_spmd

    def get(name):
        return np.asarray(inputs["L0_" + name])

    def by_rows(w):
        return w.reshape(-1, 128, w.shape[1]).transpose(1, 0, 2).reshape(128, -1)

    def on_all(row):
        return np.broadcast_to(row.reshape(1, -1), (128, row.size))

    x = get("attn_x").reshape(NT, 2, NM, CH, D).transpose(1, 3, 2, 0, 4).reshape(128, NM, NT * D)
    first = [get("ffn_rw1")[e] for e in range(E)] + [get("ffn_sw1")]
    second = [get("ffn_rw2")[e] for e in range(E)] + [get("ffn_sw2")]
    w_experts = np.stack([np.concatenate([by_rows(a), by_rows(b)], 1) for a, b in zip(first, second)], 1)
    wk, wv, wq = (get(f"attn_w{n}_w").T for n in "kvq")
    w_attn = np.concatenate([by_rows(np.concatenate([wk, wv], 1)), by_rows(wq)], 1)
    w0, w1 = get("attn_mem_w0"), get("attn_mem_w1")
    mem = np.concatenate([by_rows(w1.T), by_rows(w0.T), on_all(get("attn_mem_ln_w"))], 1)
    f32 = x.dtype
    p = np.arange(128)
    b1 = np.concatenate([get("ffn_rb1"), get("ffn_sb1")[None]]).reshape(NU * IC, 128).T
    b2 = np.zeros((128, D), f32)
    b2[0:E], b2[E] = get("ffn_rb2"), get("ffn_sb2")
    gate_w = [np.concatenate([get(f"attn_{n}_w").reshape(CH, D)] * 2) for n in ("theta", "alpha", "eta")]
    consts = np.concatenate([
        np.eye(128, dtype=f32), (p[:, None] // CH == p[None] // CH).astype(f32), np.ones((128, 128), f32),
        *gate_w, on_all(get("attn_k_norm_w")), on_all(get("attn_q_norm_w")), b1,
        on_all(get("ffn_router_b")), on_all(np.arange(E, 0, -1).astype(f32)), by_rows(get("ffn_router_w")), b2], 1)
    arrays = {"x_in": x, "w_experts": w_experts, "w_attn": w_attn, "mem_in": mem, "w1n_in": by_rows(w1),
              "consts_in": consts}
    arrays = {n: np.ascontiguousarray(a) for n, a in arrays.items()}

    nc = bacc.Bacc("TRN2", target_bir_lowering=False, num_devices=1)
    args = {n: nc.dram_tensor(n, a.shape, mb.dt.from_np(a.dtype), kind="ExternalInput").ap()
            for n, a in arrays.items()}
    args["out"] = nc.dram_tensor("out", (128, NM, NT * D), mb.dt.float32, kind="ExternalOutput").ap()
    macaron_kernel(nc, **args)
    got = run_bass_kernel_spmd(nc, [arrays], core_ids=[0]).results[0]["out"]
    return got.reshape(2, CH, NM, NT, D).transpose(3, 0, 2, 1, 4).reshape(B, S, D)
```

```python
import concourse.bass as bass
from concourse import mybir
from contextlib import ExitStack

B, S, D = 8, 512, 256
CH = 64
NM = S // CH
NT = B * CH // 128
TOK = NT * 128
I = 512
E = 8
NU = E + 1
DC, IC = D // 128, I // 128
B_LOW = 32
B_K = B_LOW + NU
WE = DC * I + IC * D
MEMW = IC * D + DC * I + D

SX = 64.0
SW = 64.0
SH = 16.0
SK = 16.0
LN_EPS, RMS_EPS = 1e-5, 1e-6
H_SCALE = 0.5 * SH / (SK * SW)
GRAD = 2.0 * 0.01 / (B * CH * D)

C_ID = 0
C_B1 = C_ID + 128
C_RB = C_B1 + NU * IC
C_REV = C_RB + E
C_RW = C_REV + E
C_BLK = C_RW + DC * E
C_ONE = C_BLK + 128
C_AW = C_ONE + 128
C_KN = C_AW + 3 * D
C_QN = C_KN + D
C_B2 = C_QN + D
NC_COLS = C_B2 + D


class Event:

    def __init__(self, sem, per):
        self.sem, self.per = sem, per

    def at(self, occurrence, k=None):
        return occurrence * self.per + (self.per if k is None else k)


def macaron_kernel(nc, x_in, w_experts, w_attn, mem_in, consts_in, out):
    F, H = mybir.dt.float32, mybir.dt.float16
    ALU, ACT, AX = mybir.AluOpType, mybir.ActivationFunctionType, mybir.AxisListType
    x1_dram = nc.dram_tensor("x1_scratch", (128, NM, NT * D), F, kind="Internal").ap()

    ctx = ExitStack()
    with ctx:
        def sb(name, shape, dt=F):
            return ctx.enter_context(nc.sbuf_tensor(name, shape, dt))

        def ev(name, per=1):
            return Event(ctx.enter_context(nc.semaphore(name)), per)

        we_hi = sb("we_hi", [128, NU, WE], H)
        we_lo = sb("we_lo", [128, NU, WE], H)
        wa_hi = sb("wa_hi", [128, 3 * DC * D], H)
        wa_lo = sb("wa_lo", [128, 3 * DC * D], H)
        rw_hi = sb("rw_hi", [128, DC * E], H)
        rw_lo = sb("rw_lo", [128, DC * E], H)
        cst = sb("cst", [128, C_B2])
        xt = sb("xt", [128, 2, NT, D])
        fx_hi = sb("fx_hi", [128, 2, DC, TOK], H)
        fx_lo = sb("fx_lo", [128, 2, DC, TOK], H)
        gel = sb("gel", [128, IC, TOK])
        hh = sb("hh", [128, 2, IC, TOK], H)
        hl = sb("hl", [128, 2, IC, TOK], H)
        mem = sb("mem", [128, MEMW])
        sur = sb("sur", [128, MEMW])
        w1n = sb("w1n", [128, DC, I])
        reg_a = sb("reg_a", [128, MEMW])
        reg_b = sb("reg_b", [128, WE])
        reg_c = sb("reg_c", [128, NT, D])
        reg_d = sb("reg_d", [128, NT, D])
        reg_e = sb("reg_e", [128, NT * D])
        reg_f = sb("reg_f", [128, DC, TOK])
        kn = sb("kn", [128, NT, D])
        kv = sb("kv", [128, NT, D])
        hp = sb("hp", [128, NT, I])
        d2 = sb("d2", [128, NT, I])
        stats = sb("stats", [128, 2, NT, 6])
        mv = sb("mv", [128, 2, NT, 2])
        sm = sb("sm", [128, 128])
        lg = sb("lg", [128, 10, NT, E])
        wgt = sb("wgt", [128, NT, B_K], H)
        b2p = sb("b2p", [128, D], H)
        ident_h = sb("ident_h", [128, 128], H)
        wacc = sb("wacc", [128, 2, NT, E])
        wgt_t = d2[:, 0, :].bitcast(H)[0:B_K, 0:TOK].rearrange("u (j t) -> u j t", j=NT)

        ident = cst[:, C_ID:C_ID + 128]
        blk = cst[:, C_BLK:C_BLK + 128]
        ones = cst[:, C_ONE:C_ONE + 128]
        aw = cst[:, C_AW:C_AW + 3 * D].rearrange("p (g d) -> p g d", g=3)
        knb, qnb = cst[:, C_KN:C_KN + D], cst[:, C_QN:C_QN + D]
        rb = cst[:, C_RB:C_RB + E]
        rev = cst[:, C_REV:C_REV + E]
        b2 = sur[:, 0:D]

        def parts(region, chunks, width):
            both = region.bitcast(H)
            n = chunks * width
            return tuple(both[:, k * n:(k + 1) * n].rearrange("p (c w) -> p c w", c=chunks) for k in range(2))

        stage = [reg_a[:, 0:WE], reg_b[:, :]]
        tnh = reg_a[:, 0:NT * I].rearrange("p (j i) -> p j i", j=NT)
        ht_hi, ht_lo = parts(reg_a[:, 0:IC * TOK], IC, TOK)
        grad = reg_a
        sp = reg_b[:, :].rearrange("p (j i) -> p j i", j=NT)
        dz = sp
        xna, yn = reg_c, reg_c
        gy = reg_d
        reg_b4 = reg_b[:, 0:NT * D].rearrange("p (j d) -> p j d", j=NT)

        def xnf(M):
            return reg_d if isinstance(M, int) and M < 2 else reg_b4

        ax_hi, ax_lo = parts(reg_e[:, :], DC, TOK)
        pr = reg_e[:, :].rearrange("p (j d) -> p j d", j=NT)
        kt_hi, kt_lo = parts(reg_f[:, :, :].rearrange("p c t -> p (c t)"), DC, TOK)
        dyt = reg_f
        w0_hi, w0_lo = parts(d2[:, 2:4, :].rearrange("p a i -> p (a i)"), DC, I)
        w1_hi, w1_lo = parts(reg_d[:, :, :].rearrange("p j d -> p (j d)"), IC, D)
        tnh_q = hp
        junk = reg_f[:, 0, 0:D]
        mem_w1t = mem[:, 0:IC * D].rearrange("p (c d) -> p c d", c=IC)
        mem_w0t = mem[:, IC * D:IC * D + DC * I].rearrange("p (c i) -> p c i", c=DC)
        mem_ln = mem[:, IC * D + DC * I:MEMW]

        at_sm = [0]

        def col(n):
            at_sm[0] += n
            return sm[:, at_sm[0] - n:at_sm[0]]

        var_eps, rstd = [col(NT), col(NT)], [col(NT), col(NT)]
        neg_half, pos_half, ln_eps, rms_eps, unscale = col(NT), col(1), col(NT), col(NT), col(NT)
        gate_dot = col(3 * NT)
        gate_in, gate_tanh, gate = col(NT + 2), col(NT + 2), col(NT + 2)
        k_ms, k_ms_eps, k_r = col(NT), col(NT), col(NT)
        y_ms, y_ms_eps, y_r, y_rs, theta_r = (col(NT) for _ in range(5))
        dot, dot_neg = col(NT), col(NT)
        nrm, nrm_sum, nrm_all, nrm_root = col(2), col(1), col(1), col(1)
        nrm_c = [col(1) for _ in range(3)]
        waited = [col(1) for _ in range(5)]

        def bank(name):
            return ctx.enter_context(nc.psum_tensor(name, [128, 512], F))

        ps_h = [bank(f"ps_h{i}") for i in range(2)]
        ps_y = [bank(f"ps_y{i}") for i in range(2)]
        ps_s = [bank(f"ps_s{i}") for i in range(4)]

        c_in, c_rest = ev("constants_loaded", 16), ev("more_constants_loaded", 16)
        mem_ld = ev("memory_loaded", 16)
        stage_ld = [ev(f"stage{i}_loaded", 16) for i in range(2)]
        x_ld = ev("x_loaded", 16)
        x_st = ev("x_stored", 16)
        pool_c = ev("pool_constants", 5)
        w_hi, w_lo = ev("weights_hi"), ev("weights_lo")
        rw_h, rw_l = ev("router_weights_hi"), ev("router_weights_lo")
        nscale = ev("norm_weights_scaled")
        ones_col = ev("shared_weight_set", 3)
        id_h = ev("identity_in_fp16")
        b2_ld = ev("biases_loaded", 16)
        b2_h, b2_l = ev("biases_hi"), ev("biases_lo")
        mm1_ps = ev("hidden_in_psum", IC)
        gelu_ok, hid_hi, hid_lo = ev("gelu_done", IC), ev("hidden_hi", IC), ev("hidden_lo", IC)
        mm2_ps = ev("expert_out_in_psum", 2)
        acc_ok = ev("expert_out_added", 2)
        nm = ["ffn", "attn"]
        ln_st = [ev(f"{n}_ln_stats", NT) for n in nm]
        ln_mv = [ev(f"{n}_ln_mean_var", NT) for n in nm]
        ln_ve = [ev(f"{n}_ln_var_eps") for n in nm]
        ln_rs = [ev(f"{n}_ln_rstd") for n in nm]
        ln_xn = [ev(f"{n}_ln_out", NT) for n in nm]
        ln_tp = [ev(f"{n}_lnT_in_psum", DC) for n in nm]
        ln_hi = [ev(f"{n}_lnT_hi", DC) for n in nm]
        ln_lo = [ev(f"{n}_lnT_lo", DC) for n in nm]
        lg_ps, lg_v = ev("logits_in_psum"), ev("router_steps", 21)
        ex_ok = ev("router_exp")
        wt_ps, wt_ok = ev("weightsT_in_psum"), ev("weightsT_copied")
        b_ps, b_ok = ev("bias_in_psum", 2), ev("bias_added", 2)
        g_v, g_ps, g_th, g_ok = ev("gate_dots", 3), ev("gates_in_psum"), ev("gate_tanh", 2), ev("gates", 2)
        p_ps, p_th, p_s = ev("proj_in_psum", NT), ev("proj_tanh", NT), ev("proj_silu", NT)
        p_sq, p_ve, p_r = ev("k_mean_square", NT), ev("k_ms_eps"), ev("k_rms_inv")
        k_ok, kv_ok = ev("k_done", NT), ev("k_minus_v")
        kt_ps, kt_h, kt_ok = ev("kT_in_psum", DC), ev("kT_hi", DC), ev("kT_lo", DC)
        z_ps, z_th, h_ok = ev("z_in_psum", NT), ev("z_tanh", NT), ev("hidden_mem", NT)
        d2_ok = ev("silu_derivative", 2)
        ht_ps, ht_h, ht_ok = ev("hT_in_psum", IC), ev("hT_hi", IC), ev("hT_lo", IC)
        y_ps, y_sq, y_ve, y_ri = ev("y_in_psum", 2), ev("y_mean_square", NT), ev("y_ms_eps"), ev("y_rms_inv", 2)
        y_n = ev("y_normalised", NT)
        pred_v = ev("memory_out", 2)
        x_att = ev("attention_added")
        tr_ok, bw, dy_ok = ev("theta_over_rms"), ev("backward_steps", 5), ev("dy_done", NT)
        gy_ok = ev("ln_grad_steps", 4)
        dln_ps, dln_ok = ev("dln_in_psum"), ev("dln_copied")
        dyt_ps, dyt_ok = ev("dyT_in_psum", DC), ev("dyT_copied", DC)
        dh_ps, dz_ok = ev("dh_in_psum", NT), ev("dz_done", NT)
        dw_ps, dw_ok, dw_sq = ev("dW_in_psum", 4), ev("dW_copied", 4), ev("grad_squares", 2)
        n_v, n_sum, n_rt = ev("norm_partial"), ev("norm_summed"), ev("norm_root")
        clip = ev("clip_steps", 4)
        sur_ok = ev("surprise_updated")
        mem_hi, mem_lo = ev("memory_hi", 2), ev("memory_lo", 2)
        mem_ok = ev("memory_in_place")
        w1_ps, w1_ok = ev("w1_in_psum", DC), ev("w1_copied", DC)

        block = ctx.enter_context(nc.Block())

        @block.sync
        def _(sp_eng):
            eng = sp_eng

            def load_x(M, src):
                eng.dma_start(xt[:, M % 2, :, :].rearrange("p j d -> p (j d)"), src)\
                   .then_inc(x_ld.sem, 16)

            eng.dma_start(xt[:, 0, :, :].rearrange("p j d -> p (j d)"), x_in[:, 0, :]).then_inc(x_ld.sem, 16)
            for k in range(2):
                eng.dma_start(stage[k], w_experts[:, k, :]).then_inc(stage_ld[k].sem, 16)
            eng.dma_start(cst[:, C_BLK:C_B2], consts_in[:, C_BLK:C_B2]).then_inc(c_rest.sem, 16)
            eng.dma_start(b2, consts_in[:, C_B2:NC_COLS]).then_inc(b2_ld.sem, 16)
            eng.dma_start(mem[:, :], mem_in).then_inc(mem_ld.sem, 16)
            eng.wait_ge(x_ld.sem, x_ld.at(0))
            load_x(1, x_in[:, 1, :])
            for k in range(2, NU + 1):
                eng.wait_ge(w_lo.sem, w_lo.at(k - 2))
                if k < NU:
                    eng.dma_start(stage[k % 2], w_experts[:, k, :]).then_inc(stage_ld[k % 2].sem, 16)
                else:
                    eng.dma_start(stage[k % 2][:, 0:3 * DC * D], w_attn).then_inc(stage_ld[k % 2].sem, 16)

            def store(M, dst):
                eng.wait_ge(acc_ok.sem, acc_ok.at(NU * M + E))
                eng.wait_ge(b_ok.sem, b_ok.at(M))
                eng.dma_start(dst, xt[:, M % 2, :, :].rearrange("p j d -> p (j d)"))\
                   .then_inc(x_st.sem, 16)

            def turn_over(M, dst, src):
                store(M - 1, dst)
                eng.wait_ge(x_st.sem, x_st.at(M - 1))
                load_x(M + 1, src)

            with eng.Fori(1, NM - 1) as M:
                eng.wait_ge(ln_xn[1].sem, ln_xn[1].at(M - 1))
                turn_over(M, x1_dram[:, M - 1, :], x_in[:, M + 1, :])
            for M in (NM - 1, NM):
                eng.wait_ge(ln_xn[1].sem, ln_xn[1].at(M - 1))
                turn_over(M, x1_dram[:, M - 1, :], x1_dram[:, M + 1 - NM, :])
            with eng.Fori(NM + 1, 2 * NM - 1) as M:
                turn_over(M, out[:, M - 1 - NM, :], x1_dram[:, M + 1 - NM, :])
            store(2 * NM - 2, out[:, NM - 2, :])
            store(2 * NM - 1, out[:, NM - 1, :])
            eng.wait_ge(x_st.sem, x_st.at(2 * NM - 1))

        @block.gpsimd
        def _(pool):
            pool.memset(neg_half, -0.5).then_inc(pool_c.sem, 1)
            pool.memset(pos_half, 0.5).then_inc(pool_c.sem, 1)
            pool.memset(ln_eps, LN_EPS).then_inc(pool_c.sem, 1)
            pool.memset(rms_eps, RMS_EPS).then_inc(pool_c.sem, 1)
            pool.memset(unscale, 1.0 / (SH * SW)).then_inc(pool_c.sem, 1)
            pool.wait_ge(pool_c.sem, pool_c.at(0))

            def ln_rstd(n, occ):
                pool.wait_ge(ln_mv[n].sem, ln_mv[n].at(occ))
                pool.tensor_tensor(var_eps[n], mv[:, n, :, 1], ln_eps, ALU.add)\
                    .then_inc(ln_ve[n].sem, 1)
                pool.wait_ge(ln_ve[n].sem, ln_ve[n].at(occ))
                pool.tensor_tensor(rstd[n], var_eps[n], neg_half, ALU.pow).then_inc(ln_rs[n].sem, 1)

            def rms_inv(ms, ms_eps, r, have, mid, done, occ):
                pool.wait_ge(have.sem, have.at(occ))
                pool.tensor_tensor(ms_eps, ms, rms_eps, ALU.add).then_inc(mid.sem, 1)
                pool.wait_ge(mid.sem, mid.at(occ))
                pool.tensor_tensor(r, ms_eps, neg_half, ALU.pow).then_inc(done.sem, 1)

            def k_rms(a):
                rms_inv(k_ms, k_ms_eps, k_r, p_sq, p_ve, p_r, a)

            def y_rms(a):
                rms_inv(y_ms, y_ms_eps, y_r, y_sq, y_ve, y_ri, a)
                pool.wait_ge(y_ri.sem, y_ri.at(a, 1))
                pool.tensor_tensor(y_rs, y_r, unscale, ALU.mult).then_inc(y_ri.sem, 1)

            def ln_grad(a):
                pool.wait_ge(bw.sem, bw.at(a, 2))
                theta = gate[:, 0:NT].unsqueeze(2).to_broadcast([128, NT, D])
                for n, (dst, x, y, op) in enumerate(((gy[:, :, :], kv[:, :, :], theta, ALU.mult),
                                                     (gy[:, :, :], gy[:, :, :], yn[:, :, :], ALU.mult),
                                                     (gy[:, 0:2, :], gy[:, 0:2, :], gy[:, 2:4, :], ALU.add),
                                                     (gy[:, 0, :], gy[:, 0, :], gy[:, 1, :], ALU.add))):
                    if n > 0:
                        pool.wait_ge(gy_ok.sem, gy_ok.at(a, n))
                    pool.tensor_tensor(dst, x, y, op).then_inc(gy_ok.sem, 1)

            def scan(a, next_tile=None, after_y=None):
                ln_rstd(1, a)
                k_rms(a)
                if next_tile is not None:
                    ln_rstd(0, next_tile)
                y_rms(a)
                pool.wait_ge(g_ok.sem, g_ok.at(a))
                pool.tensor_tensor(theta_r, y_r, gate[:, 0:NT], ALU.mult).then_inc(tr_ok.sem, 1)
                ln_grad(a)
                if after_y is not None:
                    after_y()
                pool.wait_ge(n_v.sem, n_v.at(a))
                pool.tensor_tensor(waited[4], rms_eps[:, 0:1], rms_eps[:, 0:1], ALU.add)
                pool.partition_all_reduce(nrm_all, nrm_sum, 128, bass.bass_isa.ReduceOp.add).then_inc(n_sum.sem, 1)
                pool.wait_ge(n_sum.sem, n_sum.at(a))
                pool.tensor_tensor(nrm_root, nrm_all, pos_half, ALU.pow).then_inc(n_rt.sem, 1)

            def apply(a):
                ln_rstd(1, a)
                k_rms(a)
                y_rms(a)

            ln_rstd(0, 0)
            ln_rstd(0, 1)
            scan(0, 2)
            with pool.Fori(2, NM - 1) as M:
                scan(M - 1, M + 1)
            scan(NM - 2)
            scan(NM - 1, after_y=lambda: ln_rstd(1, NM))
            k_rms(NM)
            y_rms(NM)
            ln_rstd(0, NM)
            with pool.Fori(NM, 2 * NM - 1) as M:
                apply(M + 1)
                ln_rstd(0, M + 1)

        @block.tensor
        def _(pe):
            def products(out_ap, pairs):
                for n, (lhs, rhs) in enumerate(pairs):
                    last = pe.matmul(out_ap, lhs, rhs, start=(n == 0), stop=(n == len(pairs) - 1))
                return last

            def guard(*waits):
                for event, value in waits:
                    pe.wait_ge(event.sem, value)

            def mm1(M, e):
                u = NU * M + e
                for c in range(IC):
                    if not (isinstance(M, int) and M == 0 and e == 0 and c < 2):
                        pe.wait_ge(gelu_ok.sem, gelu_ok.at(u, c - 1))
                    pairs = []
                    for dc in range(DC):
                        w = slice(dc * I + c * 128, dc * I + (c + 1) * 128)
                        pairs += [(we_hi[:, e, w], fx_hi[:, M % 2, dc, :]), (we_hi[:, e, w], fx_lo[:, M % 2, dc, :]),
                                  (we_lo[:, e, w], fx_hi[:, M % 2, dc, :])]
                    products(ps_h[c % 2][:, :], pairs).then_inc(mm1_ps.sem, 1)

            def mm2(M, e):
                u = NU * M + e
                pe.wait_ge(hid_lo.sem, hid_lo.at(u))
                for b in range(2):
                    if not (isinstance(M, int) and M == 0 and e == 0):
                        pe.wait_ge(acc_ok.sem, acc_ok.at(u - 1, b + 1))
                    for j in (2 * b, 2 * b + 1):
                        pairs = []
                        for c in range(IC):
                            w = slice(DC * I + c * D, DC * I + (c + 1) * D)
                            t = slice(j * 128, (j + 1) * 128)
                            pairs += [(hh[:, e % 2, c, t], we_hi[:, e, w]), (hh[:, e % 2, c, t], we_lo[:, e, w]),
                                      (hl[:, e % 2, c, t], we_hi[:, e, w])]
                        last = products(ps_y[b][:, (j % 2) * D:(j % 2 + 1) * D], pairs)
                    last.then_inc(mm2_ps.sem, 1)

            def transposes(src, banks, done, occ_wait, *guards):
                guard(occ_wait, *guards)
                for c, ps in enumerate(banks):
                    for j in range(NT):
                        last = pe.transpose(ps[:, j * 128:(j + 1) * 128], src[:, j, c * 128:(c + 1) * 128], ident)
                    last.then_inc(done.sem, 1)

            def ln_t(n, occ, *guards):
                src, banks = (xnf(occ), ps_s[2:4]) if n == 0 else (xna, ps_s[0:2])
                transposes(src, banks, ln_tp[n], (ln_xn[n], ln_xn[n].at(occ)), *guards)

            def router(M, *guards):
                guard((ln_lo[0], ln_lo[0].at(M)), *guards)
                for j in range(NT):
                    t = slice(j * 128, (j + 1) * 128)
                    pairs = []
                    for c in range(DC):
                        w = slice(c * E, (c + 1) * E)
                        x_hi, x_lo = fx_hi[:, M % 2, c, t], fx_lo[:, M % 2, c, t]
                        pairs += [(x_hi, rw_hi[:, w]), (x_hi, rw_lo[:, w]), (x_lo, rw_hi[:, w])]
                    last = products(ps_s[2][:, j * E:(j + 1) * E], pairs)
                last.then_inc(lg_ps.sem, 1)

            def weights_t(M):
                guard((lg_v, lg_v.at(M)))
                for j in range(NT):
                    last = pe.matmul(ps_s[3][0:B_K, j * 128:(j + 1) * 128], wgt[:, j, :], ident_h[:, :],
                                     start=True, stop=True)
                last.then_inc(wt_ps.sem, 1)

            def biases(M, *guards):
                guard((wt_ok, wt_ok.at(M)), *guards)
                for b in range(2):
                    for j in (2 * b, 2 * b + 1):
                        last = pe.matmul(ps_s[b][:, (j % 2) * D:(j % 2 + 1) * D], wgt_t[:, j, :], b2p[0:B_K, :],
                                         start=True, stop=True)
                    last.then_inc(b_ps.sem, 1)

            def gates(a, *guards):
                guard((g_v, g_v.at(a)), *guards)
                pe.matmul(ps_s[2][:, 0:NT], blk, gate_in[:, 0:NT], start=True, stop=True)
                pe.matmul(ps_s[2][:, NT:NT + 2], ones, gate_in[:, NT:NT + 2], start=True, stop=True)\
                  .then_inc(g_ps.sem, 1)

            def project(a, first, width, where, *guards):
                guard((ln_lo[1], ln_lo[1].at(a)), *guards)
                for j in range(NT):
                    t = slice(j * 128, (j + 1) * 128)
                    pairs = []
                    for c in range(DC):
                        w = slice(first + c * width, first + (c + 1) * width)
                        pairs += [(ax_hi[:, c, t], wa_hi[:, w]), (ax_hi[:, c, t], wa_lo[:, w]),
                                  (ax_lo[:, c, t], wa_hi[:, w])]
                    products(where(j), pairs).then_inc(p_ps.sem, 1)

            def project_kv(a, *guards):
                project(a, 0, 2 * D, lambda j: ps_s[j][:, :], *guards)

            def project_q(a, *guards):
                project(a, 2 * DC * D, D, lambda j: ps_s[j // 2][:, (j % 2) * D:(j % 2 + 1) * D], *guards)

            def k_t(a, *guards):
                transposes(kn, ps_s[2:4], kt_ps, (k_ok, k_ok.at(a)), *guards)

            def z(a, *guards):
                guard((kt_ok, kt_ok.at(a)), *guards)
                for j in range(NT):
                    t = slice(j * 128, (j + 1) * 128)
                    pairs = []
                    for c in range(DC):
                        pairs += [(kt_hi[:, c, t], w0_hi[:, c, :]), (kt_hi[:, c, t], w0_lo[:, c, :]),
                                  (kt_lo[:, c, t], w0_hi[:, c, :])]
                    products(ps_s[j][:, :], pairs).then_inc(z_ps.sem, 1)

            def z_t(a, *guards):
                guard((kt_ok, kt_ok.at(a)), *guards)
                for c in range(IC):
                    w = slice(c * 128, (c + 1) * 128)
                    pairs = []
                    for dc in range(DC):
                        pairs += [(w0_hi[:, dc, w], kt_hi[:, dc, :]), (w0_hi[:, dc, w], kt_lo[:, dc, :]),
                                  (w0_lo[:, dc, w], kt_hi[:, dc, :])]
                    products(ps_s[c][:, :], pairs).then_inc(z_ps.sem, 1)

            def h_t(a, *guards):
                transposes(hp, ps_s, ht_ps, (h_ok, h_ok.at(a)), *guards)

            def y(a):
                guard((ht_ok, ht_ok.at(a)))
                for b in range(2):
                    for j in (2 * b, 2 * b + 1):
                        t = slice(j * 128, (j + 1) * 128)
                        pairs = []
                        for c in range(IC):
                            pairs += [(ht_hi[:, c, t], w1_hi[:, c, :]), (ht_hi[:, c, t], w1_lo[:, c, :]),
                                      (ht_lo[:, c, t], w1_hi[:, c, :])]
                        last = products(ps_s[b][:, (j % 2) * D:(j % 2 + 1) * D], pairs)
                    last.then_inc(y_ps.sem, 1)

            def dln_dyt(a):
                transposes(pr, ps_s[2:4], dyt_ps, (dy_ok, dy_ok.at(a)))
                guard((gy_ok, gy_ok.at(a)), (w1_ok, w1_ok.at(a)))
                products(ps_s[0][:, 0:D], [(ones, gy[:, 0, :])]).then_inc(dln_ps.sem, 1)

            def dh(a):
                guard((dyt_ok, dyt_ok.at(a)), (dln_ok, dln_ok.at(a)))
                for j in range(NT):
                    t = slice(j * 128, (j + 1) * 128)
                    products(ps_s[j][:, :], [(dyt[:, c, t], w1n[:, c, :]) for c in range(DC)])\
                        .then_inc(dh_ps.sem, 1)

            def dw(a):
                guard((dz_ok, dz_ok.at(a)))
                for b in range(2):
                    for c in (2 * b, 2 * b + 1):
                        last = products(ps_s[b][:, (c % 2) * D:(c % 2 + 1) * D],
                                        [(hp[:, j, c * 128:(c + 1) * 128], pr[:, j, :]) for j in range(NT)])
                    last.then_inc(dw_ps.sem, 1)
                for c in range(DC):
                    products(ps_s[2 + c][:, :],
                             [(kn[:, j, c * 128:(c + 1) * 128], dz[:, j, :]) for j in range(NT)])\
                        .then_inc(dw_ps.sem, 1)

            def w1_natural(a, *guards):
                guard((mem_ok, mem_ok.at(a)), *guards)
                for dc in range(DC):
                    for c in range(IC):
                        last = pe.transpose(ps_s[dc][:, c * 128:(c + 1) * 128],
                                            mem_w1t[:, c, dc * 128:(dc + 1) * 128], ident)
                    last.then_inc(w1_ps.sem, 1)

            def experts(M, fill, first=False):
                guard((ln_lo[0], ln_lo[0].at(M)))
                if first:
                    guard((w_lo, w_lo.at(0)))
                mm1(M, 0)
                for e in range(NU):
                    if e < NU - 1:
                        if first:
                            guard((w_lo, w_lo.at(e + 1)))
                        mm1(M, e + 1)
                    for step in fill.get(2 * e, ()):
                        step()
                    mm2(M, e)
                    for step in fill.get(2 * e + 1, ()):
                        step()

            def scan_fill(a, M, more=True):
                fill = {
                    2: [lambda: ln_t(1, a), lambda: weights_t(M)],
                    4: [lambda: project_kv(a, (wt_ok, wt_ok.at(M)))],
                    5: [lambda: biases(M, (p_s, p_s.at(a))), lambda: gates(a)],
                    6: [lambda: k_t(a, (g_th, g_th.at(a)))],
                    7: [lambda: z(a, (b_ok, b_ok.at(M)), (mem_lo, mem_lo.at(a)))],
                    9: [lambda: h_t(a)],
                    10: [lambda: y(a)],
                    12: [lambda: w1_natural(a, (y_n, y_n.at(a)))],
                    13: [lambda: dln_dyt(a)],
                    14: [lambda: dh(a)],
                    15: [lambda: dw(a)],
                }
                if more:
                    fill[8] = [lambda: ln_t(0, M + 1, (h_ok, h_ok.at(a)))]
                    fill[9] = [lambda: h_t(a, (ln_lo[0], ln_lo[0].at(M + 1)))]
                    fill[11] = [lambda: router(M + 1, (ht_ok, ht_ok.at(a)))]
                    fill[13] = [lambda: guard((lg_v, lg_v.at(M + 1, 1))), lambda: dln_dyt(a)]
                return fill

            def apply_steps(a, *guards):
                return [lambda: ln_t(1, a, *guards), lambda: project_q(a), lambda: k_t(a),
                        lambda: z_t(a), lambda: y(a)]

            guard((c_in, c_in.at(0)))
            ln_t(0, 0)
            guard((rw_l, rw_l.at(0)))
            router(0)
            experts(0, {2: [lambda: guard((id_h, id_h.at(0))), lambda: weights_t(0)],
                        5: [lambda: biases(0, (b2_l, b2_l.at(0)))], 8: [lambda: ln_t(0, 1, (wt_ok, wt_ok.at(0)))], 10: [lambda: router(1)]}, first=True)
            guard((w_lo, w_lo.at(NU)))
            experts(1, scan_fill(0, 1))
            with pe.Fori(2, NM - 1) as M:
                experts(M, scan_fill(M - 1, M))
            experts(NM - 1, scan_fill(NM - 2, NM - 1, more=False))
            tail = scan_fill(NM - 1, NM - 1, more=False)
            tail[2].pop()
            tail[5] = [lambda: gates(NM - 1, (p_s, p_s.at(NM - 1)))]
            for place in sorted(tail):
                for step in tail[place]:
                    step()
            for step in apply_steps(NM, (dw_ok, dw_ok.at(NM - 1)))[0:3]:
                step()
            guard((mem_lo, mem_lo.at(NM)))
            for step in apply_steps(NM)[3:]:
                step()
            ln_t(0, NM)
            router(NM)

            def apply_fill(M):
                steps = apply_steps(M + 1)
                return {2: [steps[0], lambda: weights_t(M)], 4: steps[1:2],
                        5: [lambda: biases(M, (p_s, p_s.at(M + 1)))], 6: steps[2:3],
                        8: [lambda: guard((b_ok, b_ok.at(M))), steps[3]], 10: steps[4:5],
                        14: [lambda: ln_t(0, M + 1)], 15: [lambda: router(M + 1)]}

            with pe.Fori(NM, 2 * NM - 1) as M:
                experts(M, apply_fill(M))
            M = 2 * NM - 1
            experts(M, {2: [lambda: weights_t(M)], 5: [lambda: biases(M)]})

        @block.scalar
        def _(act):
            act.dma_start(cst[:, 0:C_BLK], consts_in[:, 0:C_BLK]).then_inc(c_in.sem, 16)

            def copy(dst, src, scale=1.0):
                return act.activation(dst, src, ACT.Copy, scale=scale)

            def split_weights(k):
                act.wait_ge(stage_ld[k % 2].sem, stage_ld[k % 2].at(k // 2))
                if k < NU:
                    copy(we_hi[:, k, :], stage[k % 2], SW).then_inc(w_hi.sem, 1)
                else:
                    copy(wa_hi[:, :], stage[k % 2][:, 0:3 * DC * D], SW).then_inc(w_hi.sem, 1)

            def hidden(M, e):
                u = NU * M + e
                first = isinstance(M, int) and M == 0 and e == 0

                def high(c):
                    if c == 0 and not (isinstance(M, int) and M == 0 and e < 2):
                        act.wait_ge(mm2_ps.sem, mm2_ps.at(u - (1 if e == 0 else 2)))
                    act.wait_ge(gelu_ok.sem, gelu_ok.at(u, c + 1))
                    copy(hh[:, e % 2, c, :], gel[:, c, :], SH).then_inc(hid_hi.sem, 1)

                for c in range(IC):
                    act.wait_ge(mm1_ps.sem, mm1_ps.at(u, c + 1))
                    if not first:
                        act.wait_ge(hid_lo.sem, hid_lo.at(u - 1, c + 1))
                    act.activation(gel[:, c, :], ps_h[c % 2][:, :], ACT.Gelu, scale=1.0 / (SX * SW),
                                   bias=cst[:, C_B1 + e * IC + c:C_B1 + e * IC + c + 1])\
                       .then_inc(gelu_ok.sem, 1)
                    if c > 0:
                        high(c - 1)
                high(IC - 1)

            def ln_high(n, occ):
                dst, banks = (fx_hi[:, occ % 2, :, :], ps_s[2:4]) if n == 0 else (ax_hi, ps_s[0:2])
                for c in range(DC):
                    act.wait_ge(ln_tp[n].sem, ln_tp[n].at(occ, c + 1))
                    copy(dst[:, c, :], banks[c][:, :], SX).then_inc(ln_hi[n].sem, 1)

            def router_exp(M):
                act.wait_ge(lg_v.sem, lg_v.at(M, 3))
                act.activation(lg[:, 2, :, :], lg[:, 1, :, :], ACT.Exp).then_inc(ex_ok.sem, 1)

            def weights_t(M):
                act.wait_ge(wt_ps.sem, wt_ps.at(M))
                copy(wgt_t.rearrange("u j t -> u (j t)"), ps_s[3][0:B_K, :]).then_inc(wt_ok.sem, 1)

            def gates(a):
                act.wait_ge(g_ps.sem, g_ps.at(a))
                act.activation(gate_tanh[:, 0:NT], ps_s[2][:, 0:NT], ACT.Tanh, scale=0.5).then_inc(g_th.sem, 1)
                act.activation(gate_tanh[:, NT:NT + 2], ps_s[2][:, NT:NT + 2], ACT.Tanh, scale=0.5 / B)\
                   .then_inc(g_th.sem, 1)

            def project(a, width, where, ready, dst):
                for j in range(NT):
                    act.wait_ge(p_ps.sem, p_ps.at(a, ready(j)))
                    act.activation(dst[:, j, 0:width], where(j), ACT.Tanh, scale=0.5 / (SX * SW))\
                       .then_inc(p_th.sem, 1)
                for j in range(NT):
                    act.wait_ge(p_s.sem, p_s.at(a, j + 1))
                    act.wait_ge(p_sq.sem, p_sq.at(a, j))
                    act.activation(junk, sp[:, j, 0:D], ACT.Square, scale=1.0 / (2 * SX * SW * D ** 0.5),
                                   accum_out=k_ms[:, j:j + 1]).then_inc(p_sq.sem, 1)

            def project_kv(a):
                project(a, 2 * D, lambda j: ps_s[j][:, :], lambda j: j + 1, tnh)

            def project_q(a):
                project(a, D, lambda j: ps_s[j // 2][:, (j % 2) * D:(j % 2 + 1) * D],
                        lambda j: 2 * (j // 2) + 2, tnh_q)

            def k_t(a):
                act.wait_ge(p_sq.sem, p_sq.at(a))
                for c in range(DC):
                    act.wait_ge(kt_ps.sem, kt_ps.at(a, c + 1))
                    copy(kt_hi[:, c, :], ps_s[2 + c][:, :], SK).then_inc(kt_h.sem, 1)

            def z(a):
                for j in range(NT):
                    act.wait_ge(z_ps.sem, z_ps.at(a, j + 1))
                    act.activation(tnh[:, j, :], ps_s[j][:, :], ACT.Tanh, scale=0.5 / (SK * SW)).then_inc(z_th.sem, 1)

            def h_t(a):
                act.wait_ge(d2_ok.sem, d2_ok.at(a))
                for c in range(IC):
                    act.wait_ge(ht_ps.sem, ht_ps.at(a, c + 1))
                    copy(ht_hi[:, c, :], ps_s[c][:, :], H_SCALE).then_inc(ht_h.sem, 1)

            def h_high(a):
                for c in range(IC):
                    act.wait_ge(h_ok.sem, h_ok.at(a, c + 1))
                    copy(ht_hi[:, c, :], hp[:, c, :], H_SCALE).then_inc(ht_h.sem, 1)

            def y(a):
                for j in range(NT):
                    act.wait_ge(y_ps.sem, y_ps.at(a, j // 2 + 1))
                    act.wait_ge(y_sq.sem, y_sq.at(a, j))
                    act.activation(junk, ps_s[j // 2][:, (j % 2) * D:(j % 2 + 1) * D], ACT.Square,
                                   scale=1.0 / (SH * SW * D ** 0.5), accum_out=y_ms[:, j:j + 1]).then_inc(y_sq.sem, 1)

            def y_norm(a):
                act.wait_ge(y_ri.sem, y_ri.at(a))
                for j in range(NT):
                    copy(yn[:, j, :], ps_s[j // 2][:, (j % 2) * D:(j % 2 + 1) * D], y_rs[:, j:j + 1])\
                        .then_inc(y_n.sem, 1)

            def dyt_copy(a):
                for c in range(DC):
                    act.wait_ge(dyt_ps.sem, dyt_ps.at(a, c + 1))
                    copy(dyt[:, c, :], ps_s[2 + c][:, :]).then_inc(dyt_ok.sem, 1)
                act.wait_ge(dln_ps.sem, dln_ps.at(a))
                copy(grad[:, IC * D + DC * I:MEMW], ps_s[0][:, 0:D]).then_inc(dln_ok.sem, 1)

            def dw(a):
                for b in range(4):
                    act.wait_ge(dw_ps.sem, dw_ps.at(a, b + 1))
                    copy(grad[:, b * 512:(b + 1) * 512], ps_s[b][:, :], 0.5 / (SK * SW) if b < 2 else 0.5)\
                        .then_inc(dw_ok.sem, 1)
                act.wait_ge(dw_ok.sem, dw_ok.at(a))
                act.activation(d2[:, :, :].rearrange("p j i -> p (j i)"), grad[:, 0:IC * D + DC * I],
                               ACT.Square, accum_out=nrm[:, 0:1]).then_inc(dw_sq.sem, 1)
                act.wait_ge(dln_ok.sem, dln_ok.at(a))
                act.activation(junk, grad[:, IC * D + DC * I:MEMW], ACT.Square, accum_out=nrm[:, 1:2])\
                   .then_inc(dw_sq.sem, 1)

            def w1_natural(a):
                for c in range(DC):
                    act.wait_ge(w1_ps.sem, w1_ps.at(a, c + 1))
                    copy(w1n[:, c, :], ps_s[c][:, :]).then_inc(w1_ok.sem, 1)

            def memory_high(occ):
                act.wait_ge(mem_ok.sem, mem_ok.at(occ))
                copy(w0_hi, mem_w0t, SW).then_inc(mem_hi.sem, 1)
                copy(w1_hi, mem_w1t, SW).then_inc(mem_hi.sem, 1)

            def experts(M, fill, prep=()):
                hidden(M, 0)
                for e in range(NU):
                    if e < NU - 1:
                        hidden(M, e + 1)
                    if e in prep:
                        split_weights(e + 2)
                    for step in fill.get(2 * e, ()):
                        step()
                    for step in fill.get(2 * e + 1, ()):
                        step()

            def scan_fill(a, M, more=True, after_update=True):
                fill = {
                    2: [lambda: ln_high(1, a), lambda: weights_t(M)],
                    4: [lambda: project_kv(a)],
                    5: [lambda: gates(a)],
                    6: [lambda: k_t(a)],
                    7: [lambda: z(a)],
                    9: [lambda: h_t(a)],
                    10: [lambda: y(a), lambda: y_norm(a)],
                    12: [lambda: w1_natural(a)],
                    13: [lambda: dyt_copy(a)],
                    15: [lambda: dw(a)],
                }
                if after_update:
                    fill[4].insert(0, lambda: memory_high(a))
                if more:
                    fill[8] = [lambda: ln_high(0, M + 1)]
                    fill[13] = [lambda: router_exp(M + 1), lambda: dyt_copy(a)]
                return fill

            def apply_steps(a):
                return [lambda: ln_high(1, a), lambda: project_q(a), lambda: k_t(a), lambda: z(a),
                        lambda: h_high(a), lambda: y(a), lambda: y_norm(a)]

            act.wait_ge(c_in.sem, c_in.at(0))
            copy(ident_h[:, :], ident).then_inc(id_h.sem, 1)
            copy(rw_hi[:, :], cst[:, C_RW:C_RW + DC * E], SW).then_inc(rw_h.sem, 1)
            ln_high(0, 0)
            split_weights(0)
            router_exp(0)
            split_weights(1)
            def biases_high():
                act.wait_ge(b2_ld.sem, b2_ld.at(0))
                copy(b2p[0:B_K, :], b2[0:B_K, :], SW).then_inc(b2_h.sem, 1)

            experts(0, {2: [lambda: weights_t(0), biases_high], 8: [lambda: ln_high(0, 1)],
                        10: [lambda: router_exp(1)]}, prep=range(NU - 1))
            memory_high(0)
            experts(1, scan_fill(0, 1, after_update=False))
            with act.Fori(2, NM - 1) as M:
                experts(M, scan_fill(M - 1, M))
            experts(NM - 1, scan_fill(NM - 2, NM - 1, more=False))
            tail = scan_fill(NM - 1, NM - 1, more=False)
            tail[2].pop()
            for place in sorted(tail):
                for step in tail[place]:
                    step()
            for step in apply_steps(NM)[0:3]:
                step()
            memory_high(NM)
            for step in apply_steps(NM)[3:]:
                step()
            ln_high(0, NM)
            router_exp(NM)
            with act.Fori(NM, 2 * NM - 1) as M:
                steps = apply_steps(M + 1)
                experts(M, {2: [steps[0], lambda: weights_t(M)], 4: steps[1:2], 6: steps[2:3],
                            8: steps[3:5], 10: steps[5:7],
                            14: [lambda: ln_high(0, M + 1)], 15: [lambda: router_exp(M + 1)]})
            M = 2 * NM - 1
            experts(M, {2: [lambda: weights_t(M)]})

        @block.vector
        def _(dve):
            def low(dst, src, hi, scale):
                return dve.scalar_tensor_tensor(dst, src, scale, hi, ALU.mult, ALU.subtract)

            def over_d(c):
                return c.unsqueeze(2).to_broadcast([128, NT, D])

            def over_tiles(row, n=D):
                return row.unsqueeze(1).to_broadcast([128, NT, n])

            def split_weights(k):
                dve.wait_ge(w_hi.sem, w_hi.at(k))
                if k < NU:
                    low(we_lo[:, k, :], stage[k % 2], we_hi[:, k, :], SW).then_inc(w_lo.sem, 1)
                else:
                    low(wa_lo[:, :], stage[k % 2][:, 0:3 * DC * D], wa_hi[:, :], SW).then_inc(w_lo.sem, 1)

            def hidden(M, e):
                u = NU * M + e
                for c in range(IC):
                    dve.wait_ge(hid_hi.sem, hid_hi.at(u, c + 1))
                    low(hl[:, e % 2, c, :], gel[:, c, :], hh[:, e % 2, c, :], SH).then_inc(hid_lo.sem, 1)

            def accumulate(M, e):
                u = NU * M + e
                if e == 0:
                    dve.wait_ge(lg_v.sem, lg_v.at(M))
                else:
                    dve.wait_ge(acc_ok.sem, acc_ok.at(u - 1))
                if e == 3:
                    dve.wait_ge(b_ok.sem, b_ok.at(M))
                for b in range(2):
                    dve.wait_ge(mm2_ps.sem, mm2_ps.at(u, b + 1))
                    for j in (2 * b, 2 * b + 1):
                        w = wacc[:, M % 2, j, e:e + 1] if e < E else 0.5 / (SH * SW)
                        x = xt[:, M % 2, j, :]
                        last = dve.scalar_tensor_tensor(x, ps_y[b][:, (j % 2) * D:(j % 2 + 1) * D], w, x,
                                                        ALU.mult, ALU.add)
                    last.then_inc(acc_ok.sem, 1)

            def layer_norm(n, occ, *waits):
                dst = xnf(occ) if n == 0 else xna
                for event, value in waits:
                    dve.wait_ge(event.sem, value)
                dve.memset(waited[2 * n], 0.0)
                for j in range(NT):
                    dve.bn_stats(stats[:, n, j, :], xt[:, occ % 2, j, :]).then_inc(ln_st[n].sem, 1)
                dve.wait_ge(ln_st[n].sem, ln_st[n].at(occ))
                dve.memset(waited[2 * n + 1], 0.0)
                for j in range(NT):
                    dve.bn_aggr(mv[:, n, j, :], stats[:, n, j, :]).then_inc(ln_mv[n].sem, 1)
                dve.wait_ge(ln_rs[n].sem, ln_rs[n].at(occ))
                for j in range(NT):
                    dve.tensor_scalar(dst[:, j, :], xt[:, occ % 2, j, :], mv[:, n, j, 0:1],
                                      rstd[n][:, j:j + 1], ALU.subtract, ALU.mult).then_inc(ln_xn[n].sem, 1)

            def ln_low(n, occ):
                f_lo, f_hi = fx_lo[:, occ % 2, :, :], fx_hi[:, occ % 2, :, :]
                dst, hi, banks = (f_lo, f_hi, ps_s[2:4]) if n == 0 else (ax_lo, ax_hi, ps_s[0:2])
                for c in range(DC):
                    dve.wait_ge(ln_hi[n].sem, ln_hi[n].at(occ, c + 1))
                    low(dst[:, c, :], banks[c][:, :], hi[:, c, :], SX).then_inc(ln_lo[n].sem, 1)

            def logits(M):
                dve.wait_ge(lg_ps.sem, lg_ps.at(M))
                dve.scalar_tensor_tensor(lg[:, 0, :, :], ps_s[2][:, 0:NT * E].rearrange("p (j e) -> p j e", j=NT),
                                         1.0 / (SX * SW), over_tiles(rb, E), ALU.mult, ALU.add)\
                   .then_inc(lg_v.sem, 1)

            def router(M):
                k = [1]

                def step(ins):
                    k[0] += 1
                    ins.then_inc(lg_v.sem, 1)
                    dve.wait_ge(lg_v.sem, lg_v.at(M, k[0]))

                def over_e(c):
                    return c.unsqueeze(2).to_broadcast([128, NT, E])

                top, rnk, tot, inv = lg[:, 3, :, 0], lg[:, 3, :, 1], lg[:, 3, :, 2], lg[:, 3, :, 3]
                prob, rest, eq, order, s1, s2 = (lg[:, n, :, :] for n in range(4, 10))
                dve.wait_ge(lg_v.sem, lg_v.at(M, 1))
                step(dve.tensor_reduce(top, lg[:, 0, :, :], AX.X, ALU.max))
                step(dve.tensor_tensor(lg[:, 1, :, :], lg[:, 0, :, :], over_e(top), ALU.subtract))
                dve.wait_ge(ex_ok.sem, ex_ok.at(M))
                step(dve.tensor_reduce(tot, lg[:, 2, :, :], AX.X, ALU.add))
                step(dve.reciprocal(inv, tot))
                step(dve.tensor_tensor(prob, lg[:, 2, :, :], over_e(inv), ALU.mult))

                def first_of_largest(values, chosen):
                    step(dve.tensor_reduce(top, values, AX.X, ALU.max))
                    step(dve.tensor_tensor(eq, values, over_e(top), ALU.is_equal))
                    step(dve.tensor_tensor(order, eq, over_tiles(rev, E), ALU.mult))
                    step(dve.tensor_reduce(rnk, order, AX.X, ALU.max))
                    step(dve.tensor_tensor(chosen, order, over_e(rnk), ALU.is_equal))

                first_of_largest(prob, s1)
                step(dve.scalar_tensor_tensor(rest, s1, -4.0, prob, ALU.mult, ALU.add))
                first_of_largest(rest, s2)
                step(dve.tensor_tensor(s1, s1, s2, ALU.add))
                step(dve.scalar_tensor_tensor(rest, prob, SX, s1, ALU.mult, ALU.mult))
                step(dve.tensor_scalar(wgt[:, :, 0:E], rest, 1.0, None, ALU.mult))
                dve.tensor_scalar(wgt[:, :, B_LOW:B_LOW + E], rest, 1.0, None, ALU.mult)
                dve.tensor_tensor(wgt[:, :, NU:NU + E], rest, wgt[:, :, 0:E], ALU.subtract)
                dve.scalar_tensor_tensor(wacc[:, M % 2, :, :], prob, 0.5 / (SH * SW), s1, ALU.mult, ALU.mult)\
                   .then_inc(lg_v.sem, 1)

            def biases(M):
                dve.wait_ge(acc_ok.sem, acc_ok.at(NU * M + 2))
                for b in range(2):
                    dve.wait_ge(b_ps.sem, b_ps.at(M, b + 1))
                    x = xt[:, M % 2, 2 * b:2 * b + 2, :].rearrange("p j d -> p (j d)")
                    dve.scalar_tensor_tensor(x, ps_s[b][:, :], 0.5 / (SX * SW), x, ALU.mult, ALU.add)\
                       .then_inc(b_ok.sem, 1)

            def gate_dots(a):
                k = [0]

                def step(ins):
                    k[0] += 1
                    ins.then_inc(g_v.sem, 1)
                    dve.wait_ge(g_v.sem, g_v.at(a, k[0]))

                dve.wait_ge(ln_xn[1].sem, ln_xn[1].at(a))
                products = [kv, hp[:, 0:2, :].rearrange("p a (b d) -> p (a b) d", b=2),
                            hp[:, 2:4, :].rearrange("p a (b d) -> p (a b) d", b=2)]
                for g in range(3):
                    dst = gate_in if g == 0 else gate_dot[:, g * NT:(g + 1) * NT]
                    for j in range(NT):
                        last = dve.tensor_tensor_reduce(out=products[g][:, j, :], in0=xna[:, j, :], in1=aw[:, g, :],
                                                        scale=1.0, scalar=0.0, op0=ALU.mult, op1=ALU.add,
                                                        accum_out=dst[:, j:j + 1])
                step(last)
                step(dve.tensor_reduce(gate_in[:, NT:NT + 1], gate_dot[:, NT:2 * NT], AX.X, ALU.add))
                step(dve.tensor_reduce(gate_in[:, NT + 1:NT + 2], gate_dot[:, 2 * NT:3 * NT], AX.X, ALU.add))

            def gates(a):
                dve.wait_ge(g_th.sem, g_th.at(a))
                dve.tensor_scalar(gate[:, :], gate_tanh[:, :], 0.5, 0.5, ALU.mult, ALU.add).then_inc(g_ok.sem, 1)
                dve.wait_ge(g_ok.sem, g_ok.at(a, 1))
                dve.tensor_scalar(gate[:, NT:NT + 1], gate_tanh[:, NT:NT + 1], -0.5, 0.5, ALU.mult, ALU.add)\
                   .then_inc(g_ok.sem, 1)

            def project(a, width, where, weight, with_v):
                src = tnh if with_v else tnh_q
                for j in range(NT):
                    dve.wait_ge(p_th.sem, p_th.at(a, j + 1) if with_v else p_th.at(a, 2 * (j // 2) + 2))
                    dve.scalar_tensor_tensor(sp[:, j, 0:width], src[:, j, 0:width], 1.0, where(j),
                                             ALU.add, ALU.mult).then_inc(p_s.sem, 1)
                dve.wait_ge(p_r.sem, p_r.at(a))
                dve.wait_ge(p_s.sem, p_s.at(a))
                for j in range(NT):
                    dve.scalar_tensor_tensor(kn[:, j, :], sp[:, j, 0:D], k_r[:, j:j + 1], weight,
                                             ALU.mult, ALU.mult).then_inc(k_ok.sem, 1)

            def project_kv(a):
                project(a, 2 * D, lambda j: ps_s[j][:, :], knb, True)
                dve.wait_ge(k_ok.sem, k_ok.at(a))
                dve.scalar_tensor_tensor(kv[:, :, :], sp[:, :, D:2 * D], -0.5 / (SX * SW), kn[:, :, :],
                                         ALU.mult, ALU.add).then_inc(kv_ok.sem, 1)

            def project_q(a):
                project(a, D, lambda j: ps_s[j // 2][:, (j % 2) * D:(j % 2 + 1) * D], qnb, False)

            def z(a):
                for j in range(NT):
                    dve.wait_ge(z_th.sem, z_th.at(a, j + 1))
                    dve.scalar_tensor_tensor(hp[:, j, :], tnh[:, j, :], 1.0, ps_s[j][:, :], ALU.add, ALU.mult)\
                       .then_inc(h_ok.sem, 1)

            def k_low(a):
                for c in range(DC):
                    dve.wait_ge(kt_h.sem, kt_h.at(a, c + 1))
                    low(kt_lo[:, c, :], ps_s[2 + c][:, :], kt_hi[:, c, :], SK).then_inc(kt_ok.sem, 1)

            def h_low(a, transposed=False):
                if transposed:
                    dve.wait_ge(h_ok.sem, h_ok.at(a))
                for c in range(IC):
                    dve.wait_ge(ht_h.sem, ht_h.at(a, c + 1))
                    low(ht_lo[:, c, :], hp[:, c, :] if transposed else ps_s[c][:, :], ht_hi[:, c, :], H_SCALE)\
                        .then_inc(ht_ok.sem, 1)

            def memory_low(occ):
                for n, (dst, src, hi) in enumerate(((w0_lo, mem_w0t, w0_hi), (w1_lo, mem_w1t, w1_hi))):
                    dve.wait_ge(mem_hi.sem, mem_hi.at(occ, n + 1))
                    low(dst, src, hi, SW).then_inc(mem_lo.sem, 1)

            def derivative(a):
                dve.wait_ge(h_ok.sem, h_ok.at(a))
                dve.scalar_tensor_tensor(d2[:, :, :], tnh[:, :, :], 1.0, hp[:, :, :], ALU.subtract, ALU.mult)\
                   .then_inc(d2_ok.sem, 1)
                dve.wait_ge(d2_ok.sem, d2_ok.at(a, 1))
                dve.scalar_tensor_tensor(d2[:, :, :], d2[:, :, :], -0.5 / (SK * SW), tnh[:, :, :], ALU.mult, ALU.add)\
                   .then_inc(d2_ok.sem, 1)

            def step_of(event, occ, first=0):
                k = [first]

                def step(ins):
                    k[0] += 1
                    ins.then_inc(event.sem, 1)
                    dve.wait_ge(event.sem, event.at(occ, k[0]))
                return step

            def backward(a):
                dve.wait_ge(y_n.sem, y_n.at(a))
                step = step_of(bw, a)
                step(dve.tensor_tensor(pr, yn[:, :, :], over_tiles(mem_ln), ALU.mult))
                step(dve.tensor_tensor(kv[:, :, :], pr, kv[:, :, :], ALU.add))
                dve.wait_ge(tr_ok.sem, tr_ok.at(a))
                for j in range(NT):
                    last = dve.scalar_tensor_tensor(pr[:, j, :], kv[:, j, :], theta_r[:, j:j + 1], mem_ln,
                                                    ALU.mult, ALU.mult)
                step(last)
                for j in range(NT):
                    last = dve.tensor_tensor_reduce(out=reg_b4[:, j, :], in0=pr[:, j, :], in1=yn[:, j, :], scale=1.0,
                                                    scalar=0.0, op0=ALU.mult, op1=ALU.add, accum_out=dot[:, j:j + 1])
                step(last)
                step(dve.tensor_scalar(dot_neg, dot, -1.0 / D, None, ALU.mult))
                for j in range(NT):
                    dve.scalar_tensor_tensor(pr[:, j, :], yn[:, j, :], dot_neg[:, j:j + 1], pr[:, j, :],
                                             ALU.mult, ALU.add).then_inc(dy_ok.sem, 1)

            def output_y(a):
                dve.wait_ge(y_n.sem, y_n.at(a))
                dve.tensor_tensor(pr, yn[:, :, :], over_tiles(mem_ln), ALU.mult).then_inc(pred_v.sem, 1)
                dve.wait_ge(pred_v.sem, pred_v.at(a - NM, 1))
                dve.tensor_tensor(pr, pr, kn[:, :, :], ALU.add).then_inc(pred_v.sem, 1)
                dve.wait_ge(pred_v.sem, pred_v.at(a - NM))
                x = xt[:, a % 2, :, :]
                dve.tensor_tensor(x, x, pr, ALU.add).then_inc(x_att.sem, 1)

            def dz_step(a):
                for j in range(NT):
                    dve.wait_ge(dh_ps.sem, dh_ps.at(a, j + 1))
                    dve.scalar_tensor_tensor(dz[:, j, :], d2[:, j, :], 1.0, ps_s[j][:, :], ALU.add, ALU.mult)\
                       .then_inc(dz_ok.sem, 1)

            def norm_sum(a):
                dve.wait_ge(dw_sq.sem, dw_sq.at(a))
                dve.scalar_tensor_tensor(nrm_sum, nrm[:, 1:2], 1.0 / 128, nrm[:, 0:1], ALU.mult, ALU.add)\
                   .then_inc(n_v.sem, 1)

            def update(a):
                dve.wait_ge(n_rt.sem, n_rt.at(a))
                total, inv, lim = nrm_c
                dve.tensor_scalar(total, nrm_root, GRAD, 1e-6, ALU.mult, ALU.add).then_inc(clip.sem, 1)
                dve.wait_ge(clip.sem, clip.at(a, 1))
                dve.reciprocal(inv, total).then_inc(clip.sem, 1)
                dve.wait_ge(clip.sem, clip.at(a, 2))
                dve.tensor_scalar(lim, inv, 1.0, -GRAD, ALU.min, ALU.mult).then_inc(clip.sem, 1)
                dve.wait_ge(clip.sem, clip.at(a, 3))
                dve.tensor_scalar(grad[:, :], grad[:, :], lim, None, ALU.mult).then_inc(clip.sem, 1)
                dve.wait_ge(clip.sem, clip.at(a))
                dve.scalar_tensor_tensor(sur[:, :], sur[:, :], gate[:, NT + 1:NT + 2], grad[:, :], ALU.mult, ALU.add)\
                   .then_inc(sur_ok.sem, 1)
                dve.wait_ge(sur_ok.sem, sur_ok.at(a))
                dve.scalar_tensor_tensor(mem[:, :], mem[:, :], gate[:, NT:NT + 1], sur[:, :], ALU.mult, ALU.add)\
                   .then_inc(mem_ok.sem, 1)

            def experts(M, fill, prep=()):
                hidden(M, 0)
                for e in range(NU):
                    if e < NU - 1:
                        hidden(M, e + 1)
                    if e in prep:
                        split_weights(e + 2)
                    for step in fill.get(2 * e, ()):
                        step()
                    accumulate(M, e)
                    for step in fill.get(2 * e + 1, ()):
                        step()

            def attn_ln(a):
                return lambda: layer_norm(1, a, (acc_ok, acc_ok.at(NU * a + E)), (b_ok, b_ok.at(a)))

            def scan_fill(a, M, more=True, after_update=True):
                fill = {
                    0: [attn_ln(a)],
                    2: [lambda: ln_low(1, a), lambda: gate_dots(a)],
                    4: [lambda: project_kv(a)],
                    5: [lambda: biases(M)],
                    6: [lambda: gates(a), lambda: k_low(a)],
                    7: [lambda: z(a)],
                    8: [lambda: derivative(a)],
                    9: [lambda: h_low(a)],
                    11: [lambda: backward(a)],
                    14: [lambda: dz_step(a)],
                    17: [lambda: norm_sum(a)],
                }
                if after_update:
                    fill[3] = [lambda: update(a - 1)]
                    fill[5].append(lambda: memory_low(a))
                if more:
                    fill[6].append(lambda: layer_norm(0, M + 1, (x_ld, x_ld.at(M + 1))))
                    fill[8] = [lambda: ln_low(0, M + 1), lambda: derivative(a)]
                    fill[12] = [lambda: logits(M + 1)]
                    fill[13] = [lambda: router(M + 1)]
                return fill

            def apply_steps(a):
                return [lambda: layer_norm(1, a, (x_ld, x_ld.at(a))), lambda: ln_low(1, a), lambda: project_q(a),
                        lambda: k_low(a), lambda: z(a), lambda: h_low(a, transposed=True), lambda: output_y(a)]

            dve.wait_ge(c_in.sem, c_in.at(0))
            dve.memset(wgt[:, :, :], 0.0).then_inc(ones_col.sem, 1)
            dve.wait_ge(ones_col.sem, ones_col.at(0, 1))
            for k in (E, B_LOW + E):
                dve.memset(wgt[:, :, k:k + 1], SX).then_inc(ones_col.sem, 1)
            dve.wait_ge(ones_col.sem, ones_col.at(0))
            dve.wait_ge(rw_h.sem, rw_h.at(0))
            low(rw_lo[:, :], cst[:, C_RW:C_RW + DC * E], rw_hi[:, :], SW).then_inc(rw_l.sem, 1)
            layer_norm(0, 0, (x_ld, x_ld.at(0)))
            ln_low(0, 0)
            split_weights(0)
            logits(0)
            router(0)
            split_weights(1)
            def biases_low():
                dve.wait_ge(b2_h.sem, b2_h.at(0))
                low(b2p[B_LOW:B_K, :], b2[B_LOW:B_K, :], b2p[B_LOW:B_K, :], SW).then_inc(b2_l.sem, 1)

            experts(0, {3: [biases_low], 5: [lambda: biases(0)], 6: [lambda: layer_norm(0, 1, (x_ld, x_ld.at(1)))],
                        8: [lambda: ln_low(0, 1)], 10: [lambda: logits(1), lambda: router(1)]}, prep=range(NU - 1))
            dve.wait_ge(mem_ld.sem, mem_ld.at(0))
            dve.wait_ge(b2_l.sem, b2_l.at(0))
            dve.memset(sur[:, :], 0.0).then_inc(mem_ok.sem, 1)
            memory_low(0)
            dve.wait_ge(c_rest.sem, c_rest.at(0))
            dve.tensor_scalar(cst[:, C_KN:C_KN + 2 * D], cst[:, C_KN:C_KN + 2 * D], 0.5 / (SX * SW), None,
                              ALU.mult).then_inc(nscale.sem, 1)
            dve.wait_ge(nscale.sem, nscale.at(0))
            experts(1, scan_fill(0, 1, after_update=False))
            with dve.Fori(2, NM - 1) as M:
                experts(M, scan_fill(M - 1, M))
            experts(NM - 1, scan_fill(NM - 2, NM - 1, more=False))
            tail = scan_fill(NM - 1, NM - 1, more=False)
            tail[5].pop(0)
            steps = apply_steps(NM)
            tail[14].append(steps[0])
            tail[17] += [steps[1], lambda: update(NM - 1)] + steps[2:4] + [lambda: memory_low(NM)] + steps[4:]
            for place in sorted(tail):
                for step in tail[place]:
                    step()
            layer_norm(0, NM, (x_att, x_att.at(0)))
            ln_low(0, NM)
            logits(NM)
            router(NM)
            with dve.Fori(NM, 2 * NM - 1) as M:
                steps = apply_steps(M + 1)
                experts(M, {0: steps[0:1], 2: steps[1:2], 4: steps[2:3], 5: [lambda: biases(M)], 6: steps[3:4],
                            8: steps[4:6],
                            11: [steps[6], lambda: layer_norm(0, M + 1, (x_att, x_att.at(M + 1 - NM)))],
                            14: [lambda: ln_low(0, M + 1)], 15: [lambda: logits(M + 1), lambda: router(M + 1)]})
            M = 2 * NM - 1
            experts(M, {5: [lambda: biases(M)]})


def kernel(**inputs):
    import numpy as np
    import concourse.bacc as bacc
    from concourse import mybir as mb
    from concourse.bass_utils import run_bass_kernel_spmd

    def get(name):
        return np.asarray(inputs["L0_" + name])

    def by_rows(w):
        return w.reshape(-1, 128, w.shape[1]).transpose(1, 0, 2).reshape(128, -1)

    def on_all(row):
        return np.broadcast_to(row.reshape(1, -1), (128, row.size))

    x = get("attn_x").reshape(NT, 2, NM, CH, D).transpose(1, 3, 2, 0, 4).reshape(128, NM, NT * D)
    first = [get("ffn_rw1")[e] for e in range(E)] + [get("ffn_sw1")]
    second = [get("ffn_rw2")[e] for e in range(E)] + [get("ffn_sw2")]
    w_experts = np.stack([np.concatenate([by_rows(a), by_rows(b)], 1) for a, b in zip(first, second)], 1)
    wk, wv, wq = (get(f"attn_w{n}_w").T for n in "kvq")
    w_attn = np.concatenate([by_rows(np.concatenate([wk, wv], 1)), by_rows(wq)], 1)
    w0, w1 = get("attn_mem_w0"), get("attn_mem_w1")
    mem = np.concatenate([by_rows(w1.T), by_rows(w0.T), on_all(get("attn_mem_ln_w"))], 1)
    f32 = x.dtype
    p = np.arange(128)
    b1 = np.concatenate([get("ffn_rb1"), get("ffn_sb1")[None]]).reshape(NU * IC, 128).T
    b2 = np.zeros((128, D), f32)
    for row in (0, NU, B_LOW):
        b2[row:row + E], b2[row + E] = get("ffn_rb2"), get("ffn_sb2")
    gate_w = [np.concatenate([get(f"attn_{n}_w").reshape(CH, D)] * 2) for n in ("theta", "alpha", "eta")]
    consts = np.concatenate([
        np.eye(128, dtype=f32), b1, on_all(get("ffn_router_b")), on_all(np.arange(E, 0, -1).astype(f32)),
        by_rows(get("ffn_router_w")), (p[:, None] // CH == p[None] // CH).astype(f32), np.ones((128, 128), f32),
        *gate_w, on_all(get("attn_k_norm_w")), on_all(get("attn_q_norm_w")), b2], 1)
    arrays = {"x_in": x, "w_experts": w_experts, "w_attn": w_attn, "mem_in": mem,
              "consts_in": consts}
    arrays = {n: np.ascontiguousarray(a) for n, a in arrays.items()}

    nc = bacc.Bacc("TRN2", target_bir_lowering=False, num_devices=1)
    args = {n: nc.dram_tensor(n, a.shape, mb.dt.from_np(a.dtype), kind="ExternalInput").ap()
            for n, a in arrays.items()}
    args["out"] = nc.dram_tensor("out", (128, NM, NT * D), mb.dt.float32, kind="ExternalOutput").ap()
    macaron_kernel(nc, **args)
    got = run_bass_kernel_spmd(nc, [arrays], core_ids=[0]).results[0]["out"]
    return got.reshape(2, CH, NM, NT, D).transpose(3, 0, 2, 1, 4).reshape(B, S, D)
```

```python
import concourse.bass as bass
from concourse import mybir
from collections import namedtuple
from contextlib import ExitStack

B, S, D = 8, 512, 256
CH = 64
NM = S // CH
NT = B * CH // 128
TOK = NT * 128
I = 512
E = 8
NU = E + 1
DC, IC = D // 128, I // 128
B_LOW = 32
B_K = B_LOW + NU
WE = DC * I + IC * D
MEMW = IC * D + DC * I + D

SX = 64.0
SW = 64.0
SH = 16.0
SK = 16.0
SG = 0.25
LN_EPS, RMS_EPS = 1e-5, 1e-6
H_SCALE = 0.5 * SH / (SK * SW)
GRAD = 2.0 * 0.01 / (B * CH * D)

C_ID = 0
C_B1 = C_ID + 128
C_RB = C_B1 + NU * IC
C_REV = C_RB + E
C_RW = C_REV + E
C_BLK = C_RW + DC * E
C_ONE = C_BLK + 128
C_AW = C_ONE + 128
C_KN = C_AW + 3 * D
C_QN = C_KN + D
C_B2 = C_QN + D
NC_COLS = C_B2 + D


class Event:

    def __init__(self, sem, per):
        self.sem, self.per = sem, per

    def at(self, occurrence, k=None):
        return occurrence * self.per + (self.per if k is None else k)


def macaron_kernel(nc, x_in, w_experts, w_attn, mem_in, consts_in, out):
    F, H = mybir.dt.float32, mybir.dt.float16
    ALU, ACT, AX = mybir.AluOpType, mybir.ActivationFunctionType, mybir.AxisListType
    x1_dram = nc.dram_tensor("x1_scratch", (128, NM, NT * D), F, kind="Internal").ap()

    ctx = ExitStack()
    with ctx:
        def sb(name, shape, dt=F):
            return ctx.enter_context(nc.sbuf_tensor(name, shape, dt))

        def ev(name, per=1):
            return Event(ctx.enter_context(nc.semaphore(name)), per)

        we_hi = sb("we_hi", [128, NU, WE], H)
        we_lo = sb("we_lo", [128, NU, WE], H)
        wa_hi = sb("wa_hi", [128, 3 * DC * D], H)
        wa_lo = sb("wa_lo", [128, 3 * DC * D], H)
        rw_hi = sb("rw_hi", [128, DC * E], H)
        rw_lo = sb("rw_lo", [128, DC * E], H)
        cst = sb("cst", [128, C_B2])
        xt = sb("xt", [128, 2, NT, D])
        fx_hi = sb("fx_hi", [128, 2, DC, TOK], H)
        fx_lo = sb("fx_lo", [128, 2, DC, TOK], H)
        gel = sb("gel", [128, IC, TOK])
        hh = sb("hh", [128, 2, IC, TOK], H)
        hl = sb("hl", [128, 2, IC, TOK], H)
        mem = sb("mem", [128, MEMW])
        sur = sb("sur", [128, MEMW])
        w1n = sb("w1n", [128, DC, I])
        reg_a = sb("reg_a", [128, MEMW])
        reg_b = sb("reg_b", [128, WE])
        reg_c = sb("reg_c", [128, NT, D])
        reg_d = sb("reg_d", [128, NT, D])
        reg_e = sb("reg_e", [128, NT * D])
        reg_f = sb("reg_f", [128, DC, TOK])
        kn = sb("kn", [128, NT, D])
        kv = sb("kv", [128, NT, D])
        hp = sb("hp", [128, NT, I])
        d2 = sb("d2", [128, NT, I])
        stats = sb("stats", [128, 2, NT, 6])
        mv = sb("mv", [128, 2, NT, 2])
        sm = sb("sm", [128, 128])
        lg = sb("lg", [128, 10, NT, E])
        wgt = sb("wgt", [128, NT, B_K], H)
        b2p = sb("b2p", [128, D], H)
        ident_h = sb("ident_h", [128, 128], H)
        wacc = sb("wacc", [128, 2, NT, E])
        wgt_t = d2[:, 0, :].bitcast(H)[0:B_K, 0:TOK].rearrange("u (j t) -> u j t", j=NT)

        ident = cst[:, C_ID:C_ID + 128]
        blk = cst[:, C_BLK:C_BLK + 128]
        ones = cst[:, C_ONE:C_ONE + 128]
        aw = cst[:, C_AW:C_AW + 3 * D].rearrange("p (g d) -> p g d", g=3)
        knb, qnb = cst[:, C_KN:C_KN + D], cst[:, C_QN:C_QN + D]
        rb = cst[:, C_RB:C_RB + E]
        rev = cst[:, C_REV:C_REV + E]
        b2 = sur[:, 0:D]

        def parts(region, chunks, width):
            both = region.bitcast(H)
            n = chunks * width
            return tuple(both[:, k * n:(k + 1) * n].rearrange("p (c w) -> p c w", c=chunks) for k in range(2))

        stage = [reg_a[:, 0:WE], reg_b[:, :]]
        tnh = reg_a[:, 0:NT * I].rearrange("p (j i) -> p j i", j=NT)
        ht_hi, ht_lo = parts(reg_a[:, 0:IC * TOK], IC, TOK)
        grad = reg_a
        sp = reg_b[:, :].rearrange("p (j i) -> p j i", j=NT)
        dz = sp
        xna, yn = reg_c, reg_c
        gy = reg_d
        reg_b4 = reg_b[:, 0:NT * D].rearrange("p (j d) -> p j d", j=NT)

        def xnf(M):
            return reg_d if isinstance(M, int) and M < 2 else reg_b4

        ax_hi, ax_lo = parts(reg_e[:, :], DC, TOK)
        pr = reg_e[:, :].rearrange("p (j d) -> p j d", j=NT)
        kt_hi, kt_lo = parts(reg_f[:, :, :].rearrange("p c t -> p (c t)"), DC, TOK)
        dyt_hi, dyt_lo = kt_hi, kt_lo
        w1n_hi, w1n_lo = parts(w1n[:, :, :].rearrange("p c i -> p (c i)"), DC, I)
        w0_hi, w0_lo = parts(d2[:, 2:4, :].rearrange("p a i -> p (a i)"), DC, I)
        w1_hi, w1_lo = parts(reg_d[:, :, :].rearrange("p j d -> p (j d)"), IC, D)
        tnh_q = hp
        junk = reg_f[:, 0, 0:D]
        mem_w1t = mem[:, 0:IC * D].rearrange("p (c d) -> p c d", c=IC)
        mem_w0t = mem[:, IC * D:IC * D + DC * I].rearrange("p (c i) -> p c i", c=DC)
        mem_ln = mem[:, IC * D + DC * I:MEMW]

        at_sm = [0]

        def col(n):
            at_sm[0] += n
            return sm[:, at_sm[0] - n:at_sm[0]]

        var_eps, rstd = [col(NT), col(NT)], [col(NT), col(NT)]
        neg_half, pos_half, ln_eps, rms_eps, unscale = col(NT), col(1), col(NT), col(NT), col(NT)
        gate_dot = col(3 * NT)
        gate_in, gate_tanh, gate = col(NT + 2), col(NT + 2), col(NT + 2)
        k_ms, k_ms_eps, k_r = col(NT), col(NT), col(NT)
        y_ms, y_ms_eps, y_r, y_rs, theta_r = (col(NT) for _ in range(5))
        dot, dot_neg = col(NT), col(NT)
        nrm, nrm_sum, nrm_all, nrm_root = col(5), col(1), col(1), col(1)
        nrm_c = [col(1) for _ in range(3)]
        waited = [col(1) for _ in range(5)]

        def bank(name):
            return ctx.enter_context(nc.psum_tensor(name, [128, 512], F))

        ps_h = [bank(f"ps_h{i}") for i in range(2)]
        ps_y = [bank(f"ps_y{i}") for i in range(2)]
        ps_s = [bank(f"ps_s{i}") for i in range(4)]

        Place = namedtuple("Place", "hi lo t_banks q_banks tanh silu q qt_banks")
        usual_place = Place(ax_hi, ax_lo, ps_s[0:2], ps_s[0:2], tnh_q[:, :, 0:D], sp[:, :, 0:D], kn[:, :, :],
                            ps_s[2:4])
        first_place = Place(hh[:, 0, 0:DC, :], hl[:, 0, 0:DC, :], ps_y, ps_y, gel[:, :, D:2 * D], gel[:, :, 0:D],
                            kv[:, :, :], ps_h)

        def place(a):
            return first_place if isinstance(a, int) and a == NM else usual_place

        def tanh_of(a):
            return gel[:, :, :] if isinstance(a, int) and a == NM - 1 else tnh

        def w1_banks(a):
            return ps_y if isinstance(a, int) and a == NM - 1 else ps_s[0:2]

        c_in, c_rest = ev("constants_loaded", 16), ev("more_constants_loaded", 16)
        mem_ld = ev("memory_loaded", 16)
        stage_ld = [ev(f"stage{i}_loaded", 16) for i in range(2)]
        x_ld = ev("x_loaded", 16)
        x_st = ev("x_stored", 16)
        pool_c = ev("pool_constants", 5)
        w_hi, w_lo = ev("weights_hi"), ev("weights_lo")
        rw_h, rw_l = ev("router_weights_hi"), ev("router_weights_lo")
        nscale = ev("norm_weights_scaled")
        ones_col = ev("shared_weight_set", 3)
        id_h = ev("identity_in_fp16")
        b2_ld = ev("biases_loaded", 16)
        b2_h, b2_l = ev("biases_hi"), ev("biases_lo")
        mm1_ps = ev("hidden_in_psum", IC)
        gelu_ok, hid_hi, hid_lo = ev("gelu_done", IC), ev("hidden_hi", IC), ev("hidden_lo", IC)
        mm2_ps = ev("expert_out_in_psum", 2)
        acc_ok = ev("expert_out_added", 2)
        nm = ["ffn", "attn"]
        ln_st = [ev(f"{n}_ln_stats", NT) for n in nm]
        ln_mv = [ev(f"{n}_ln_mean_var", NT) for n in nm]
        ln_ve = [ev(f"{n}_ln_var_eps") for n in nm]
        ln_rs = [ev(f"{n}_ln_rstd") for n in nm]
        ln_xn = [ev(f"{n}_ln_out", NT) for n in nm]
        ln_tp = [ev(f"{n}_lnT_in_psum", DC) for n in nm]
        ln_hi = [ev(f"{n}_lnT_hi", DC) for n in nm]
        ln_lo = [ev(f"{n}_lnT_lo", DC) for n in nm]
        lg_ps, lg_v = ev("logits_in_psum"), ev("router_steps", 21)
        ex_ok = ev("router_exp")
        wt_ps, wt_ok = ev("weightsT_in_psum"), ev("weightsT_copied")
        b_ps, b_ok = ev("bias_in_psum", 2), ev("bias_added", 2)
        g_v, g_ps, g_th, g_ok = ev("gate_dots", 3), ev("gates_in_psum"), ev("gate_tanh", 2), ev("gates", 2)
        p_ps, p_th, p_s = ev("proj_in_psum", NT), ev("proj_tanh", NT), ev("proj_silu", NT)
        p_sq, p_ve, p_r = ev("k_mean_square", NT), ev("k_ms_eps"), ev("k_rms_inv")
        k_ok, kv_ok = ev("k_done", NT), ev("k_minus_v")
        kt_ps, kt_h, kt_ok = ev("kT_in_psum", DC), ev("kT_hi", DC), ev("kT_lo", DC)
        z_ps, z_th, h_ok = ev("z_in_psum", NT), ev("z_tanh", NT), ev("hidden_mem", NT)
        d2_ok = ev("silu_derivative", 2)
        ht_ps, ht_h, ht_ok = ev("hT_in_psum", IC), ev("hT_hi", IC), ev("hT_lo", IC)
        y_ps, y_sq, y_ve, y_ri = ev("y_in_psum", 2), ev("y_mean_square", NT), ev("y_ms_eps"), ev("y_rms_inv", 2)
        y_n = ev("y_normalised", NT)
        pred_v = ev("memory_out", NT)
        q_add = ev("queries_added")
        x_att = ev("attention_added")
        tr_ok, bw, dy_ok = ev("theta_over_rms"), ev("backward_steps", 5), ev("dy_done", NT)
        gy_ok = ev("ln_grad_steps", 4)
        dln_ps, dln_ok = ev("dln_in_psum"), ev("dln_copied")
        dyt_ps, dyt_h, dyt_ok = ev("dyT_in_psum", DC), ev("dyT_hi", DC), ev("dyT_lo", DC)
        dh_ps, dz_ok = ev("dh_in_psum", NT), ev("dz_done", NT)
        dw_ps, dw_ok, dw_sq = ev("dW_in_psum", 4), ev("dW_copied", 4), ev("grad_squares", 5)
        n_v, n_sum, n_rt = ev("norm_partial"), ev("norm_summed"), ev("norm_root")
        clip = ev("clip_steps", 4)
        sur_ok = ev("surprise_updated")
        fin, fin_w = ev("final_decay", 2), ev("final_memory", 2)
        mem_hi, mem_lo = ev("memory_hi", 2), ev("memory_lo", 2)
        mem_ok = ev("memory_in_place")
        w1_ps, w1_h, w1_ok = ev("w1_in_psum", DC), ev("w1_hi_copied", DC), ev("w1_lo_copied", DC)

        block = ctx.enter_context(nc.Block())

        @block.sync
        def _(sp_eng):
            eng = sp_eng

            def load_x(M, src):
                eng.dma_start(xt[:, M % 2, :, :].rearrange("p j d -> p (j d)"), src)\
                   .then_inc(x_ld.sem, 16)

            eng.dma_start(xt[:, 0, :, :].rearrange("p j d -> p (j d)"), x_in[:, 0, :]).then_inc(x_ld.sem, 16)
            for k in range(2):
                eng.dma_start(stage[k], w_experts[:, k, :]).then_inc(stage_ld[k].sem, 16)
            eng.dma_start(cst[:, C_BLK:C_B2], consts_in[:, C_BLK:C_B2]).then_inc(c_rest.sem, 16)
            eng.dma_start(b2, consts_in[:, C_B2:NC_COLS]).then_inc(b2_ld.sem, 16)
            eng.dma_start(mem[:, :], mem_in).then_inc(mem_ld.sem, 16)
            eng.wait_ge(x_ld.sem, x_ld.at(0))
            load_x(1, x_in[:, 1, :])
            for k in range(2, NU + 1):
                eng.wait_ge(w_lo.sem, w_lo.at(k - 2))
                if k < NU:
                    eng.dma_start(stage[k % 2], w_experts[:, k, :]).then_inc(stage_ld[k % 2].sem, 16)
                else:
                    eng.dma_start(stage[k % 2][:, 0:3 * DC * D], w_attn).then_inc(stage_ld[k % 2].sem, 16)

            def store(M, dst):
                eng.wait_ge(acc_ok.sem, acc_ok.at(NU * M + E))
                eng.wait_ge(b_ok.sem, b_ok.at(M))
                eng.dma_start(dst, xt[:, M % 2, :, :].rearrange("p j d -> p (j d)"))\
                   .then_inc(x_st.sem, 16)

            def turn_over(M, dst, src):
                store(M - 1, dst)
                eng.wait_ge(x_st.sem, x_st.at(M - 1))
                load_x(M + 1, src)

            with eng.Fori(1, NM - 1) as M:
                eng.wait_ge(ln_xn[1].sem, ln_xn[1].at(M - 1))
                turn_over(M, x1_dram[:, M - 1, :], x_in[:, M + 1, :])
            for M in (NM - 1, NM):
                eng.wait_ge(ln_xn[1].sem, ln_xn[1].at(M - 1))
                turn_over(M, x1_dram[:, M - 1, :], x1_dram[:, M + 1 - NM, :])
            with eng.Fori(NM + 1, 2 * NM - 1) as M:
                turn_over(M, out[:, M - 1 - NM, :], x1_dram[:, M + 1 - NM, :])
            store(2 * NM - 2, out[:, NM - 2, :])
            store(2 * NM - 1, out[:, NM - 1, :])
            eng.wait_ge(x_st.sem, x_st.at(2 * NM - 1))

        @block.gpsimd
        def _(pool):
            pool.memset(neg_half, -0.5).then_inc(pool_c.sem, 1)
            pool.memset(pos_half, 0.5).then_inc(pool_c.sem, 1)
            pool.memset(ln_eps, LN_EPS).then_inc(pool_c.sem, 1)
            pool.memset(rms_eps, RMS_EPS).then_inc(pool_c.sem, 1)
            pool.memset(unscale, 1.0 / (SH * SW)).then_inc(pool_c.sem, 1)
            pool.wait_ge(pool_c.sem, pool_c.at(0))

            def ln_rstd(n, occ):
                pool.wait_ge(ln_mv[n].sem, ln_mv[n].at(occ))
                pool.tensor_tensor(var_eps[n], mv[:, n, :, 1], ln_eps, ALU.add)\
                    .then_inc(ln_ve[n].sem, 1)
                pool.wait_ge(ln_ve[n].sem, ln_ve[n].at(occ))
                pool.tensor_tensor(rstd[n], var_eps[n], neg_half, ALU.pow).then_inc(ln_rs[n].sem, 1)

            def rms_inv(ms, ms_eps, r, have, mid, done, occ):
                pool.wait_ge(have.sem, have.at(occ))
                pool.tensor_tensor(ms_eps, ms, rms_eps, ALU.add).then_inc(mid.sem, 1)
                pool.wait_ge(mid.sem, mid.at(occ))
                pool.tensor_tensor(r, ms_eps, neg_half, ALU.pow).then_inc(done.sem, 1)

            def k_rms(a):
                rms_inv(k_ms, k_ms_eps, k_r, p_sq, p_ve, p_r, a)

            def y_rms(a):
                rms_inv(y_ms, y_ms_eps, y_r, y_sq, y_ve, y_ri, a)
                pool.wait_ge(y_ri.sem, y_ri.at(a, 1))
                pool.tensor_tensor(y_rs, y_r, unscale, ALU.mult).then_inc(y_ri.sem, 1)

            def ln_grad(a):
                pool.wait_ge(bw.sem, bw.at(a, 2))
                theta = gate[:, 0:NT].unsqueeze(2).to_broadcast([128, NT, D])
                for n, (dst, x, y, op) in enumerate(((gy[:, :, :], kv[:, :, :], theta, ALU.mult),
                                                     (gy[:, :, :], gy[:, :, :], yn[:, :, :], ALU.mult),
                                                     (gy[:, 0:2, :], gy[:, 0:2, :], gy[:, 2:4, :], ALU.add),
                                                     (gy[:, 0, :], gy[:, 0, :], gy[:, 1, :], ALU.add))):
                    if n > 0:
                        pool.wait_ge(gy_ok.sem, gy_ok.at(a, n))
                    pool.tensor_tensor(dst, x, y, op).then_inc(gy_ok.sem, 1)

            def scan(a, next_tile=None, after_y=None):
                ln_rstd(1, a)
                k_rms(a)
                if next_tile is not None:
                    ln_rstd(0, next_tile)
                y_rms(a)
                pool.wait_ge(g_ok.sem, g_ok.at(a))
                pool.tensor_tensor(theta_r, y_r, gate[:, 0:NT], ALU.mult).then_inc(tr_ok.sem, 1)
                ln_grad(a)
                if after_y is not None:
                    after_y()
                pool.wait_ge(n_v.sem, n_v.at(a))
                pool.tensor_tensor(waited[4], rms_eps[:, 0:1], rms_eps[:, 0:1], ALU.add)
                pool.partition_all_reduce(nrm_all, nrm_sum, 128, bass.bass_isa.ReduceOp.add).then_inc(n_sum.sem, 1)
                pool.wait_ge(n_sum.sem, n_sum.at(a))
                pool.tensor_tensor(nrm_root, nrm_all, pos_half, ALU.pow).then_inc(n_rt.sem, 1)

            def apply(a):
                ln_rstd(1, a)
                k_rms(a)
                y_rms(a)

            ln_rstd(0, 0)
            ln_rstd(0, 1)
            scan(0, 2)
            with pool.Fori(2, NM - 1) as M:
                scan(M - 1, M + 1)
            scan(NM - 2)
            scan(NM - 1, after_y=lambda: (ln_rstd(1, NM), k_rms(NM)))
            y_rms(NM)
            ln_rstd(0, NM)
            with pool.Fori(NM, 2 * NM - 1) as M:
                apply(M + 1)
                ln_rstd(0, M + 1)

        @block.tensor
        def _(pe):
            def products(out_ap, pairs):
                for n, (lhs, rhs) in enumerate(pairs):
                    last = pe.matmul(out_ap, lhs, rhs, start=(n == 0), stop=(n == len(pairs) - 1))
                return last

            def guard(*waits):
                for event, value in waits:
                    pe.wait_ge(event.sem, value)

            def mm1(M, e):
                u = NU * M + e
                for c in range(IC):
                    if not (isinstance(M, int) and M == 0 and e == 0 and c < 2):
                        pe.wait_ge(gelu_ok.sem, gelu_ok.at(u, c - 1))
                    pairs = []
                    for dc in range(DC):
                        w = slice(dc * I + c * 128, dc * I + (c + 1) * 128)
                        pairs += [(we_hi[:, e, w], fx_hi[:, M % 2, dc, :]), (we_hi[:, e, w], fx_lo[:, M % 2, dc, :]),
                                  (we_lo[:, e, w], fx_hi[:, M % 2, dc, :])]
                    products(ps_h[c % 2][:, :], pairs).then_inc(mm1_ps.sem, 1)

            def mm2(M, e):
                u = NU * M + e
                pe.wait_ge(hid_lo.sem, hid_lo.at(u))
                for b in range(2):
                    if not (isinstance(M, int) and M == 0 and e == 0):
                        pe.wait_ge(acc_ok.sem, acc_ok.at(u - 1, b + 1))
                    for j in (2 * b, 2 * b + 1):
                        pairs = []
                        for c in range(IC):
                            w = slice(DC * I + c * D, DC * I + (c + 1) * D)
                            t = slice(j * 128, (j + 1) * 128)
                            pairs += [(hh[:, e % 2, c, t], we_hi[:, e, w]), (hh[:, e % 2, c, t], we_lo[:, e, w]),
                                      (hl[:, e % 2, c, t], we_hi[:, e, w])]
                        last = products(ps_y[b][:, (j % 2) * D:(j % 2 + 1) * D], pairs)
                    last.then_inc(mm2_ps.sem, 1)

            def transposes(src, banks, done, occ_wait, *guards):
                guard(occ_wait, *guards)
                for c, ps in enumerate(banks):
                    for j in range(NT):
                        last = pe.transpose(ps[:, j * 128:(j + 1) * 128], src[:, j, c * 128:(c + 1) * 128], ident)
                    last.then_inc(done.sem, 1)

            def ln_t(n, occ, *guards):
                src, banks = (xnf(occ), ps_s[2:4]) if n == 0 else (xna, place(occ).t_banks)
                transposes(src, banks, ln_tp[n], (ln_xn[n], ln_xn[n].at(occ)), *guards)

            def router(M, *guards):
                guard((ln_lo[0], ln_lo[0].at(M)), *guards)
                for j in range(NT):
                    t = slice(j * 128, (j + 1) * 128)
                    pairs = []
                    for c in range(DC):
                        w = slice(c * E, (c + 1) * E)
                        x_hi, x_lo = fx_hi[:, M % 2, c, t], fx_lo[:, M % 2, c, t]
                        pairs += [(x_hi, rw_hi[:, w]), (x_hi, rw_lo[:, w]), (x_lo, rw_hi[:, w])]
                    last = products(ps_s[2][:, j * E:(j + 1) * E], pairs)
                last.then_inc(lg_ps.sem, 1)

            def weights_t(M):
                guard((lg_v, lg_v.at(M)))
                for j in range(NT):
                    last = pe.matmul(ps_s[3][0:B_K, j * 128:(j + 1) * 128], wgt[:, j, :], ident_h[:, :],
                                     start=True, stop=True)
                last.then_inc(wt_ps.sem, 1)

            def biases(M, *guards):
                guard((wt_ok, wt_ok.at(M)), *guards)
                for b in range(2):
                    for j in (2 * b, 2 * b + 1):
                        last = pe.matmul(ps_s[b][:, (j % 2) * D:(j % 2 + 1) * D], wgt_t[:, j, :], b2p[0:B_K, :],
                                         start=True, stop=True)
                    last.then_inc(b_ps.sem, 1)

            def gates(a, *guards):
                guard((g_v, g_v.at(a)), *guards)
                pe.matmul(ps_s[2][:, 0:NT], blk, gate_in[:, 0:NT], start=True, stop=True)
                pe.matmul(ps_s[2][:, NT:NT + 2], ones, gate_in[:, NT:NT + 2], start=True, stop=True)\
                  .then_inc(g_ps.sem, 1)

            def project(a, first, width, where, ax_hi, ax_lo, *guards):
                guard((ln_lo[1], ln_lo[1].at(a)), *guards)
                for j in range(NT):
                    t = slice(j * 128, (j + 1) * 128)
                    pairs = []
                    for c in range(DC):
                        w = slice(first + c * width, first + (c + 1) * width)
                        pairs += [(ax_hi[:, c, t], wa_hi[:, w]), (ax_hi[:, c, t], wa_lo[:, w]),
                                  (ax_lo[:, c, t], wa_hi[:, w])]
                    products(where(j), pairs).then_inc(p_ps.sem, 1)

            def project_kv(a, *guards):
                project(a, 0, 2 * D, lambda j: ps_s[j][:, :], ax_hi, ax_lo, *guards)

            def project_q(a, *guards):
                at = place(a)
                project(a, 2 * DC * D, D, lambda j: at.q_banks[j // 2][:, (j % 2) * D:(j % 2 + 1) * D],
                        at.hi, at.lo, *guards)

            def k_t(a, *guards):
                transposes(place(a).q, place(a).qt_banks, kt_ps, (k_ok, k_ok.at(a)), *guards)

            def z(a, *guards):
                guard((kt_ok, kt_ok.at(a)), *guards)
                for j in range(NT):
                    t = slice(j * 128, (j + 1) * 128)
                    pairs = []
                    for c in range(DC):
                        pairs += [(kt_hi[:, c, t], w0_hi[:, c, :]), (kt_hi[:, c, t], w0_lo[:, c, :]),
                                  (kt_lo[:, c, t], w0_hi[:, c, :])]
                    products(ps_s[j][:, :], pairs).then_inc(z_ps.sem, 1)

            def z_t(a, *guards):
                guard((kt_ok, kt_ok.at(a)), *guards)
                for c in range(IC):
                    w = slice(c * 128, (c + 1) * 128)
                    pairs = []
                    for dc in range(DC):
                        pairs += [(w0_hi[:, dc, w], kt_hi[:, dc, :]), (w0_hi[:, dc, w], kt_lo[:, dc, :]),
                                  (w0_lo[:, dc, w], kt_hi[:, dc, :])]
                    products(ps_s[c][:, :], pairs).then_inc(z_ps.sem, 1)

            def h_t(a, *guards):
                transposes(hp, ps_s, ht_ps, (h_ok, h_ok.at(a)), *guards)

            def y(a):
                guard((ht_ok, ht_ok.at(a)))
                for b in range(2):
                    for j in (2 * b, 2 * b + 1):
                        t = slice(j * 128, (j + 1) * 128)
                        pairs = []
                        for c in range(IC):
                            pairs += [(ht_hi[:, c, t], w1_hi[:, c, :]), (ht_hi[:, c, t], w1_lo[:, c, :]),
                                      (ht_lo[:, c, t], w1_hi[:, c, :])]
                        last = products(ps_s[b][:, (j % 2) * D:(j % 2 + 1) * D], pairs)
                    last.then_inc(y_ps.sem, 1)

            def dln_dyt(a):
                transposes(pr, ps_s[2:4], dyt_ps, (dy_ok, dy_ok.at(a)))
                guard((gy_ok, gy_ok.at(a)), (w1_ok, w1_ok.at(a)))
                products(ps_s[0][:, 0:D], [(ones, gy[:, 0, :])]).then_inc(dln_ps.sem, 1)

            def dh(a):
                guard((dyt_ok, dyt_ok.at(a)), (dln_ok, dln_ok.at(a)))
                for j in range(NT):
                    t = slice(j * 128, (j + 1) * 128)
                    pairs = []
                    for c in range(DC):
                        pairs += [(dyt_hi[:, c, t], w1n_hi[:, c, :]), (dyt_hi[:, c, t], w1n_lo[:, c, :]),
                                  (dyt_lo[:, c, t], w1n_hi[:, c, :])]
                    products(ps_s[j][:, :], pairs).then_inc(dh_ps.sem, 1)

            def dw1(a):
                guard((dz_ok, dz_ok.at(a)))
                for b in range(2):
                    for c in (2 * b, 2 * b + 1):
                        last = products(ps_s[b][:, (c % 2) * D:(c % 2 + 1) * D],
                                        [(hp[:, j, c * 128:(c + 1) * 128], pr[:, j, :]) for j in range(NT)])
                    last.then_inc(dw_ps.sem, 1)

            def dw0(a):
                for c in range(DC):
                    products(ps_s[2 + c][:, :],
                             [(kn[:, j, c * 128:(c + 1) * 128], dz[:, j, :]) for j in range(NT)])\
                        .then_inc(dw_ps.sem, 1)

            def w1_natural(a, *guards):
                banks = w1_banks(a)
                guard((mem_ok, mem_ok.at(a)), *guards)
                for dc in range(DC):
                    for c in range(IC):
                        last = pe.transpose(banks[dc][:, c * 128:(c + 1) * 128],
                                            mem_w1t[:, c, dc * 128:(dc + 1) * 128], ident)
                    last.then_inc(w1_ps.sem, 1)

            def experts(M, fill, first=False):
                guard((ln_lo[0], ln_lo[0].at(M)))
                if first:
                    guard((w_lo, w_lo.at(0)))
                mm1(M, 0)
                for e in range(NU):
                    if e < NU - 1:
                        if first:
                            guard((w_lo, w_lo.at(e + 1)))
                        mm1(M, e + 1)
                    for step in fill.get(2 * e, ()):
                        step()
                    mm2(M, e)
                    for step in fill.get(2 * e + 1, ()):
                        step()

            def scan_fill(a, M, more=True):
                fill = {
                    2: [lambda: ln_t(1, a), lambda: weights_t(M)],
                    4: [lambda: project_kv(a, (wt_ok, wt_ok.at(M)))],
                    5: [lambda: biases(M, (p_s, p_s.at(a)))],
                    6: [lambda: k_t(a)],
                    7: [lambda: z(a, (b_ok, b_ok.at(M)), (mem_lo, mem_lo.at(a)))],
                    9: [lambda: h_t(a)],
                    10: [lambda: y(a), lambda: gates(a)],
                    12: [lambda: w1_natural(a, (y_n, y_n.at(a)))],
                    13: [lambda: dln_dyt(a)],
                    14: [lambda: dh(a)],
                    15: [lambda: dw1(a), lambda: dw0(a)],
                }
                if not more:
                    fill[13] = [lambda: dln_dyt(a), lambda: dh(a)]
                    fill[14], fill[15] = fill[15], []
                if more:
                    fill[8] = [lambda: ln_t(0, M + 1, (h_ok, h_ok.at(a)))]
                    fill[9] = [lambda: h_t(a, (ln_lo[0], ln_lo[0].at(M + 1)))]
                    fill[11] = [lambda: router(M + 1, (g_th, g_th.at(a)))]
                    fill[13] = [lambda: guard((lg_v, lg_v.at(M + 1, 1))), lambda: dln_dyt(a)]
                return fill

            def apply_steps(a, *guards):
                return [lambda: ln_t(1, a, *guards), lambda: project_q(a), lambda: k_t(a),
                        lambda: z_t(a), lambda: y(a)]

            def keep_warm(moving, n, bank=ps_h[0]):
                for _ in range(n):
                    pe.matmul(bank[:, 0:moving.shape[-1]], ident_h[:, :], moving, start=True, stop=True)

            wide = we_hi[:, 0, 0:512]
            guard((id_h, id_h.at(0)))
            keep_warm(ident_h[:, :], 44)
            guard((c_in, c_in.at(0)))
            ln_t(0, 0)
            guard((rw_l, rw_l.at(0)))
            router(0)
            experts(0, {2: [lambda: weights_t(0)],
                        5: [lambda: biases(0, (b2_l, b2_l.at(0)))],
                        8: [lambda: ln_t(0, 1, (wt_ok, wt_ok.at(0)))], 10: [lambda: router(1)]}, first=True)
            guard((w_lo, w_lo.at(NU)))
            experts(1, scan_fill(0, 1))
            with pe.Fori(2, NM - 1) as M:
                experts(M, scan_fill(M - 1, M))
            experts(NM - 1, scan_fill(NM - 2, NM - 1, more=False))
            a = NM - 1
            keep_warm(wide, 20)
            ln_t(1, a)
            project_kv(a)
            keep_warm(wide, 28)
            k_t(a, (p_s, p_s.at(a)))
            w1_natural(a, (acc_ok, acc_ok.at(NU * a + E)))
            z(a, (mem_lo, mem_lo.at(a)))
            h_t(a)
            y(a)
            gates(a)
            keep_warm(wide, 40)
            dln_dyt(a)
            dh(a)
            ln_t(1, NM)
            dw1(a)
            project_q(NM)
            dw0(a)
            k_t(NM)
            keep_warm(wide, 32, ps_y[1])
            z_t(NM, (mem_lo, mem_lo.at(NM)))
            keep_warm(wide, 14)
            y(NM)
            keep_warm(wide, 40)
            ln_t(0, NM)
            router(NM)

            def apply_fill(M):
                steps = apply_steps(M + 1)
                return {2: [steps[0], lambda: weights_t(M)], 4: steps[1:2],
                        5: [lambda: biases(M, (p_s, p_s.at(M + 1)))], 6: steps[2:3],
                        8: [lambda: guard((b_ok, b_ok.at(M))), steps[3]], 10: steps[4:5],
                        14: [lambda: ln_t(0, M + 1)], 15: [lambda: router(M + 1)]}

            with pe.Fori(NM, 2 * NM - 1) as M:
                experts(M, apply_fill(M))
            M = 2 * NM - 1
            experts(M, {2: [lambda: weights_t(M)], 5: [lambda: biases(M)]})

        @block.scalar
        def _(act):
            act.dma_start(cst[:, 0:C_BLK], consts_in[:, 0:C_BLK]).then_inc(c_in.sem, 16)

            def copy(dst, src, scale=1.0):
                return act.activation(dst, src, ACT.Copy, scale=scale)

            def split_weights(k):
                act.wait_ge(stage_ld[k % 2].sem, stage_ld[k % 2].at(k // 2))
                if k < NU:
                    copy(we_hi[:, k, :], stage[k % 2], SW).then_inc(w_hi.sem, 1)
                else:
                    copy(wa_hi[:, :], stage[k % 2][:, 0:3 * DC * D], SW).then_inc(w_hi.sem, 1)

            def hidden(M, e):
                u = NU * M + e
                first = isinstance(M, int) and M == 0 and e == 0

                def high(c):
                    if c == 0 and not (isinstance(M, int) and M == 0 and e < 2):
                        act.wait_ge(mm2_ps.sem, mm2_ps.at(u - (1 if e == 0 else 2)))
                    act.wait_ge(gelu_ok.sem, gelu_ok.at(u, c + 1))
                    copy(hh[:, e % 2, c, :], gel[:, c, :], SH).then_inc(hid_hi.sem, 1)

                for c in range(IC):
                    act.wait_ge(mm1_ps.sem, mm1_ps.at(u, c + 1))
                    if not first:
                        act.wait_ge(hid_lo.sem, hid_lo.at(u - 1, c + 1))
                    act.activation(gel[:, c, :], ps_h[c % 2][:, :], ACT.Gelu, scale=1.0 / (SX * SW),
                                   bias=cst[:, C_B1 + e * IC + c:C_B1 + e * IC + c + 1])\
                       .then_inc(gelu_ok.sem, 1)
                    if c > 0:
                        high(c - 1)
                high(IC - 1)

            def ln_high(n, occ):
                dst, banks = (fx_hi[:, occ % 2, :, :], ps_s[2:4]) if n == 0 else (place(occ).hi, place(occ).t_banks)
                for c in range(DC):
                    act.wait_ge(ln_tp[n].sem, ln_tp[n].at(occ, c + 1))
                    copy(dst[:, c, :], banks[c][:, :], SX).then_inc(ln_hi[n].sem, 1)

            def router_exp(M):
                act.wait_ge(lg_v.sem, lg_v.at(M, 3))
                act.activation(lg[:, 2, :, :], lg[:, 1, :, :], ACT.Exp).then_inc(ex_ok.sem, 1)

            def weights_t(M):
                act.wait_ge(wt_ps.sem, wt_ps.at(M))
                copy(wgt_t.rearrange("u j t -> u (j t)"), ps_s[3][0:B_K, :]).then_inc(wt_ok.sem, 1)

            def gates(a):
                act.wait_ge(g_ps.sem, g_ps.at(a))
                act.activation(gate_tanh[:, 0:NT], ps_s[2][:, 0:NT], ACT.Tanh, scale=0.5).then_inc(g_th.sem, 1)
                act.activation(gate_tanh[:, NT:NT + 2], ps_s[2][:, NT:NT + 2], ACT.Tanh, scale=0.5 / B)\
                   .then_inc(g_th.sem, 1)

            def project(a, width, where, ready, dst, silu):
                for j in range(NT):
                    act.wait_ge(p_ps.sem, p_ps.at(a, ready(j)))
                    act.activation(dst[:, j, 0:width], where(j), ACT.Tanh, scale=0.5 / (SX * SW))\
                       .then_inc(p_th.sem, 1)
                for j in range(NT):
                    act.wait_ge(p_s.sem, p_s.at(a, j + 1))
                    act.wait_ge(p_sq.sem, p_sq.at(a, j))
                    act.activation(junk, silu[:, j, 0:D], ACT.Square, scale=1.0 / (2 * SX * SW * D ** 0.5),
                                   accum_out=k_ms[:, j:j + 1]).then_inc(p_sq.sem, 1)

            def project_kv(a):
                project(a, 2 * D, lambda j: ps_s[j][:, :], lambda j: j + 1, tanh_of(a), sp)

            def project_q(a):
                at = place(a)
                project(a, D, lambda j: at.q_banks[j // 2][:, (j % 2) * D:(j % 2 + 1) * D],
                        lambda j: 2 * (j // 2) + 2, at.tanh, at.silu)

            def k_t(a):
                act.wait_ge(p_sq.sem, p_sq.at(a))
                for c in range(DC):
                    act.wait_ge(kt_ps.sem, kt_ps.at(a, c + 1))
                    copy(kt_hi[:, c, :], place(a).qt_banks[c][:, :], SK).then_inc(kt_h.sem, 1)

            def z(a):
                for j in range(NT):
                    act.wait_ge(z_ps.sem, z_ps.at(a, j + 1))
                    act.activation(tanh_of(a)[:, j, :], ps_s[j][:, :], ACT.Tanh, scale=0.5 / (SK * SW))\
                       .then_inc(z_th.sem, 1)

            def h_t(a):
                if not (isinstance(a, int) and a == NM - 1):
                    act.wait_ge(d2_ok.sem, d2_ok.at(a))
                for c in range(IC):
                    act.wait_ge(ht_ps.sem, ht_ps.at(a, c + 1))
                    copy(ht_hi[:, c, :], ps_s[c][:, :], H_SCALE).then_inc(ht_h.sem, 1)

            def h_high(a):
                for c in range(IC):
                    act.wait_ge(h_ok.sem, h_ok.at(a, c + 1))
                    copy(ht_hi[:, c, :], hp[:, c, :], H_SCALE).then_inc(ht_h.sem, 1)

            def y(a):
                for j in range(NT):
                    act.wait_ge(y_ps.sem, y_ps.at(a, j // 2 + 1))
                    act.wait_ge(y_sq.sem, y_sq.at(a, j))
                    act.activation(junk, ps_s[j // 2][:, (j % 2) * D:(j % 2 + 1) * D], ACT.Square,
                                   scale=1.0 / (SH * SW * D ** 0.5), accum_out=y_ms[:, j:j + 1]).then_inc(y_sq.sem, 1)

            def y_norm(a):
                act.wait_ge(y_ri.sem, y_ri.at(a))
                for j in range(NT):
                    copy(yn[:, j, :], ps_s[j // 2][:, (j % 2) * D:(j % 2 + 1) * D], y_rs[:, j:j + 1])\
                        .then_inc(y_n.sem, 1)

            def dyt_copy(a):
                for c in range(DC):
                    act.wait_ge(dyt_ps.sem, dyt_ps.at(a, c + 1))
                    copy(dyt_hi[:, c, :], ps_s[2 + c][:, :], SG).then_inc(dyt_h.sem, 1)
                act.wait_ge(dln_ps.sem, dln_ps.at(a))
                copy(grad[:, IC * D + DC * I:MEMW], ps_s[0][:, 0:D]).then_inc(dln_ok.sem, 1)

            def dw(a, banks=range(4)):
                for b in banks:
                    scale = 0.5 / (SK * SW) if b < 2 else 0.5 / (SG * SW)
                    act.wait_ge(dw_ps.sem, dw_ps.at(a, b + 1))
                    act.activation(d2[:, b, :], ps_s[b][:, :], ACT.Square, scale=scale,
                                   accum_out=nrm[:, b:b + 1]).then_inc(dw_sq.sem, 1)
                    copy(grad[:, b * 512:(b + 1) * 512], ps_s[b][:, :], scale).then_inc(dw_ok.sem, 1)
                    if b == 0:
                        act.wait_ge(dln_ok.sem, dln_ok.at(a))
                        act.activation(junk, grad[:, IC * D + DC * I:MEMW], ACT.Square, scale=128.0 ** -0.5,
                                       accum_out=nrm[:, 4:5]).then_inc(dw_sq.sem, 1)

            def w1_natural(a):
                for c in range(DC):
                    act.wait_ge(w1_ps.sem, w1_ps.at(a, c + 1))
                    copy(w1n_hi[:, c, :], w1_banks(a)[c][:, :], SW).then_inc(w1_h.sem, 1)

            def memory_high(occ):
                final = isinstance(occ, int) and occ == NM
                if final:
                    act.wait_ge(fin_w.sem, fin_w.at(0, 1))
                else:
                    act.wait_ge(mem_ok.sem, mem_ok.at(occ))
                copy(w0_hi, mem_w0t, SW).then_inc(mem_hi.sem, 1)
                if final:
                    act.wait_ge(fin_w.sem, fin_w.at(0))
                copy(w1_hi, mem_w1t, SW).then_inc(mem_hi.sem, 1)

            def experts(M, fill, prep=()):
                hidden(M, 0)
                for e in range(NU):
                    if e < NU - 1:
                        hidden(M, e + 1)
                    if e in prep:
                        split_weights(e + 2)
                    for step in fill.get(2 * e, ()):
                        step()
                    for step in fill.get(2 * e + 1, ()):
                        step()

            def scan_fill(a, M, more=True, after_update=True):
                fill = {
                    2: [lambda: ln_high(1, a), lambda: weights_t(M)],
                    4: [lambda: project_kv(a)],
                    6: [lambda: k_t(a)],
                    7: [lambda: z(a)],
                    9: [lambda: h_t(a)],
                    10: [lambda: y(a), lambda: gates(a), lambda: y_norm(a)],
                    12: [lambda: w1_natural(a)],
                    13: [lambda: dyt_copy(a)],
                    15: [lambda: dw(a)],
                }
                if not more:
                    fill[14], fill[15] = fill[15], []
                if after_update:
                    fill[4].insert(0, lambda: memory_high(a))
                if more:
                    fill[8] = [lambda: ln_high(0, M + 1)]
                    fill[15] = [lambda: router_exp(M + 1), lambda: dw(a)]
                return fill

            def apply_steps(a):
                return [lambda: ln_high(1, a), lambda: project_q(a), lambda: k_t(a), lambda: z(a),
                        lambda: h_high(a), lambda: y(a)]

            act.wait_ge(c_in.sem, c_in.at(0))
            copy(ident_h[:, :], ident).then_inc(id_h.sem, 1)
            copy(rw_hi[:, :], cst[:, C_RW:C_RW + DC * E], SW).then_inc(rw_h.sem, 1)
            split_weights(0)
            ln_high(0, 0)
            router_exp(0)
            split_weights(1)

            def biases_high():
                act.wait_ge(b2_ld.sem, b2_ld.at(0))
                copy(b2p[0:B_K, :], b2[0:B_K, :], SW).then_inc(b2_h.sem, 1)

            experts(0, {2: [lambda: weights_t(0), biases_high], 8: [lambda: ln_high(0, 1)],
                        10: [lambda: router_exp(1)], 15: [lambda: memory_high(0)]}, prep=range(NU - 1))
            experts(1, scan_fill(0, 1, after_update=False))
            with act.Fori(2, NM - 1) as M:
                experts(M, scan_fill(M - 1, M))
            experts(NM - 1, scan_fill(NM - 2, NM - 1, more=False))
            a = NM - 1
            ln_high(1, a)
            project_kv(a)
            memory_high(a)
            k_t(a)
            w1_natural(a)
            z(a)
            h_t(a)
            y(a)
            gates(a)
            y_norm(a)
            dyt_copy(a)
            ln_high(1, NM)
            dw(a, range(0, 2))
            project_q(NM)
            dw(a, range(2, 4))
            k_t(NM)
            memory_high(NM)
            for step in apply_steps(NM)[3:]:
                step()
            ln_high(0, NM)
            router_exp(NM)
            with act.Fori(NM, 2 * NM - 1) as M:
                steps = apply_steps(M + 1)
                experts(M, {2: [steps[0], lambda: weights_t(M)], 4: steps[1:2], 6: steps[2:3],
                            8: steps[3:5], 10: steps[5:6],
                            14: [lambda: ln_high(0, M + 1)], 15: [lambda: router_exp(M + 1)]})
            M = 2 * NM - 1
            experts(M, {2: [lambda: weights_t(M)]})

        @block.vector
        def _(dve):
            def low(dst, src, hi, scale):
                return dve.scalar_tensor_tensor(dst, src, scale, hi, ALU.mult, ALU.subtract)

            def over_tiles(row, n=D):
                return row.unsqueeze(1).to_broadcast([128, NT, n])

            def split_weights(k):
                dve.wait_ge(w_hi.sem, w_hi.at(k))
                if k < NU:
                    low(we_lo[:, k, :], stage[k % 2], we_hi[:, k, :], SW).then_inc(w_lo.sem, 1)
                else:
                    low(wa_lo[:, :], stage[k % 2][:, 0:3 * DC * D], wa_hi[:, :], SW).then_inc(w_lo.sem, 1)

            def hidden(M, e):
                u = NU * M + e
                for c in range(IC):
                    dve.wait_ge(hid_hi.sem, hid_hi.at(u, c + 1))
                    low(hl[:, e % 2, c, :], gel[:, c, :], hh[:, e % 2, c, :], SH).then_inc(hid_lo.sem, 1)

            def accumulate(M, e):
                u = NU * M + e
                if e == 0:
                    dve.wait_ge(lg_v.sem, lg_v.at(M))
                else:
                    dve.wait_ge(acc_ok.sem, acc_ok.at(u - 1))
                if e == 3:
                    dve.wait_ge(b_ok.sem, b_ok.at(M))
                for b in range(2):
                    dve.wait_ge(mm2_ps.sem, mm2_ps.at(u, b + 1))
                    for j in (2 * b, 2 * b + 1):
                        w = wacc[:, M % 2, j, e:e + 1] if e < E else 0.5 / (SH * SW)
                        x = xt[:, M % 2, j, :]
                        last = dve.scalar_tensor_tensor(x, ps_y[b][:, (j % 2) * D:(j % 2 + 1) * D], w, x,
                                                        ALU.mult, ALU.add)
                    last.then_inc(acc_ok.sem, 1)

            def layer_norm(n, occ, *waits):
                dst = xnf(occ) if n == 0 else xna
                for event, value in waits:
                    dve.wait_ge(event.sem, value)
                dve.memset(waited[2 * n], 0.0)
                for j in range(NT):
                    dve.bn_stats(stats[:, n, j, :], xt[:, occ % 2, j, :]).then_inc(ln_st[n].sem, 1)
                dve.wait_ge(ln_st[n].sem, ln_st[n].at(occ))
                dve.memset(waited[2 * n + 1], 0.0)
                for j in range(NT):
                    dve.bn_aggr(mv[:, n, j, :], stats[:, n, j, :]).then_inc(ln_mv[n].sem, 1)
                dve.wait_ge(ln_rs[n].sem, ln_rs[n].at(occ))
                for j in range(NT):
                    dve.tensor_scalar(dst[:, j, :], xt[:, occ % 2, j, :], mv[:, n, j, 0:1],
                                      rstd[n][:, j:j + 1], ALU.subtract, ALU.mult).then_inc(ln_xn[n].sem, 1)

            def ln_low(n, occ):
                f_lo, f_hi = fx_lo[:, occ % 2, :, :], fx_hi[:, occ % 2, :, :]
                at = place(occ)
                dst, hi, banks = (f_lo, f_hi, ps_s[2:4]) if n == 0 else (at.lo, at.hi, at.t_banks)
                for c in range(DC):
                    dve.wait_ge(ln_hi[n].sem, ln_hi[n].at(occ, c + 1))
                    low(dst[:, c, :], banks[c][:, :], hi[:, c, :], SX).then_inc(ln_lo[n].sem, 1)

            def logits(M):
                dve.wait_ge(lg_ps.sem, lg_ps.at(M))
                dve.scalar_tensor_tensor(lg[:, 0, :, :], ps_s[2][:, 0:NT * E].rearrange("p (j e) -> p j e", j=NT),
                                         1.0 / (SX * SW), over_tiles(rb, E), ALU.mult, ALU.add)\
                   .then_inc(lg_v.sem, 1)

            def router(M):
                k = [1]

                def step(ins):
                    k[0] += 1
                    ins.then_inc(lg_v.sem, 1)
                    dve.wait_ge(lg_v.sem, lg_v.at(M, k[0]))

                def over_e(c):
                    return c.unsqueeze(2).to_broadcast([128, NT, E])

                top, rnk, tot, inv = lg[:, 3, :, 0], lg[:, 3, :, 1], lg[:, 3, :, 2], lg[:, 3, :, 3]
                prob, rest, eq, order, s1, s2 = (lg[:, n, :, :] for n in range(4, 10))
                dve.wait_ge(lg_v.sem, lg_v.at(M, 1))
                step(dve.tensor_reduce(top, lg[:, 0, :, :], AX.X, ALU.max))
                step(dve.tensor_tensor(lg[:, 1, :, :], lg[:, 0, :, :], over_e(top), ALU.subtract))
                dve.wait_ge(ex_ok.sem, ex_ok.at(M))
                step(dve.tensor_reduce(tot, lg[:, 2, :, :], AX.X, ALU.add))
                step(dve.reciprocal(inv, tot))
                step(dve.tensor_tensor(prob, lg[:, 2, :, :], over_e(inv), ALU.mult))

                def first_of_largest(values, chosen):
                    step(dve.tensor_reduce(top, values, AX.X, ALU.max))
                    step(dve.tensor_tensor(eq, values, over_e(top), ALU.is_equal))
                    step(dve.tensor_tensor(order, eq, over_tiles(rev, E), ALU.mult))
                    step(dve.tensor_reduce(rnk, order, AX.X, ALU.max))
                    step(dve.tensor_tensor(chosen, order, over_e(rnk), ALU.is_equal))

                first_of_largest(prob, s1)
                step(dve.scalar_tensor_tensor(rest, s1, -4.0, prob, ALU.mult, ALU.add))
                first_of_largest(rest, s2)
                step(dve.tensor_tensor(s1, s1, s2, ALU.add))
                step(dve.scalar_tensor_tensor(rest, prob, SX, s1, ALU.mult, ALU.mult))
                step(dve.tensor_scalar(wgt[:, :, 0:E], rest, 1.0, None, ALU.mult))
                dve.tensor_scalar(wgt[:, :, B_LOW:B_LOW + E], rest, 1.0, None, ALU.mult)
                dve.tensor_tensor(wgt[:, :, NU:NU + E], rest, wgt[:, :, 0:E], ALU.subtract)
                dve.scalar_tensor_tensor(wacc[:, M % 2, :, :], prob, 0.5 / (SH * SW), s1, ALU.mult, ALU.mult)\
                   .then_inc(lg_v.sem, 1)

            def biases(M):
                dve.wait_ge(acc_ok.sem, acc_ok.at(NU * M + 2))
                for b in range(2):
                    dve.wait_ge(b_ps.sem, b_ps.at(M, b + 1))
                    x = xt[:, M % 2, 2 * b:2 * b + 2, :].rearrange("p j d -> p (j d)")
                    dve.scalar_tensor_tensor(x, ps_s[b][:, :], 0.5 / (SX * SW), x, ALU.mult, ALU.add)\
                       .then_inc(b_ok.sem, 1)

            def gate_dots(a):
                k = [0]

                def step(ins):
                    k[0] += 1
                    ins.then_inc(g_v.sem, 1)
                    dve.wait_ge(g_v.sem, g_v.at(a, k[0]))

                dve.wait_ge(ln_xn[1].sem, ln_xn[1].at(a))
                products = [pr, *(sp[:, k:k + 2, :].rearrange("p a (b d) -> p (a b) d", b=2) for k in (0, 2))]
                for g in range(3):
                    dst = gate_in if g == 0 else gate_dot[:, g * NT:(g + 1) * NT]
                    for j in range(NT):
                        last = dve.tensor_tensor_reduce(out=products[g][:, j, :], in0=xna[:, j, :], in1=aw[:, g, :],
                                                        scale=1.0, scalar=0.0, op0=ALU.mult, op1=ALU.add,
                                                        accum_out=dst[:, j:j + 1])
                step(last)
                step(dve.tensor_reduce(gate_in[:, NT:NT + 1], gate_dot[:, NT:2 * NT], AX.X, ALU.add))
                step(dve.tensor_reduce(gate_in[:, NT + 1:NT + 2], gate_dot[:, 2 * NT:3 * NT], AX.X, ALU.add))

            def gates(a):
                dve.wait_ge(g_th.sem, g_th.at(a))
                dve.tensor_scalar(gate[:, :], gate_tanh[:, :], 0.5, 0.5, ALU.mult, ALU.add).then_inc(g_ok.sem, 1)
                dve.wait_ge(g_ok.sem, g_ok.at(a, 1))
                dve.tensor_scalar(gate[:, NT:NT + 1], gate_tanh[:, NT:NT + 1], -0.5, 0.5, ALU.mult, ALU.add)\
                   .then_inc(g_ok.sem, 1)

            def project(a, width, where, weight, with_v, src, silu, dst, before_norm=()):
                for j in range(NT):
                    dve.wait_ge(p_th.sem, p_th.at(a, j + 1) if with_v else p_th.at(a, 2 * (j // 2) + 2))
                    dve.scalar_tensor_tensor(silu[:, j, 0:width], src[:, j, 0:width], 1.0, where(j),
                                             ALU.add, ALU.mult).then_inc(p_s.sem, 1)
                for step in before_norm:
                    step()
                dve.wait_ge(p_r.sem, p_r.at(a))
                dve.wait_ge(p_s.sem, p_s.at(a))
                for j in range(NT):
                    dve.scalar_tensor_tensor(dst[:, j, :], silu[:, j, 0:D], k_r[:, j:j + 1], weight,
                                             ALU.mult, ALU.mult).then_inc(k_ok.sem, 1)

            def project_kv(a, before_norm=()):
                project(a, 2 * D, lambda j: ps_s[j][:, :], knb, True, tanh_of(a), sp, kn,
                        before_norm)
                dve.wait_ge(k_ok.sem, k_ok.at(a))
                dve.scalar_tensor_tensor(kv[:, :, :], sp[:, :, D:2 * D], -0.5 / (SX * SW), kn[:, :, :],
                                         ALU.mult, ALU.add).then_inc(kv_ok.sem, 1)

            def project_q(a):
                at = place(a)
                project(a, D, lambda j: at.q_banks[j // 2][:, (j % 2) * D:(j % 2 + 1) * D], qnb, False,
                        at.tanh, at.silu, at.q)

            def z(a):
                for j in range(NT):
                    dve.wait_ge(z_th.sem, z_th.at(a, j + 1))
                    dve.scalar_tensor_tensor(hp[:, j, :], tanh_of(a)[:, j, :], 1.0, ps_s[j][:, :], ALU.add, ALU.mult)\
                       .then_inc(h_ok.sem, 1)

            def k_low(a):
                for c in range(DC):
                    dve.wait_ge(kt_h.sem, kt_h.at(a, c + 1))
                    low(kt_lo[:, c, :], place(a).qt_banks[c][:, :], kt_hi[:, c, :], SK).then_inc(kt_ok.sem, 1)

            def h_low(a, transposed=False):
                if transposed:
                    dve.wait_ge(h_ok.sem, h_ok.at(a))
                for c in range(IC):
                    dve.wait_ge(ht_h.sem, ht_h.at(a, c + 1))
                    low(ht_lo[:, c, :], hp[:, c, :] if transposed else ps_s[c][:, :], ht_hi[:, c, :], H_SCALE)\
                        .then_inc(ht_ok.sem, 1)

            def dyt_low(a):
                for c in range(DC):
                    dve.wait_ge(dyt_h.sem, dyt_h.at(a, c + 1))
                    low(dyt_lo[:, c, :], ps_s[2 + c][:, :], dyt_hi[:, c, :], SG).then_inc(dyt_ok.sem, 1)

            def w1_natural_low(a):
                for c in range(DC):
                    dve.wait_ge(w1_h.sem, w1_h.at(a, c + 1))
                    low(w1n_lo[:, c, :], w1_banks(a)[c][:, :], w1n_hi[:, c, :], SW).then_inc(w1_ok.sem, 1)

            def memory_low(occ):
                for n, (dst, src, hi) in enumerate(((w0_lo, mem_w0t, w0_hi), (w1_lo, mem_w1t, w1_hi))):
                    dve.wait_ge(mem_hi.sem, mem_hi.at(occ, n + 1))
                    low(dst, src, hi, SW).then_inc(mem_lo.sem, 1)

            def derivative(a):
                dve.wait_ge(h_ok.sem, h_ok.at(a))
                tnh = tanh_of(a)
                dve.scalar_tensor_tensor(d2[:, :, :], tnh[:, :, :], 1.0, hp[:, :, :], ALU.subtract, ALU.mult)\
                   .then_inc(d2_ok.sem, 1)
                dve.wait_ge(d2_ok.sem, d2_ok.at(a, 1))
                dve.scalar_tensor_tensor(d2[:, :, :], d2[:, :, :], -0.5 / (SK * SW), tnh[:, :, :], ALU.mult, ALU.add)\
                   .then_inc(d2_ok.sem, 1)

            def step_of(event, occ, first=0):
                k = [first]

                def step(ins):
                    k[0] += 1
                    ins.then_inc(event.sem, 1)
                    dve.wait_ge(event.sem, event.at(occ, k[0]))
                return step

            def backward(a):
                dve.wait_ge(y_n.sem, y_n.at(a))
                step = step_of(bw, a)
                step(dve.tensor_tensor(pr, yn[:, :, :], over_tiles(mem_ln), ALU.mult))
                step(dve.tensor_tensor(kv[:, :, :], pr, kv[:, :, :], ALU.add))
                dve.wait_ge(tr_ok.sem, tr_ok.at(a))
                for j in range(NT):
                    last = dve.scalar_tensor_tensor(pr[:, j, :], kv[:, j, :], theta_r[:, j:j + 1], mem_ln,
                                                    ALU.mult, ALU.mult)
                step(last)
                for j in range(NT):
                    last = dve.tensor_tensor_reduce(out=reg_b4[:, j, :], in0=pr[:, j, :], in1=yn[:, j, :], scale=1.0,
                                                    scalar=0.0, op0=ALU.mult, op1=ALU.add, accum_out=dot[:, j:j + 1])
                step(last)
                step(dve.tensor_scalar(dot_neg, dot, -1.0 / D, None, ALU.mult))
                for j in range(NT):
                    dve.scalar_tensor_tensor(pr[:, j, :], yn[:, j, :], dot_neg[:, j:j + 1], pr[:, j, :],
                                             ALU.mult, ALU.add).then_inc(dy_ok.sem, 1)

            def add_q(a):
                dve.wait_ge(k_ok.sem, k_ok.at(a))
                x = xt[:, a % 2, :, :]
                dve.tensor_tensor(x, x, place(a).q, ALU.add).then_inc(q_add.sem, 1)

            def output_y(a):
                dve.wait_ge(y_ri.sem, y_ri.at(a))
                for j in range(NT):
                    dve.scalar_tensor_tensor(pr[:, j, :], ps_s[j // 2][:, (j % 2) * D:(j % 2 + 1) * D],
                                             y_rs[:, j:j + 1], mem_ln, ALU.mult, ALU.mult).then_inc(pred_v.sem, 1)
                dve.wait_ge(pred_v.sem, pred_v.at(a - NM))
                dve.wait_ge(q_add.sem, q_add.at(a - NM))
                x = xt[:, a % 2, :, :]
                dve.tensor_tensor(x, x, pr, ALU.add).then_inc(x_att.sem, 1)

            def dz_step(a):
                for j in range(NT):
                    dve.wait_ge(dh_ps.sem, dh_ps.at(a, j + 1))
                    dve.scalar_tensor_tensor(dz[:, j, :], d2[:, j, :], 1.0, ps_s[j][:, :], ALU.add, ALU.mult)\
                       .then_inc(dz_ok.sem, 1)

            def norm_sum(a):
                dve.wait_ge(dw_sq.sem, dw_sq.at(a))
                if not (isinstance(a, int) and a == NM - 1):
                    dve.wait_ge(dw_ok.sem, dw_ok.at(a))
                dve.tensor_reduce(nrm_sum, nrm, AX.X, ALU.add).then_inc(n_v.sem, 1)

            def clipping(a):
                dve.wait_ge(n_rt.sem, n_rt.at(a))
                total, inv, lim = nrm_c
                dve.tensor_scalar(total, nrm_root, GRAD, 1e-6, ALU.mult, ALU.add).then_inc(clip.sem, 1)
                dve.wait_ge(clip.sem, clip.at(a, 1))
                dve.reciprocal(inv, total).then_inc(clip.sem, 1)
                dve.wait_ge(clip.sem, clip.at(a, 2))
                dve.tensor_scalar(lim, inv, 1.0, -GRAD, ALU.min, ALU.mult).then_inc(clip.sem, 1)
                dve.wait_ge(clip.sem, clip.at(a, 3))
                return lim

            def clip_gradients(a):
                lim = clipping(a)
                dve.tensor_scalar(grad[:, :], grad[:, :], lim, None, ALU.mult).then_inc(clip.sem, 1)

            def move_memory(a):
                dve.wait_ge(clip.sem, clip.at(a))
                dve.scalar_tensor_tensor(sur[:, :], sur[:, :], gate[:, NT + 1:NT + 2], grad[:, :], ALU.mult, ALU.add)\
                   .then_inc(sur_ok.sem, 1)
                dve.wait_ge(sur_ok.sem, sur_ok.at(a))
                dve.scalar_tensor_tensor(mem[:, :], mem[:, :], gate[:, NT:NT + 1], sur[:, :], ALU.mult, ALU.add)\
                   .then_inc(mem_ok.sem, 1)

            def final_decay():
                dve.tensor_scalar(sur[:, :], sur[:, :], gate[:, NT + 1:NT + 2], None, ALU.mult).then_inc(fin.sem, 1)
                dve.wait_ge(fin.sem, fin.at(0, 1))
                dve.scalar_tensor_tensor(mem[:, :], mem[:, :], gate[:, NT:NT + 1], sur[:, :], ALU.mult, ALU.add)\
                   .then_inc(fin.sem, 1)

            def final_update(a):
                lim = clipping(a)
                dve.wait_ge(fin.sem, fin.at(0))
                dve.wait_ge(dw_ok.sem, dw_ok.at(a))
                for part in (slice(IC * D, MEMW), slice(0, IC * D)):
                    dve.scalar_tensor_tensor(mem[:, part], grad[:, part], lim, mem[:, part], ALU.mult, ALU.add)\
                       .then_inc(fin_w.sem, 1)

            def experts(M, fill, prep=()):
                hidden(M, 0)
                for e in range(NU):
                    if e < NU - 1:
                        hidden(M, e + 1)
                    if e in prep:
                        split_weights(e + 2)
                    for step in fill.get(2 * e, ()):
                        step()
                    accumulate(M, e)
                    for step in fill.get(2 * e + 1, ()):
                        step()

            def attn_ln(a):
                return lambda: layer_norm(1, a, (acc_ok, acc_ok.at(NU * a + E)), (b_ok, b_ok.at(a)))

            def scan_fill(a, M, more=True, after_update=True):
                fill = {
                    0: [attn_ln(a)],
                    2: [lambda: ln_low(1, a)],
                    4: [lambda: project_kv(a)],
                    5: [lambda: biases(M)],
                    6: [lambda: k_low(a)],
                    7: [lambda: z(a)],
                    8: [lambda: derivative(a)],
                    9: [lambda: h_low(a), lambda: gate_dots(a)],
                    11: [lambda: gates(a), lambda: backward(a)],
                    12: [lambda: w1_natural_low(a)],
                    13: [lambda: dyt_low(a)],
                    14: [lambda: dz_step(a)],
                    17: [lambda: norm_sum(a)],
                }
                if not more:
                    fill[13] += fill[14]
                    fill[14] = []
                if after_update:
                    fill[3] = [lambda: clip_gradients(a - 1), lambda: move_memory(a - 1)]
                    fill[5].append(lambda: memory_low(a))
                if more:
                    fill[6].append(lambda: layer_norm(0, M + 1, (x_ld, x_ld.at(M + 1))))
                    fill[8] = [lambda: ln_low(0, M + 1), lambda: derivative(a)]
                    fill[12].insert(0, lambda: logits(M + 1))
                    fill[15] = [lambda: router(M + 1)]
                return fill

            def apply_steps(a):
                return [lambda: layer_norm(1, a, (x_ld, x_ld.at(a))), lambda: ln_low(1, a), lambda: project_q(a),
                        lambda: k_low(a), lambda: z(a), lambda: h_low(a, transposed=True), lambda: add_q(a),
                        lambda: output_y(a)]

            dve.wait_ge(c_in.sem, c_in.at(0))
            dve.memset(wgt[:, :, :], 0.0).then_inc(ones_col.sem, 1)
            dve.wait_ge(ones_col.sem, ones_col.at(0, 1))
            for k in (E, B_LOW + E):
                dve.memset(wgt[:, :, k:k + 1], SX).then_inc(ones_col.sem, 1)
            dve.wait_ge(ones_col.sem, ones_col.at(0))
            dve.wait_ge(rw_h.sem, rw_h.at(0))
            low(rw_lo[:, :], cst[:, C_RW:C_RW + DC * E], rw_hi[:, :], SW).then_inc(rw_l.sem, 1)
            layer_norm(0, 0, (x_ld, x_ld.at(0)))
            split_weights(0)
            ln_low(0, 0)
            logits(0)
            router(0)
            split_weights(1)

            def biases_low():
                dve.wait_ge(b2_h.sem, b2_h.at(0))
                low(b2p[B_LOW:B_K, :], b2[B_LOW:B_K, :], b2p[B_LOW:B_K, :], SW).then_inc(b2_l.sem, 1)

            def first_memory():
                dve.wait_ge(mem_ld.sem, mem_ld.at(0))
                dve.wait_ge(b2_l.sem, b2_l.at(0))
                dve.memset(sur[:, :], 0.0).then_inc(mem_ok.sem, 1)
                dve.wait_ge(c_rest.sem, c_rest.at(0))
                dve.tensor_scalar(cst[:, C_KN:C_KN + 2 * D], cst[:, C_KN:C_KN + 2 * D], 0.5 / (SX * SW), None,
                                  ALU.mult).then_inc(nscale.sem, 1)
                memory_low(0)

            experts(0, {3: [biases_low], 5: [lambda: biases(0)], 6: [lambda: layer_norm(0, 1, (x_ld, x_ld.at(1)))],
                        8: [lambda: ln_low(0, 1)], 10: [lambda: logits(1), lambda: router(1)],
                        15: [first_memory]}, prep=range(NU - 1))
            dve.wait_ge(nscale.sem, nscale.at(0))
            experts(1, scan_fill(0, 1, after_update=False))
            with dve.Fori(2, NM - 1) as M:
                experts(M, scan_fill(M - 1, M))
            experts(NM - 1, scan_fill(NM - 2, NM - 1, more=False))
            a = NM - 1
            attn_ln(a)()
            clip_gradients(a - 1)
            ln_low(1, a)
            move_memory(a - 1)
            project_kv(a, before_norm=[lambda: memory_low(a)])
            k_low(a)
            w1_natural_low(a)
            z(a)
            h_low(a)
            gate_dots(a)
            derivative(a)
            gates(a)
            backward(a)
            dyt_low(a)
            layer_norm(1, NM, (x_ld, x_ld.at(NM)), (dy_ok, dy_ok.at(a)), (gy_ok, gy_ok.at(a, 2)))
            dz_step(a)
            ln_low(1, NM)
            dve.wait_ge(w1_ok.sem, w1_ok.at(a))
            final_decay()
            project_q(NM)
            norm_sum(a)
            final_update(a)
            k_low(NM)
            memory_low(NM)
            for step in apply_steps(NM)[4:]:
                step()
            layer_norm(0, NM, (x_att, x_att.at(0)))
            ln_low(0, NM)
            logits(NM)
            router(NM)
            with dve.Fori(NM, 2 * NM - 1) as M:
                steps = apply_steps(M + 1)
                experts(M, {0: steps[0:1], 2: steps[1:2], 4: steps[2:3], 5: [lambda: biases(M)], 6: steps[3:4],
                            8: steps[4:6], 9: steps[6:7],
                            11: [steps[7], lambda: layer_norm(0, M + 1, (x_att, x_att.at(M + 1 - NM)))],
                            14: [lambda: ln_low(0, M + 1)], 15: [lambda: logits(M + 1), lambda: router(M + 1)]})
            M = 2 * NM - 1
            experts(M, {5: [lambda: biases(M)]})


def kernel(**inputs):
    import numpy as np
    import concourse.bacc as bacc
    from concourse import mybir as mb
    from concourse.bass_utils import run_bass_kernel_spmd

    def get(name):
        return np.asarray(inputs["L0_" + name])

    def by_rows(w):
        return w.reshape(-1, 128, w.shape[1]).transpose(1, 0, 2).reshape(128, -1)

    def on_all(row):
        return np.broadcast_to(row.reshape(1, -1), (128, row.size))

    x = get("attn_x").reshape(NT, 2, NM, CH, D).transpose(1, 3, 2, 0, 4).reshape(128, NM, NT * D)
    first = [get("ffn_rw1")[e] for e in range(E)] + [get("ffn_sw1")]
    second = [get("ffn_rw2")[e] for e in range(E)] + [get("ffn_sw2")]
    w_experts = np.stack([np.concatenate([by_rows(a), by_rows(b)], 1) for a, b in zip(first, second)], 1)
    wk, wv, wq = (get(f"attn_w{n}_w").T for n in "kvq")
    w_attn = np.concatenate([by_rows(np.concatenate([wk, wv], 1)), by_rows(wq)], 1)
    w0, w1 = get("attn_mem_w0"), get("attn_mem_w1")
    mem = np.concatenate([by_rows(w1.T), by_rows(w0.T), on_all(get("attn_mem_ln_w"))], 1)
    f32 = x.dtype
    p = np.arange(128)
    b1 = np.concatenate([get("ffn_rb1"), get("ffn_sb1")[None]]).reshape(NU * IC, 128).T
    b2 = np.zeros((128, D), f32)
    for row in (0, NU, B_LOW):
        b2[row:row + E], b2[row + E] = get("ffn_rb2"), get("ffn_sb2")
    gate_w = [np.concatenate([get(f"attn_{n}_w").reshape(CH, D)] * 2) for n in ("theta", "alpha", "eta")]
    consts = np.concatenate([
        np.eye(128, dtype=f32), b1, on_all(get("ffn_router_b")), on_all(np.arange(E, 0, -1).astype(f32)),
        by_rows(get("ffn_router_w")), (p[:, None] // CH == p[None] // CH).astype(f32), np.ones((128, 128), f32),
        *gate_w, on_all(get("attn_k_norm_w")), on_all(get("attn_q_norm_w")), b2], 1)
    arrays = {"x_in": x, "w_experts": w_experts, "w_attn": w_attn, "mem_in": mem,
              "consts_in": consts}
    arrays = {n: np.ascontiguousarray(a) for n, a in arrays.items()}

    nc = bacc.Bacc("TRN2", target_bir_lowering=False, num_devices=1)
    args = {n: nc.dram_tensor(n, a.shape, mb.dt.from_np(a.dtype), kind="ExternalInput").ap()
            for n, a in arrays.items()}
    args["out"] = nc.dram_tensor("out", (128, NM, NT * D), mb.dt.float32, kind="ExternalOutput").ap()
    macaron_kernel(nc, **args)
    got = run_bass_kernel_spmd(nc, [arrays], core_ids=[0]).results[0]["out"]
    return got.reshape(2, CH, NM, NT, D).transpose(3, 0, 2, 1, 4).reshape(B, S, D)
```
